# Optimizing a Trainium2 kernel written in Bass

```python
import numpy as np
import jax
import jax.numpy as jnp

def _softmax(x, axis=-1):
    return jax.nn.softmax(x, axis=axis)

def _gelu(x):
    return jax.nn.gelu(x, approximate=True)

def _silu(x):
    return jax.nn.silu(x)

def _sigmoid(x):
    return jax.nn.sigmoid(x)

def _layernorm(x, axis=-1, eps=1e-05):
    m = jnp.mean(x, axis=axis, keepdims=True)
    v = jnp.var(x, axis=axis, keepdims=True)
    return (x - m) / jnp.sqrt(v + eps)

def _scatter_add(tgt, idx, src, axis=0):
    return tgt.at[idx].add(src)

def _segment_sum(src, seg, n):
    return jax.ops.segment_sum(src, seg, n)
kernel_name = 'mk_audio_tower_d2_tok_audfeat512_r4_7933b7'

def setup_inputs(seed: int=0):
    np.random.seed(seed)
    _w = jnp.asarray

    def _rec_inputs():
        import jax
        import jax.numpy as jnp
        _rk = jax.random.key(seed)
        x = -0.000125008 + 0.999885 * jax.random.normal(jax.random.fold_in(_rk, 1), (8, 64, 256), jnp.float32)
        return x
    x = _rec_inputs()

    def _L0_tok_setup():
        import jax, jax.numpy as jnp
        import numpy as np
        from jax import lax
        STRIDE = 1
        PADDING = 4
        key = jax.random.key(seed)
        k1, k2, k3 = jax.random.split(key, 3)
        B, C_IN, L = (32, 64, 1024)
        C_OUT, K = (128, 9)
        x = jax.random.normal(k1, (B, C_IN, L), dtype=jnp.float32)
        weight = jax.random.normal(k2, (C_OUT, C_IN, K), dtype=jnp.float32)
        bias = jax.random.normal(k3, (C_OUT,), dtype=jnp.float32)
        return {'x': x, 'weight': weight, 'bias': bias}
    _L0_tok_all = _L0_tok_setup()
    _L0_tok_in = {k: v for k, v in _L0_tok_all.items() if k in ('weight', 'bias')}
    del _L0_tok_all

    def _L0_attn_setup():
        import jax, jax.numpy as jnp
        import numpy as np
        NUM_HEADS = 8
        EPS = 1e-06

        def _fourier_attention(x, w_qkv, w_proj, b_proj, paramR):
            B, N, C = x.shape
            H = NUM_HEADS
            Dh = C // H
            qkv = jnp.einsum('bnc,kc->bnk', x, w_qkv).reshape(B, N, 3, H, Dh)
            q = qkv[:, :, 0].transpose(0, 2, 1, 3)
            k = qkv[:, :, 1].transpose(0, 2, 1, 3)
            v = qkv[:, :, 2].transpose(0, 2, 1, 3)
            R = paramR[0]
            diff = q[:, :, :, None, :] - k[:, :, None, :, :]
            near0 = jnp.abs(diff) < 1e-08
            safe = jnp.where(near0, jnp.float32(1.0), diff)
            s = jnp.where(near0, R, jnp.sin(R * safe) / safe)
            score = jnp.prod(s, axis=-1)
            a4 = score ** 4
            attn = a4 / (jnp.sum(a4, axis=-1, keepdims=True) + EPS)
            out = jnp.einsum('bhqk,bhkd->bhqd', attn, v)
            out = out.transpose(0, 2, 1, 3).reshape(B, N, C)
            return jnp.einsum('bnc,oc->bno', out, w_proj) + b_proj
        key = jax.random.key(seed)
        k1, k2, k3 = jax.random.split(key, 3)
        B, N, C = (4, 64, 128)
        x = jax.random.normal(k1, (B, N, C), dtype=jnp.float32)
        w_qkv = jax.random.normal(k2, (3 * C, C), dtype=jnp.float32) * C ** (-0.5)
        w_proj = jax.random.normal(k3, (C, C), dtype=jnp.float32) * C ** (-0.5)
        b_proj = jnp.zeros((C,), dtype=jnp.float32)
        paramR = jnp.ones((1,), dtype=jnp.float32)
        return {'x': x, 'w_qkv': w_qkv, 'w_proj': w_proj, 'b_proj': b_proj, 'paramR': paramR}
    _L0_attn_all = _L0_attn_setup()
    _L0_attn_in = {k: v for k, v in _L0_attn_all.items() if k in ('w_qkv', 'w_proj', 'b_proj', 'paramR')}
    del _L0_attn_all

    def _L0_ffn_setup():
        import jax, jax.numpy as jnp
        import numpy as np
        B, S, D, E, O = (256, 64, 128, 16, 128)
        key = jax.random.key(seed)
        k_x, k_wg, k_bg, k_we, k_be = jax.random.split(key, 5)
        scale_g = 1.0 / np.sqrt(D)
        scale_e = 1.0 / np.sqrt(D)
        return {'x': jax.random.normal(k_x, (B, S, D), dtype=jnp.float32), 'Wg': jax.random.uniform(k_wg, (D, E), jnp.float32, -scale_g, scale_g), 'bg': jax.random.uniform(k_bg, (E,), jnp.float32, -scale_g, scale_g), 'We': jax.random.uniform(k_we, (E, D, O), jnp.float32, -scale_e, scale_e), 'be': jax.random.uniform(k_be, (E, O), jnp.float32, -scale_e, scale_e)}
    _L0_ffn_all = _L0_ffn_setup()
    _L0_ffn_in = {k: v for k, v in _L0_ffn_all.items() if k in ('Wg', 'bg', 'We', 'be')}
    del _L0_ffn_all

    def _L1_attn_setup():
        import jax, jax.numpy as jnp
        import numpy as np
        DIM = 128
        HEADS = 8
        DIM_HEAD = 64
        INNER = HEADS * DIM_HEAD
        key = jax.random.key(seed)
        kx, kq, kk, kv, ko = jax.random.split(key, 5)
        x = jax.random.normal(kx, (2, 1024, DIM), dtype=jnp.float32)
        lim = float(np.sqrt(6.0 / (DIM + INNER)))
        Wq = jax.random.uniform(kq, (INNER, DIM), minval=-lim, maxval=lim, dtype=jnp.float32)
        Wk = jax.random.uniform(kk, (INNER, DIM), minval=-lim, maxval=lim, dtype=jnp.float32)
        Wv = jax.random.uniform(kv, (INNER, DIM), minval=-lim, maxval=lim, dtype=jnp.float32) * 0.67
        lim_o = float(np.sqrt(6.0 / (INNER + DIM)))
        Wo = jax.random.uniform(ko, (DIM, INNER), minval=-lim_o, maxval=lim_o, dtype=jnp.float32) * 0.67
        return {'x': x, 'Wq': Wq, 'Wk': Wk, 'Wv': Wv, 'Wo': Wo}
    _L1_attn_all = _L1_attn_setup()
    _L1_attn_in = {k: v for k, v in _L1_attn_all.items() if k in ('Wq', 'Wk', 'Wv', 'Wo')}
    del _L1_attn_all

    def _L1_ffn_setup():
        import jax, jax.numpy as jnp
        import numpy as np
        B, S, H, E, K = (8, 1024, 128, 8, 2)
        key = jax.random.key(seed)
        ks = jax.random.split(key, 7)
        s_h = 1.0 / np.sqrt(H)
        s_2h = 1.0 / np.sqrt(2 * H)
        return {'x': jax.random.normal(ks[0], (B, S, H), dtype=jnp.float32), 'gate_w': jax.random.uniform(ks[1], (H, E), minval=-s_h, maxval=s_h, dtype=jnp.float32), 'gate_b': jax.random.uniform(ks[2], (E,), minval=-s_h, maxval=s_h, dtype=jnp.float32), 'w1': jax.random.uniform(ks[3], (E, H, 2 * H), minval=-s_h, maxval=s_h, dtype=jnp.float32), 'b1': jax.random.uniform(ks[4], (E, 2 * H), minval=-s_h, maxval=s_h, dtype=jnp.float32), 'w2': jax.random.uniform(ks[5], (E, 2 * H, H), minval=-s_2h, maxval=s_2h, dtype=jnp.float32), 'b2': jax.random.uniform(ks[6], (E, H), minval=-s_2h, maxval=s_2h, dtype=jnp.float32)}
    _L1_ffn_all = _L1_ffn_setup()
    _L1_ffn_in = {k: v for k, v in _L1_ffn_all.items() if k in ('gate_w', 'gate_b', 'w1', 'b1', 'w2', 'b2')}
    del _L1_ffn_all
    return {'x': x, 'L0_tok_weight': _L0_tok_in['weight'], 'L0_tok_bias': _L0_tok_in['bias'], 'L0_attn_w_qkv': _L0_attn_in['w_qkv'], 'L0_attn_w_proj': _L0_attn_in['w_proj'], 'L0_attn_b_proj': _L0_attn_in['b_proj'], 'L0_attn_paramR': _L0_attn_in['paramR'], 'L0_ffn_Wg': _L0_ffn_in['Wg'], 'L0_ffn_bg': _L0_ffn_in['bg'], 'L0_ffn_We': _L0_ffn_in['We'], 'L0_ffn_be': _L0_ffn_in['be'], 'L1_attn_Wq': _L1_attn_in['Wq'], 'L1_attn_Wk': _L1_attn_in['Wk'], 'L1_attn_Wv': _L1_attn_in['Wv'], 'L1_attn_Wo': _L1_attn_in['Wo'], 'L1_ffn_gate_w': _L1_ffn_in['gate_w'], 'L1_ffn_gate_b': _L1_ffn_in['gate_b'], 'L1_ffn_w1': _L1_ffn_in['w1'], 'L1_ffn_b1': _L1_ffn_in['b1'], 'L1_ffn_w2': _L1_ffn_in['w2'], 'L1_ffn_b2': _L1_ffn_in['b2']}

def reference(x, L0_tok_weight, L0_tok_bias, L0_attn_w_qkv, L0_attn_w_proj, L0_attn_b_proj, L0_attn_paramR, L0_ffn_Wg, L0_ffn_bg, L0_ffn_We, L0_ffn_be, L1_attn_Wq, L1_attn_Wk, L1_attn_Wv, L1_attn_Wo, L1_ffn_gate_w, L1_ffn_gate_b, L1_ffn_w1, L1_ffn_b1, L1_ffn_w2, L1_ffn_b2):
    import jax
    import jax.numpy as jnp

    def _L0_tok_ref(x, weight, bias):
        import jax, jax.numpy as jnp
        import numpy as np
        from jax import lax
        STRIDE = 1
        PADDING = 4
        out = lax.conv_general_dilated(x, weight, window_strides=(STRIDE,), padding=[(PADDING, PADDING)], dimension_numbers=('NCH', 'OIH', 'NCH'))
        out = out + bias[None, :, None]
        return jnp.transpose(out, (0, 2, 1))

    def _L0_attn_ref(x, w_qkv, w_proj, b_proj, paramR):
        import jax, jax.numpy as jnp
        import numpy as np
        NUM_HEADS = 8
        EPS = 1e-06

        def _fourier_attention(x, w_qkv, w_proj, b_proj, paramR):
            B, N, C = x.shape
            H = NUM_HEADS
            Dh = C // H
            qkv = jnp.einsum('bnc,kc->bnk', x, w_qkv).reshape(B, N, 3, H, Dh)
            q = qkv[:, :, 0].transpose(0, 2, 1, 3)
            k = qkv[:, :, 1].transpose(0, 2, 1, 3)
            v = qkv[:, :, 2].transpose(0, 2, 1, 3)
            R = paramR[0]
            diff = q[:, :, :, None, :] - k[:, :, None, :, :]
            near0 = jnp.abs(diff) < 1e-08
            safe = jnp.where(near0, jnp.float32(1.0), diff)
            s = jnp.where(near0, R, jnp.sin(R * safe) / safe)
            score = jnp.prod(s, axis=-1)
            a4 = score ** 4
            attn = a4 / (jnp.sum(a4, axis=-1, keepdims=True) + EPS)
            out = jnp.einsum('bhqk,bhkd->bhqd', attn, v)
            out = out.transpose(0, 2, 1, 3).reshape(B, N, C)
            return jnp.einsum('bnc,oc->bno', out, w_proj) + b_proj
        return _fourier_attention(x, w_qkv, w_proj, b_proj, paramR)

    def _L0_ffn_ref(x, Wg, bg, We, be):
        import jax, jax.numpy as jnp
        import numpy as np
        B, S, D, E, O = (256, 64, 128, 16, 128)
        scores = jax.nn.softmax(jnp.mean(x, axis=1) @ Wg + bg, axis=-1)
        idx = jnp.argmax(scores, axis=-1)
        gate = jnp.take_along_axis(scores, idx[:, None], axis=-1)
        W_sel = We[idx]
        b_sel = be[idx]
        y = jnp.einsum('bsd,bdo->bso', x, W_sel) + b_sel[:, None, :]
        return gate[:, :, None] * y

    def _L1_attn_ref(x, Wq, Wk, Wv, Wo):
        import jax, jax.numpy as jnp
        import numpy as np
        DIM = 128
        HEADS = 8
        DIM_HEAD = 64
        INNER = HEADS * DIM_HEAD
        scale = DIM_HEAD ** (-0.5)
        b, n, _ = x.shape

        def proj(W):
            t = jnp.einsum('bnc,ec->bne', x, W)
            return t.reshape(b, n, HEADS, DIM_HEAD).transpose(0, 2, 1, 3)
        q, k, v = (proj(Wq), proj(Wk), proj(Wv))
        dots = jnp.einsum('bhqd,bhkd->bhqk', q, k) * scale
        attn = jax.nn.softmax(dots, axis=-1)
        out = jnp.einsum('bhqk,bhkd->bhqd', attn, v)
        out = out.transpose(0, 2, 1, 3).reshape(b, n, INNER)
        out = jnp.einsum('bne,ce->bnc', out, Wo)
        return out + x

    def _L1_ffn_ref(x, gate_w, gate_b, w1, b1, w2, b2):
        import jax, jax.numpy as jnp
        import numpy as np
        B, S, H, E, K = (8, 1024, 128, 8, 2)
        logits = jnp.einsum('bsh,he->bse', x, gate_w) + gate_b
        topk_vals, topk_idx = jax.lax.top_k(logits, K)
        topk_weights = jax.nn.softmax(topk_vals, axis=-1)
        mask = jax.nn.one_hot(topk_idx, E, dtype=topk_weights.dtype)
        weights = jnp.einsum('bske,bsk->bse', mask, topk_weights)
        h = jax.nn.relu(jnp.einsum('bsh,ehf->bsef', x, w1) + b1)
        expert_out = jnp.einsum('bsef,efh->bseh', h, w2) + b2
        return jnp.einsum('bseh,bse->bsh', expert_out, weights)
    h = _L0_tok_ref(x, L0_tok_weight, L0_tok_bias)
    h = h + _L0_attn_ref(_layernorm(h, axis=-1), L0_attn_w_qkv, L0_attn_w_proj, L0_attn_b_proj, L0_attn_paramR)
    h = h + _L0_ffn_ref(_layernorm(h, axis=-1), L0_ffn_Wg, L0_ffn_bg, L0_ffn_We, L0_ffn_be)
    h = h + _L1_attn_ref(_layernorm(h, axis=-1), L1_attn_Wq, L1_attn_Wk, L1_attn_Wv, L1_attn_Wo)
    h = h + _L1_ffn_ref(_layernorm(h, axis=-1), L1_ffn_gate_w, L1_ffn_gate_b, L1_ffn_w1, L1_ffn_b1, L1_ffn_w2, L1_ffn_b2)
    return h

_drawn_inputs = setup_inputs


def setup_inputs(seed=0):
    import zlib

    import numpy as np

    out = dict(_drawn_inputs(seed))
    spreads = {'L0_attn_b_proj': (0.0, 0.8)}
    factors = {'L0_ffn_Wg': 8.0,
     'L0_ffn_bg': 8.0,
     'L0_ffn_We': 8.0,
     'L0_ffn_be': 30.305,
     'L1_attn_Wq': 8.0,
     'L1_attn_Wk': 8.0,
     'L1_attn_Wv': 8.0,
     'L1_attn_Wo': 8.0,
     'L1_ffn_gate_w': 8.0,
     'L1_ffn_gate_b': 8.0,
     'L1_ffn_w1': 8.0,
     'L1_ffn_b1': 8.0,
     'L1_ffn_w2': 8.0,
     'L1_ffn_b2': 61.84}
    for name, (base, spread) in spreads.items():
        noise = np.random.default_rng([zlib.crc32(name.encode()), seed]).standard_normal(out[name].shape)
        drawn = base * np.exp(spread * noise) if base else spread * noise
        out[name] = jnp.asarray(drawn.astype(out[name].dtype))
    for name, factor in factors.items():
        out[name] = (out[name] * factor).astype(out[name].dtype)
    return out
```

```python
from contextlib import ExitStack

import numpy as np
import concourse.bass as bass
from concourse import mybir

ALU = mybir.AluOpType
ACT = mybir.ActivationFunctionType
AX = mybir.AxisListType
F32 = mybir.dt.float32
BF16 = mybir.dt.bfloat16
U32 = mybir.dt.uint32

STOP = 99

P = 128
B, CIN, L = 8, 64, 256
C, TAPS, PAD = 128, 9, 4
NT = B * L // P
H, DH = 8, 16
NHEAD = B * H
NPIECE = 3
KROWS = NPIECE * DH
QROW = 64
ROWS = QROW + NPIECE
CHUNK = 2 * L
NCHUNK = DH // 2
GUARD = 1e-7
RANGE_SCALE = 2.0 ** 62
EXP_EVEN = 0x7F000000
EXP_FLIP = 0x7F800000
ATTN_EPS = 1e-6
LN_EPS = 1e-5
MAGIC = 1.5 * 2.0 ** 23
PI = float(np.float32(np.pi))
HALF_PI = float(np.nextafter(np.float32(np.pi / 2), np.float32(0)))
E0 = 16
H1, D1 = 8, 64
INNER = H1 * D1
E1, F1 = 8, 256
NG = 4


def build(nc, x, conv_w, conv_b, w_qk, w_v, w_proj, b_proj, param_r, gate0_w, gate0_b, exp0_w, exp0_b,
          wq1, wk1, wv1, wo1, gate1_w, gate1_b, w1, b1, w2, b2, neg_mask, ident_in, out):
    with ExitStack() as ctx:
        def sb(name, shape, dt=F32):
            return ctx.enter_context(nc.sbuf_tensor(name, shape, dt))

        def sem(name):
            return ctx.enter_context(nc.semaphore(name))

        bank = [ctx.enter_context(nc.psum_tensor(f"bank{i}", [P, 512], F32)) for i in range(8)]

        q_dram = nc.dram_tensor("q_pieces", [NPIECE, 2, NHEAD, DH * L], BF16, kind="Internal").ap()
        k_dram = nc.dram_tensor("k_pieces", [NPIECE, NHEAD, DH, 2, L], BF16, kind="Internal").ap()

        ident = sb("ident", [P, P])
        ones = sb("ones", [P, P])
        conv_w_sb = sb("conv_w_sb", [P, 5, C])
        conv_b_sb = sb("conv_b_sb", [P, C])
        w_qk_sb = sb("w_qk_sb", [P, 2 * C])
        w_v_sb = sb("w_v_sb", [P, C])
        w_proj_sb = sb("w_proj_sb", [P, C])
        b_proj_sb = sb("b_proj_sb", [P, C])
        gate0_w_sb = sb("gate0_w_sb", [P, E0])
        gate0_b_sb = sb("gate0_b_sb", [B, E0])
        wq1_sb = sb("wq1_sb", [P, INNER])
        wk1_sb = sb("wk1_sb", [P, INNER])
        wv1_sb = sb("wv1_sb", [P, INNER])
        wo1_sb = sb("wo1_sb", [P, INNER // P, C])
        gate1_w_sb = sb("gate1_w_sb", [P, E1])
        gate1_b_sb = sb("gate1_b_sb", [P, E1])
        w1_sb = sb("w1_sb", [P, E1, F1])
        b1_sb = sb("b1_sb", [P, 2 * E1])
        w2_sb = sb("w2_sb", [P, 2 * E1, C])
        b2_sb = sb("b2_sb", [P, C])
        r_col = sb("r_col", [P, 1])
        r_pow = sb("r_pow", [P, 4])

        h = sb("h", [P, NT, C])
        stats = sb("stats", [P, NT, 6])
        ln = sb("ln", [P, 10, NT])
        mean, rstd = ln[:, 0, :], ln[:, 1, :]
        norm = [sb(f"norm{i}", [P, C]) for i in range(4)]
        norm_t = [sb(f"norm_t{i}", [P, L]) for i in range(2)]

        xs = [sb(f"xs{i}", [P, L + 2 * PAD]) for i in range(2)]
        v_ext = sb("v_ext", [P, NHEAD, 2, DH + 1])
        o_raw = sb("o_raw", [P, NHEAD, 2, DH + 1])
        o_rec = sb("o_rec", [P, NHEAD, 2])
        o_den = sb("o_den", [P, NHEAD, 2])

        qk = sb("qk", [P, 2, 2, B * L])
        rest = sb("rest", [P, 2, B * L])
        piece = [[sb(f"piece{p}_{s}", [P, 2, B * L], BF16) for s in range(2)] for p in range(2)]

        k_op = [sb(f"k_op{i}", [P, 2, L], BF16) for i in range(2)]
        q_op = [sb(f"q_op{i}", [P, 2, DH * L], BF16) for i in range(2)]
        num = sb("num", [P, CHUNK])
        den = sb("den", [P, CHUNK])
        scale_f = sb("scale_f", [P, CHUNK])
        num_f = sb("num_f", [P, L])
        den_f = sb("den_f", [P, L])
        rec_f = sb("rec_f", [P, L])
        ratio = [sb(f"ratio{i}", [P, L]) for i in range(2)]
        score2 = sb("score2", [P, L])
        weight4 = [sb(f"weight4_{i}", [P, 2, L]) for i in range(2)]

        all_t = qk[:, 0, 0, :]
        tok_sum = sb("tok_sum", [P, B])
        lg0 = sb("lg0", [B, E0])
        ex0 = sb("ex0", [B, E0])
        top0 = sb("top0", [B, 8])
        idx0 = sb("idx0", [B, 8], U32)
        idx_row = sb("idx_row", [1, B], U32)
        sm0 = sb("sm0", [B, 8])
        gate_diag = sb("gate_diag", [B, B])
        gate_col = sb("gate_col", [P, B])
        w_sel = [sb(f"w_sel{i}", [P, C]) for i in range(2)]
        b_sel = [sb(f"b_sel{i}", [P, C]) for i in range(2)]
        tmp = [sb(f"tmp{i}", [P, C]) for i in range(4)]

        q1 = rest[:, 0, 0:4 * L].rearrange("p (a t) -> p a t", a=4)
        k1 = rest[:, 0, 4 * L:8 * L].rearrange("p (a t) -> p a t", a=4)
        v1 = rest[:, 1, 0:2 * INNER].rearrange("p (a t) -> p a t", a=2)
        neg_max = sb("neg_max", [P, 16])
        row_sum = sb("row_sum", [P, 16])
        row_rec = sb("row_rec", [P, 16])
        prob = [sb(f"prob{i}", [P, L]) for i in range(2)]
        prob_t = [sb(f"prob_t{i}", [P, 2, P]) for i in range(2)]
        o1 = rest[:, 1, 2 * INNER:3 * INNER]
        o1_t = rest[:, 1, 3 * INNER:4 * INNER].rearrange("p (a t) -> p a t", a=4)

        route = qk[:, 1, 1, 0:8 * NT * E1].rearrange("p (i t e) -> p i t e", i=8, t=NT)
        iota = sb("iota", [P, NT, E1])
        rsm = sb("rsm", [P, 10, NT])
        w_pad = sb("w_pad", [P, 4, 32])
        w_pad_t = sb("w_pad_t", [P, P])
        hid = [qk[:, 1, 0, i * 4 * P:(i + 1) * 4 * P] for i in range(4)]

        s_ident = sem("s_ident"); s_ones = sem("s_ones")
        s_w = sem("s_w"); s_w2 = sem("s_w2"); s_r = sem("s_r"); s_rpow = sem("s_rpow")
        s_late = sem("s_late")
        x_clear = sem("x_clear"); x_free = sem("x_free"); x_in = [sem(f"x_in{i}") for i in range(2)]
        conv_done = sem("conv_done"); conv_taken = sem("conv_taken")
        stats_done = sem("stats_done"); ln_chain = sem("ln_chain"); ln_var = sem("ln_var"); ln_std = sem("ln_std")
        v_set = sem("v_set")

        LNC = [0]

        def ln_math(dve, nth):
            def step(ins):
                LNC[0] += 1
                ins.then_inc(ln_chain, 1)
                dve.wait_ge(ln_chain, LNC[0])
            dve.wait_ge(stats_done, NT * (nth + 1))
            me, m2e, mo, m2o = stats[:, :, 1], stats[:, :, 2], stats[:, :, 4], stats[:, :, 5]
            s, d, d2, v, v2, var, sd, y, t = (ln[:, i, :] for i in (2, 3, 4, 5, 6, 7, 8, 9, 2))
            nc.vector.tensor_tensor(s, me, mo, ALU.add)
            nc.vector.tensor_tensor(d, me, mo, ALU.subtract)
            step(nc.vector.tensor_tensor(v, m2e, m2o, ALU.add))
            nc.vector.tensor_scalar(mean, s, 0.5, None, ALU.mult)
            nc.vector.tensor_tensor(d2, d, d, ALU.mult)
            step(nc.vector.tensor_scalar(v2, v, 1.0 / C, LN_EPS, ALU.mult, ALU.add))
            nc.vector.scalar_tensor_tensor(var, d2, 0.25, v2, ALU.mult, ALU.add).then_inc(ln_var, 1)
            dve.wait_ge(ln_std, nth + 1)
            step(nc.vector.reciprocal(y, sd))
            step(nc.vector.tensor_tensor(t, y, y, ALU.mult))
            step(nc.vector.tensor_tensor(t, t, var, ALU.mult))
            step(nc.vector.tensor_scalar(t, t, -0.5, 1.5, ALU.mult, ALU.add))
            step(nc.vector.tensor_tensor(rstd, y, t, ALU.mult))

        def ln_sqrt(act, nth):
            act.wait_ge(ln_var, nth + 1)
            nc.scalar.activation(ln[:, 8, :], ln[:, 7, :], ACT.Sqrt).then_inc(ln_std, 1)

        class Turn:
            def __init__(self, name):
                self.norm_ready = sem(name + "_norm_ready")
                self.norm_used = sem(name + "_norm_used")
                self.turned = sem(name + "_turned")
                self.copied = sem(name + "_copied")
                self.t_used = sem(name + "_t_used")

        t2, t5, t6, t7, t8 = (Turn(f"t{n}") for n in (2, 5, 6, 7, 8))

        qkv_done = sem("qkv_done"); qk_taken = sem("qk_taken"); v_taken = sem("v_taken")
        red = sem("red"); hi_done = sem("hi_done"); sub_done = sem("sub_done"); piece_out = [sem(f"piece_out{n}") for n in range(2 * NPIECE)]
        op_in = [sem(f"op_in{i}") for i in range(2)]; op_free = sem("op_free"); op_zero = sem("op_zero"); op_one = sem("op_one"); op_mask = sem("op_mask")
        mm_num = sem("mm_num"); mm_den = sem("mm_den"); sin_done = sem("sin_done")
        num_used = sem("num_used"); den_used = sem("den_used"); fold = sem("fold")
        ratio_ready = sem("ratio_ready"); sq_done = sem("sq_done"); w4_ready = sem("w4_ready")
        av_done = sem("av_done"); av_copied = sem("av_copied")
        o_chain = sem("o_chain"); proj_done = sem("proj_done"); proj_taken = sem("proj_taken"); h_sum = sem("h_sum")
        g_sum = sem("g_sum"); g_mm = sem("g_mm"); g_chain = sem("g_chain"); g_act = sem("g_act")
        g_idx = sem("g_idx"); g_row = sem("g_row"); g_in = [sem(f"g_in{i}") for i in range(2)]
        g_copied = sem("g_copied"); y_done = sem("y_done"); y_taken = sem("y_taken"); y_sum = sem("y_sum")
        p_done = sem("p_done"); p_act = sem("p_act"); p_dve = sem("p_dve")
        s_done = sem("s_done"); s_max = sem("s_max"); s_exp = sem("s_exp")
        pt_done = sem("pt_done"); pt_copied = sem("pt_copied"); pv_done = sem("pv_done"); o_norm = sem("o_norm")
        rr = sem("rr"); ot_done = sem("ot_done"); ot_copied = sem("ot_copied"); wo_done = sem("wo_done"); wo_sum = sem("wo_sum")
        h_add = sem("h_add")
        l_done = sem("l_done"); l_taken = sem("l_taken"); r_iota = sem("r_iota"); r_chain = sem("r_chain"); r_exp = sem("r_exp")
        wp_ready = sem("wp_ready"); wp_turned = sem("wp_turned"); wp_copied = sem("wp_copied")
        b2_done = sem("b2_done"); h_done = sem("h_done"); hid_ready = sem("hid_ready")
        e_done = sem("e_done"); e_sum = sem("e_sum"); out_done = sem("out_done"); wp_zero = sem("wp_zero")

        nW = [0, 0, 0]
        block = ctx.enter_context(nc.Block())

        @block.sync
        def _(sp):
            def load(dst, src, s, k):
                sp.dma_start(dst, src).then_inc(s, 16)
                nW[k] += 16
            cw = conv_w[0:8].rearrange("(j two) c o -> two c j o", two=2)
            load(conv_w_sb[0:CIN, 0:4, :], cw[0], s_w, 0)
            load(conv_w_sb[CIN:P, 0:4, :], cw[1], s_w, 0)
            load(conv_w_sb[0:CIN, 4, :], conv_w[8], s_w, 0)
            load(conv_b_sb[:, :], conv_b.rearrange("(a n) -> a n", a=1).to_broadcast([P, C]), s_w, 0)
            sp.wait_ge(x_clear, 2)
            with sp.Fori(0, B // 2) as it:
                for j in range(2):
                    sp.wait_ge(x_free, it * 2 + j + 1)
                    src = x[bass.ds(it * 2 + j, 1)].rearrange("a c l -> (a c) l")
                    sp.dma_start(xs[j][0:CIN, PAD:PAD + L], src).then_inc(x_in[j], 16)
                    sp.dma_start(xs[j][CIN:P, PAD - 1:PAD - 1 + L], src).then_inc(x_in[j], 16)
            sp.wait_ge(op_zero, 4)
            for j in range(2):
                for s in range(2):
                    sp.dma_start(q_op[j][0:KROWS, s, :], neg_mask).then_inc(op_mask, 16)
            for n in range(2 * NPIECE if STOP >= 3 else 0):
                p, s = n // 2, n % 2
                sp.wait_ge(hi_done, n + 1)
                t = piece[p % 2][s]
                sp.dma_start(q_dram[p, s].rearrange("(b g) (d t) -> (g d) b t", g=H, d=DH),
                             t[:, 0, :].rearrange("p (b t) -> p b t", b=B)).then_inc(piece_out[n], 16)
                sp.dma_start(k_dram[p, :, :, s, :].rearrange("(b g) d t -> (g d) b t", g=H),
                             t[:, 1, :].rearrange("p (b t) -> p b t", b=B)).then_inc(piece_out[n], 16)
            for n in range(2 * NPIECE if STOP >= 3 else 0):
                sp.wait_ge(piece_out[n], 32)
            with sp.Fori(0, NHEAD // 2 if STOP >= 4 else 1) as it:
                for j in range(2 if STOP >= 4 else 0):
                    i = it * 2 + j
                    sp.wait_ge(op_free, i + 1)
                    sp.dma_start(k_op[j][0:KROWS, :, :].rearrange("r s t -> r (s t)"),
                                 k_dram[:, bass.ds(i, 1)].rearrange("p i d s t -> p (i d) (s t)")).then_inc(op_in[j], 16)
                    sp.dma_start(q_op[j][QROW:QROW + NPIECE, :, :],
                                 q_dram[:, :, bass.ds(i, 1), :].rearrange("p s i n -> p s (i n)")).then_inc(op_in[j], 16)
            sp.wait_ge(g_idx, 1) if STOP >= 6 else None
            sp.dma_start(idx_row[0:1, :], idx0[:, 0:1]).then_inc(g_row, 16) if STOP >= 6 else None
            sp.wait_ge(g_row, 16) if STOP >= 6 else None
            with sp.Fori(0, B // 2 if STOP >= 6 else 1) as it:
                for j in range(2 if STOP >= 6 else 0):
                    sp.wait_ge(y_sum, it * 4 + (2 * j + 1))
                    e = sp.value_load(idx_row[0:1, bass.ds(it * 2 + j, 1)], min_val=0, max_val=E0 - 1)
                    sp.dma_start(w_sel[j][:, :], exp0_w[bass.ds(e, 1)].rearrange("a d o -> (a d) o")).then_inc(g_in[j], 16)
                    sp.dma_start(b_sel[j][:, :], exp0_b[bass.ds(e, 1), :].to_broadcast([P, C])).then_inc(g_in[j], 16)
            sp.wait_ge(e_sum, 1)
            sp.dma_start(out.rearrange("b (u p) c -> p (b u) c", p=P), h[:, :, :]).then_inc(out_done, 16)
            sp.wait_ge(out_done, 16)

        @block.gpsimd
        def _(pool):
            for j in range(2):
                nc.gpsimd.memset(xs[j][:, :], 0.0).then_inc(x_clear, 1)
            nc.gpsimd.memset(v_ext[:, :, :, :], 1.0).then_inc(v_set, 1)
            nc.gpsimd.memset(ones[:, :], 1.0).then_inc(s_ones, 1)
            for j in range(2):
                nc.gpsimd.memset(k_op[j][:, :, :], 0.0).then_inc(op_zero, 1)
                nc.gpsimd.memset(q_op[j][:, :, :], 0.0).then_inc(op_zero, 1)
            pool.wait_ge(op_zero, 4)
            for j in range(2):
                nc.gpsimd.memset(k_op[j][QROW:QROW + NPIECE, :, :], 1.0).then_inc(op_one, 1)
            pool.wait_ge(op_one, 2)
            nc.gpsimd.memset(w_pad[:, :, :], 0.0).then_inc(wp_zero, 1)
            nc.gpsimd.iota(iota[:, :, :], pattern=[[0, NT], [1, E1]], base=0, channel_multiplier=0,
                           allow_small_or_imprecise_dtypes=True).then_inc(r_iota, 1)

        @block.scalar
        def _(act):
            def load(dst, src, s, k):
                act.dma_start(dst, src).then_inc(s, 16)
                nW[k] += 16
            load(ident[:, :], ident_in, s_w2, 1)
            load(r_col[:, :], param_r.rearrange("(a n) -> a n", a=1).to_broadcast([P, 1]), s_w2, 1)
            load(w_qk_sb[:, :], w_qk, s_w2, 1)
            load(w_v_sb[:, :], w_v, s_w2, 1)
            load(w_proj_sb[:, :], w_proj, s_late, 2)
            load(b_proj_sb[:, :], b_proj.rearrange("(a n) -> a n", a=1).to_broadcast([P, C]), s_late, 2)
            load(gate0_w_sb[:, :], gate0_w, s_late, 2)
            load(gate0_b_sb[:, :], gate0_b.rearrange("(a n) -> a n", a=1).to_broadcast([B, E0]), s_late, 2)
            load(wq1_sb[:, :], wq1, s_late, 2)
            load(wk1_sb[:, :], wk1, s_late, 2)
            load(wv1_sb[:, :], wv1, s_late, 2)
            load(wo1_sb[:, :, :], wo1.rearrange("(k p) c -> p k c", p=P), s_late, 2)
            load(gate1_w_sb[:, :], gate1_w, s_late, 2)
            load(gate1_b_sb[:, :], gate1_b.rearrange("(a n) -> a n", a=1).to_broadcast([P, E1]), s_late, 2)
            load(w1_sb[:, :, :], w1.rearrange("e h f -> h e f"), s_late, 2)
            with nc.allow_non_contiguous_dma(reason="biases: 2048 single elements, once"):
                load(b1_sb[:, :], b1.rearrange("e (u p) -> p (e u)", p=P), s_late, 2)
            load(w2_sb[:, :, :], w2.rearrange("e (u p) h -> p (e u) h", p=P), s_late, 2)
            for t in range(4):
                load(b2_sb[32 * t:32 * t + E1, :], b2, s_late, 2)

            for s in (t2.copied, t5.copied, t6.copied, t8.copied, qk_taken, s_exp, hid_ready):
                act.sem_inc(s, 1)
            ln_sqrt(act, 0)
            if STOP <= 1:
                return
            act.wait_ge(s_w2, nW[1])
            with act.Fori(0, B // 2) as it:
                for j in range(2):
                    act.wait_ge(t2.turned, it * 4 + 2 * j + 2)
                    act.wait_ge(t2.t_used, it * 2 + (j + 1))
                    nc.scalar.copy(norm_t[j][:, :], bank[j][:, 0:L]).then_inc(t2.copied, 1)
                for j in range(2):
                    act.wait_ge(qkv_done, it * 4 + 2 * j + 1)
                    nc.scalar.activation(qk[:, 1, :, bass.ds((it * 2 + j) * L, L)],
                                         bank[2 + j][:, :].rearrange("p (s t) -> p s t", s=2),
                                         ACT.Copy, scale=r_col[:, 0:1]).then_inc(qk_taken, 1)
            for n in range(2 * NPIECE):
                p, s = n // 2, n % 2
                src = [[qk[:, 0], qk[:, 1]], [rest, qk[:, 0]], [rest, qk[:, 0]]]
                if p == 0:
                    act.wait_ge(red, 4) if s == 0 else act.wait_ge(qk_taken, B + 1)
                else:
                    act.wait_ge(sub_done, n - 1)
                if p == 2:
                    act.wait_ge(piece_out[s], 32)
                dst = piece[p % 2][s]
                in_ = (qk[:, s] if p == 0 else (rest[:, :, :] if s == 0 else qk[:, 0]))
                nc.scalar.copy(dst[:, :, :], in_).then_inc(hi_done, 1)
            if STOP <= 3:
                return
            act.wait_ge(s_rpow, 4)
            act.sem_inc(sq_done, 2)
            act.sem_inc(av_copied, 2)

            def squares(u_wait, i_wait, j, kt):
                act.wait_ge(ratio_ready, u_wait + 1)
                act.wait_ge(w4_ready, u_wait)
                nc.scalar.activation(score2[:, :], ratio[kt][:, :], ACT.Square,
                                     scale=r_pow[:, 3:4]).then_inc(sq_done, 1)
                act.wait_ge(sq_done, u_wait + 3)
                act.wait_ge(av_done, i_wait + 1)
                nc.scalar.activation(weight4[j][:, kt, :], score2[:, :], ACT.Square).then_inc(w4_ready, 1)

            def copy_av(i, j):
                act.wait_ge(av_done, i + 3)
                nc.scalar.copy(o_raw[:, bass.ds(i, 1), :, :].rearrange("p i u d -> p (i u d)"),
                               bank[6 + j][:, 0:2 * (DH + 1)]).then_inc(av_copied, 1)

            def sines(i, kt, c0, c1):
                for c in range(c0, c1):
                    act.wait_ge(mm_num, i * 16 + (kt * NCHUNK + c + 1))
                    a = bank[c % 4]
                    nc.scalar.activation(a[:, :], a[:, :], ACT.Sin).then_inc(sin_done, 1)

            def act_head(i, j, first):
                sines(i, 0, 0, 4)
                if not first:
                    squares(i * 2 - 1, i - 1, 1 - j, 1)
                sines(i, 0, 4, 8)
                sines(i, 1, 0, 4)
                squares(i * 2, i, j, 0)
                if not first:
                    copy_av(i - 1, 1 - j)
                sines(i, 1, 4, 8)

            act_head(0, 0, True)
            with act.Fori(0, NHEAD // 2 - 1) as it:
                act_head(it * 2 + 1, 1, False)
                act_head(it * 2 + 2, 0, False)
            act_head(NHEAD - 1, 1, False)
            squares(2 * NHEAD - 1, NHEAD - 1, 1, 1)
            copy_av(NHEAD - 1, 1)
            if STOP <= 4:
                return
            with act.Fori(0, B // 2) as it:
                for j in range(2):
                    act.wait_ge(t5.turned, it * 4 + 2 * j + 2)
                    act.wait_ge(t5.t_used, it * 2 + (j + 1))
                    nc.scalar.copy(norm_t[j][:, :], bank[j][:, 0:L]).then_inc(t5.copied, 1)
            if STOP <= 5:
                return
            ln_sqrt(act, 1)
            with act.Fori(0, B // 2) as it:
                for j in range(2):
                    act.wait_ge(t6.turned, it * 4 + 2 * j + 2)
                    nc.scalar.copy(all_t[:, bass.ds((it * 2 + j) * L, L)], bank[j][:, 0:L]).then_inc(t6.copied, 1)
            act.wait_ge(g_chain, 3)
            nc.scalar.activation(ex0[:, :], lg0[:, :], ACT.Exp, bias=sm0[:, 1:2], accum_out=sm0[:, 2:3]).then_inc(g_act, 1)
            with act.Fori(0, B // 2) as it:
                for j in range(2):
                    act.wait_ge(t6.t_used, it * 2 + (j + 1))
                    nc.scalar.copy(norm_t[j][:, :], all_t[:, bass.ds((it * 2 + j) * L, L)]).then_inc(g_copied, 1)
            if STOP <= 6:
                return
            ln_sqrt(act, 2)
            with act.Fori(0, B) as b:
                act.wait_ge(t7.turned, b * 2 + 2)
                nc.scalar.copy(norm_t[0][:, :], bank[0][:, 0:L]).then_inc(t7.copied, 1)
                act.wait_ge(p_done, b * 6 + 1)
                nc.scalar.activation(q1[:, 0:2, :], bank[1][:, :].rearrange("p (a t) -> p a t", a=2), ACT.Copy,
                                     scale=float(D1) ** -0.5).then_inc(p_act, 1)
                act.wait_ge(p_done, b * 6 + 3)
                nc.scalar.copy(k1[:, 0:2, :], bank[3][:, :].rearrange("p (a t) -> p a t", a=2)).then_inc(p_act, 1)
                act.wait_ge(p_done, b * 6 + 5)
                nc.scalar.copy(v1[:, 0, :], bank[2][:, :]).then_inc(p_act, 1)
                for m in range(16):
                    act.wait_ge(s_max, b * 16 + m + 1)
                    act.wait_ge(pt_done, b * 16 + (m + 1))
                    nc.scalar.activation(prob[m % 2][:, :], bank[4 + m % 2][:, 0:L], ACT.Exp,
                                         bias=neg_max[:, m:m + 1], accum_out=row_sum[:, m:m + 1]).then_inc(s_exp, 1)
                    if m in (12, 15):
                        act.wait_ge(ot_done, b * 2 + (2 if m == 12 else 3))
                        nc.scalar.copy(o1_t[:, :, :], bank[1][:, :].rearrange("p (a t) -> p a t", a=4)).then_inc(ot_copied, 1)
            if STOP <= 7:
                return
            ln_sqrt(act, 3)
            with act.Fori(0, B // 2) as it:
                for j in range(2):
                    act.wait_ge(t8.turned, it * 4 + 2 * j + 2)
                    act.wait_ge(t8.t_used, it * 2 + (j + 1))
                    nc.scalar.copy(norm_t[j][:, :], bank[j][:, 0:L]).then_inc(t8.copied, 1)
                    nc.scalar.copy(all_t[:, bass.ds((it * 2 + j) * L, L)], bank[j][:, 0:L]).then_inc(t8.copied, 1)
            act.wait_ge(r_chain, 10)
            nc.scalar.activation(rsm[:, 3, :], rsm[:, 2, :], ACT.Exp).then_inc(r_exp, 1)
            with act.Fori(0, NG) as g:
                for n in range(2 * E1):
                    act.wait_ge(h_done, g * 16 + n + 1)
                    act.wait_ge(e_done, g * 8 + (n // 2 + 1))
                    nc.scalar.activation(hid[n % 4][:, :], bank[n % 2][:, :], ACT.Relu,
                                         bias=b1_sb[:, n:n + 1]).then_inc(hid_ready, 1)

        @block.vector
        def _(dve):
            dve.sem_inc(conv_taken, 4)
            for s in (v_taken, proj_taken, y_taken, o_norm, wo_sum, pt_copied, l_taken, fold):
                dve.sem_inc(s, 1)
            dve.wait_ge(s_w, nW[0])
            with dve.Fori(0, B // 2) as it:
                for k in range(4):
                    n = it * 4 + k
                    dve.wait_ge(conv_done, n + 1)
                    nc.vector.tensor_tensor(h[:, bass.ds(n, 1), :].rearrange("p a c -> p (a c)"), bank[k][:, 0:C],
                                            conv_b_sb[:, :], ALU.add).then_inc(conv_taken, 1)
                    dve.wait_ge(conv_taken, n + 5)
                    nc.vector.bn_stats(stats[:, bass.ds(n, 1), :].rearrange("p a s -> p (a s)"),
                                       h[:, bass.ds(n, 1), :].rearrange("p a c -> p (a c)")).then_inc(stats_done, 1)
            ln_math(dve, 0)
            if STOP <= 1:
                dve.sem_inc(e_sum, 1)
                return

            def normalise(n, k, turn):
                dve.wait_ge(turn.norm_used, n + 1)
                nc.vector.tensor_scalar(norm[k][:, :], h[:, bass.ds(n, 1), :].rearrange("p a c -> p (a c)"),
                                        mean[:, bass.ds(n, 1)], rstd[:, bass.ds(n, 1)],
                                        ALU.subtract, ALU.mult).then_inc(turn.norm_ready, 1)

            dve.wait_ge(s_w2, nW[1])
            for n in range(4):
                a = r_col[:, 0:1] if n == 0 else r_pow[:, n - 1:n]
                if n:
                    dve.wait_ge(s_rpow, n)
                nc.vector.tensor_tensor(r_pow[:, n:n + 1], a, a, ALU.mult).then_inc(s_rpow, 1)
            dve.wait_ge(v_set, 1)
            with dve.Fori(0, B // 2) as it:
                for k in range(4):
                    normalise(it * 4 + k, k, t2)
                for j in range(2):
                    dve.wait_ge(qkv_done, it * 4 + 2 * j + 2)
                    for u in range(2):
                        nc.vector.tensor_copy(v_ext[:, bass.ds((it * 2 + j) * H, H), u, 0:DH],
                                              bank[4 + j][:, u * C:(u + 1) * C].rearrange("p (g d) -> p g d", g=H)
                                              ).then_inc(v_taken, 1)
            dve.wait_ge(qk_taken, B + 1)
            nc.vector.tensor_scalar(rest[:, :, :], qk[:, 1], 1.0 / PI, MAGIC, ALU.mult, ALU.add).then_inc(red, 1)
            dve.wait_ge(red, 1)
            nc.vector.tensor_scalar(rest[:, :, :], rest[:, :, :], MAGIC, -PI, ALU.subtract, ALU.mult).then_inc(red, 1)
            dve.wait_ge(red, 2)
            nc.vector.tensor_tensor(qk[:, 0], qk[:, 1], rest[:, :, :], ALU.add).then_inc(red, 1)
            dve.wait_ge(red, 3)
            nc.vector.tensor_scalar(qk[:, 0], qk[:, 0], HALF_PI, -HALF_PI, ALU.min, ALU.max).then_inc(red, 1)
            dve.wait_ge(red, 4)
            dve.wait_ge(hi_done, 1)
            nc.vector.tensor_tensor(rest[:, :, :], qk[:, 0], piece[0][0][:, :, :], ALU.subtract).then_inc(sub_done, 1)
            dve.wait_ge(hi_done, 2)
            dve.wait_ge(sub_done, 1)
            nc.vector.tensor_tensor(qk[:, 0], qk[:, 1], piece[0][1][:, :, :], ALU.subtract).then_inc(sub_done, 1)
            dve.wait_ge(hi_done, 3)
            nc.vector.tensor_tensor(rest[:, :, :], rest[:, :, :], piece[1][0][:, :, :], ALU.subtract).then_inc(sub_done, 1)
            dve.wait_ge(hi_done, 4)
            dve.wait_ge(sub_done, 2)
            nc.vector.tensor_tensor(qk[:, 0], qk[:, 0], piece[1][1][:, :, :], ALU.subtract).then_inc(sub_done, 1)
            if STOP <= 3:
                dve.sem_inc(e_sum, 1)
                return
            dve.sem_inc(num_used, 4)
            dve.sem_inc(den_used, 2)
            with dve.Fori(0, NHEAD // 2) as it:
                for j in range(2):
                    for kt in range(2):
                        u = it * 4 + (2 * j + kt)
                        n0 = it * 32 + (2 * j + kt) * NCHUNK
                        for c in range(NCHUNK):
                            dve.wait_ge(sin_done, n0 + (c + 1))
                            if c == 0:
                                dve.wait_ge(fold, u * 6 + 1)
                                nc.vector.tensor_scalar(num[:, :], bank[c % 4][:, :], GUARD, RANGE_SCALE,
                                                        ALU.add, ALU.mult).then_inc(num_used, 1)
                            else:
                                dve.wait_ge(num_used, n0 + (c + 4))
                                nc.vector.scalar_tensor_tensor(num[:, :], bank[c % 4][:, :], GUARD, num[:, :],
                                                               ALU.add, ALU.mult).then_inc(num_used, 1)
                            dve.wait_ge(mm_den, n0 + (c + 1))
                            if c == 0:
                                nc.vector.tensor_scalar(den[:, :], bank[4 + c % 2][:, :], GUARD, RANGE_SCALE,
                                                        ALU.add, ALU.mult).then_inc(den_used, 1)
                            else:
                                dve.wait_ge(den_used, n0 + (c + 2))
                                nc.vector.scalar_tensor_tensor(den[:, :], bank[4 + c % 2][:, :], GUARD, den[:, :],
                                                               ALU.add, ALU.mult).then_inc(den_used, 1)
                        dve.wait_ge(den_used, n0 + (NCHUNK + 2))
                        nc.vector.tensor_scalar(scale_f[:, :].bitcast(U32), den[:, :].bitcast(U32), EXP_EVEN, EXP_FLIP,
                                                ALU.bitwise_and, ALU.bitwise_xor).then_inc(fold, 1)
                        dve.wait_ge(fold, u * 6 + 2)
                        nc.vector.tensor_tensor(den[:, :], den[:, :], scale_f[:, :], ALU.mult).then_inc(fold, 1)
                        dve.wait_ge(num_used, n0 + (NCHUNK + 4))
                        nc.vector.tensor_tensor(num[:, :], num[:, :], scale_f[:, :], ALU.mult).then_inc(fold, 1)
                        dve.wait_ge(fold, u * 6 + 3)
                        nc.vector.tensor_tensor(den_f[:, :], den[:, 0:L], den[:, L:2 * L], ALU.mult).then_inc(fold, 1)
                        dve.wait_ge(fold, u * 6 + 4)
                        nc.vector.tensor_tensor(num_f[:, :], num[:, 0:L], num[:, L:2 * L], ALU.mult).then_inc(fold, 1)
                        dve.wait_ge(fold, u * 6 + 5)
                        nc.vector.reciprocal(rec_f[:, :], den_f[:, :]).then_inc(fold, 1)
                        dve.wait_ge(fold, u * 6 + 7)
                        dve.wait_ge(sq_done, u + 1)
                        nc.vector.tensor_tensor(ratio[kt][:, :], num_f[:, :], rec_f[:, :], ALU.mult).then_inc(ratio_ready, 1)
            if STOP <= 4:
                dve.sem_inc(e_sum, 1)
                return
            dve.wait_ge(av_copied, NHEAD + 2)
            nc.vector.tensor_scalar(o_den[:, :, :], o_raw[:, :, :, DH], ATTN_EPS, None, ALU.add).then_inc(o_chain, 1)
            dve.wait_ge(o_chain, 1)
            nc.vector.reciprocal(o_rec[:, :, :], o_den[:, :, :]).then_inc(o_chain, 1)
            dve.wait_ge(o_chain, 2)
            dve.wait_ge(s_late, nW[2])
            with dve.Fori(0, B // 2) as it:
                for k in range(4):
                    j, u = k // 2, k % 2
                    n = it * 4 + k
                    hs = bass.ds((it * 2 + j) * H, H)
                    dve.wait_ge(t5.norm_used, n + 1)
                    nc.vector.tensor_tensor(norm[k][:, :].rearrange("p (g d) -> p g d", g=H), o_raw[:, hs, u, 0:DH],
                                            o_rec[:, hs, u].unsqueeze(2).to_broadcast([P, H, DH]), ALU.mult
                                            ).then_inc(t5.norm_ready, 1)
                for k in range(4):
                    n = it * 4 + k
                    hn = h[:, bass.ds(n, 1), :].rearrange("p a c -> p (a c)")
                    dve.wait_ge(proj_done, n + 1)
                    nc.vector.tensor_tensor(tmp[k][:, :], bank[2 + k][:, 0:C], b_proj_sb[:, :], ALU.add).then_inc(proj_taken, 1)
                    dve.wait_ge(proj_taken, n + 2)
                    nc.vector.tensor_tensor(hn, tmp[k][:, :], hn, ALU.add).then_inc(h_sum, 1)
                    dve.wait_ge(h_sum, n + 1)
                    nc.vector.bn_stats(stats[:, bass.ds(n, 1), :].rearrange("p a s -> p (a s)"), hn).then_inc(stats_done, 1)
            if STOP <= 5:
                dve.wait_ge(stats_done, 2 * NT)
                dve.sem_inc(e_sum, 1)
                return
            ln_math(dve, 1)
            with dve.Fori(0, B // 2) as it:
                for k in range(4):
                    normalise(it * 4 + k, k, t6)
            dve.wait_ge(t6.copied, B + 1)
            nc.vector.tensor_reduce(tok_sum[:, :], all_t.rearrange("p (b t) -> p b t", b=B), AX.X, ALU.add).then_inc(g_sum, 1)
            dve.wait_ge(g_mm, 1)
            nc.vector.scalar_tensor_tensor(lg0[:, :], bank[6][0:B, 0:E0], 1.0 / L, gate0_b_sb[:, :],
                                           ALU.mult, ALU.add).then_inc(g_chain, 1)
            dve.wait_ge(g_chain, 1)
            nc.vector.tensor_reduce(sm0[:, 0:1], lg0[:, :], AX.X, ALU.max).then_inc(g_chain, 1)
            dve.wait_ge(g_chain, 2)
            nc.vector.tensor_scalar(sm0[:, 1:2], sm0[:, 0:1], -1.0, None, ALU.mult).then_inc(g_chain, 1)
            dve.wait_ge(g_act, 1)
            nc.vector.max(top0[:, :], ex0[:, :]).then_inc(g_chain, 1)
            nc.vector.reciprocal(sm0[:, 3:4], sm0[:, 2:3]).then_inc(g_chain, 1)
            dve.wait_ge(g_chain, 5)
            nc.vector.max_index(idx0[:, :], top0[:, :], ex0[:, :]).then_inc(g_idx, 1)
            nc.vector.tensor_tensor(sm0[:, 4:5], top0[:, 0:1], sm0[:, 3:4], ALU.mult).then_inc(g_chain, 1)
            dve.wait_ge(g_chain, 6)
            nc.vector.tensor_scalar(gate_diag[:, :], ident[0:B, 0:B], sm0[:, 4:5], None, ALU.mult).then_inc(g_chain, 1)
            dve.wait_ge(g_mm, 2)
            nc.vector.tensor_copy(gate_col[:, :], bank[6][:, 32:32 + B]).then_inc(g_chain, 1)
            dve.wait_ge(g_chain, 8)
            dve.sem_inc(y_sum, 3)
            with dve.Fori(0, B // 2) as it:
                for k in range(4):
                    j = k // 2
                    n = it * 4 + k
                    hn = h[:, bass.ds(n, 1), :].rearrange("p a c -> p (a c)")
                    dve.wait_ge(g_in[j], it * 32 + 32)
                    dve.wait_ge(y_done, n + 1)
                    nc.vector.tensor_tensor(tmp[k][:, :], bank[2 + k][:, 0:C], b_sel[j][:, :], ALU.add).then_inc(y_taken, 1)
                    dve.wait_ge(y_taken, n + 2)
                    nc.vector.scalar_tensor_tensor(hn, tmp[k][:, :], gate_col[:, bass.ds(it * 2 + j, 1)], hn,
                                                   ALU.mult, ALU.add).then_inc(y_sum, 1)
                    dve.wait_ge(y_sum, n + 4)
                    nc.vector.bn_stats(stats[:, bass.ds(n, 1), :].rearrange("p a s -> p (a s)"), hn).then_inc(stats_done, 1)
            if STOP <= 6:
                dve.wait_ge(stats_done, 3 * NT)
                dve.sem_inc(e_sum, 1)
                return
            ln_math(dve, 2)
            with dve.Fori(0, B) as b:
                for u in range(2):
                    hn = h[:, bass.ds(b * 2 + u, 1), :].rearrange("p a c -> p (a c)")
                    normalise(b * 2 + u, u, t7)
                    dve.wait_ge(t7.norm_ready, b * 2 + (u + 1))
                    nc.vector.tensor_tensor(hn, hn, norm[u][:, :], ALU.add).then_inc(h_add, 1)
                dve.wait_ge(p_done, b * 6 + 2)
                nc.vector.tensor_scalar(q1[:, 2:4, :], bank[2][:, :].rearrange("p (a t) -> p a t", a=2),
                                        float(D1) ** -0.5, None, ALU.mult).then_inc(p_dve, 1)
                dve.wait_ge(p_done, b * 6 + 4)
                nc.vector.tensor_copy(k1[:, 2:4, :], bank[1][:, :].rearrange("p (a t) -> p a t", a=2)).then_inc(p_dve, 1)
                dve.wait_ge(p_done, b * 6 + 6)
                nc.vector.tensor_copy(v1[:, 1, :], bank[3][:, :]).then_inc(p_dve, 1)

                def maxima(m):
                    dve.wait_ge(s_done, b * 16 + (m + 1))
                    nc.vector.tensor_reduce(neg_max[:, m:m + 1], bank[4 + m % 2][:, 0:L], AX.X, ALU.max,
                                            negate=True).then_inc(s_max, 1)

                def copy_pt(m):
                    dve.wait_ge(pt_done, b * 16 + (m + 3))
                    dve.wait_ge(pv_done, b * 16 + (m + 1))
                    nc.vector.tensor_copy(prob_t[m % 2][:, :, :],
                                          bank[6 - 3 * (m % 2)][:, 0:L].rearrange("p (a t) -> p a t", a=2)
                                          ).then_inc(pt_copied, 1)

                def norm_o(u):
                    o_ps = bank[7] if u == 0 else bank[0]
                    dve.wait_ge(s_exp, b * 16 + (8 * (u + 1) + 1))
                    nc.vector.reciprocal(row_rec[:, 8 * u:8 * u + 8], row_sum[:, 8 * u:8 * u + 8]).then_inc(rr, 1)
                    dve.wait_ge(rr, b * 2 + (u + 1))
                    dve.wait_ge(pv_done, b * 16 + (8 * (u + 1) + 2))
                    dve.wait_ge(ot_done, b * 2 + (u + 1))
                    nc.vector.tensor_tensor(o1.rearrange("p (g d) -> p g d", g=H1),
                                            o_ps[:, :].rearrange("p (g d) -> p g d", g=H1),
                                            row_rec[:, 8 * u:8 * u + 8].unsqueeze(2).to_broadcast([P, H1, D1]),
                                            ALU.mult).then_inc(o_norm, 1)

                def add_wo(u):
                    hn = h[:, bass.ds(b * 2 + u, 1), :].rearrange("p a c -> p (a c)")
                    dve.wait_ge(wo_done, b * 2 + (u + 1))
                    dve.wait_ge(h_add, b * 2 + (u + 1))
                    nc.vector.tensor_tensor(hn, bank[2][:, 0:C], hn, ALU.add).then_inc(wo_sum, 1)
                    dve.wait_ge(wo_sum, b * 2 + (u + 2))
                    nc.vector.bn_stats(stats[:, bass.ds(b * 2 + u, 1), :].rearrange("p a s -> p (a s)"), hn).then_inc(stats_done, 1)

                maxima(0)
                for m in range(16):
                    if m + 1 < 16:
                        maxima(m + 1)
                    copy_pt(m)
                    if m == 9:
                        norm_o(0)
                    if m == 13:
                        add_wo(0)
                norm_o(1)
                add_wo(1)
            if STOP <= 7:
                dve.wait_ge(stats_done, 4 * NT)
                dve.sem_inc(e_sum, 1)
                return
            ln_math(dve, 3)
            LG, A, M1, C1, M2, C2, WT, W2 = (route[:, i] for i in range(8))
            with dve.Fori(0, B // 2) as it:
                for k in range(4):
                    normalise(it * 4 + k, k, t8)
                for k in range(4):
                    dve.wait_ge(l_done, it * 4 + (k + 1))
                    nc.vector.tensor_tensor(LG[:, bass.ds(it * 4 + k, 1), :].rearrange("p a e -> p (a e)"),
                                            bank[2 + k][:, 0:E1], gate1_b_sb[:, :], ALU.add).then_inc(l_taken, 1)
            cnt = [0]

            def step(ins):
                cnt[0] += 1
                ins.then_inc(r_chain, 1)
                dve.wait_ge(r_chain, cnt[0])

            def wide(a):
                return a.unsqueeze(2).to_broadcast([P, NT, E1])
            dve.wait_ge(l_taken, NT + 1)
            dve.wait_ge(r_iota, 1)
            best, second, first_at, second_at = (rsm[:, i, :] for i in (0, 1, 4, 5))
            step(nc.vector.tensor_reduce(best, LG, AX.X, ALU.max))
            step(nc.vector.tensor_tensor(A, LG, wide(best), ALU.is_lt))
            step(nc.vector.scalar_tensor_tensor(C1, A, float(E1), iota[:, :, :], ALU.mult, ALU.add))
            step(nc.vector.tensor_reduce(first_at, C1, AX.X, ALU.min))
            step(nc.vector.tensor_tensor(M1, iota[:, :, :], wide(first_at), ALU.is_equal))
            step(nc.vector.scalar_tensor_tensor(C1, M1, -3e38, LG, ALU.mult, ALU.add))
            step(nc.vector.tensor_reduce(second, C1, AX.X, ALU.max))
            step(nc.vector.tensor_tensor(A, C1, wide(second), ALU.is_lt))
            step(nc.vector.scalar_tensor_tensor(C2, A, float(E1), iota[:, :, :], ALU.mult, ALU.add))
            step(nc.vector.tensor_tensor(rsm[:, 2, :], second, best, ALU.subtract))
            step(nc.vector.tensor_reduce(second_at, C2, AX.X, ALU.min))
            step(nc.vector.tensor_tensor(M2, iota[:, :, :], wide(second_at), ALU.is_equal))
            dve.wait_ge(r_exp, 1)
            step(nc.vector.tensor_scalar(rsm[:, 6, :], rsm[:, 3, :], 1.0, None, ALU.add))
            step(nc.vector.reciprocal(rsm[:, 7, :], rsm[:, 6, :]))
            step(nc.vector.tensor_tensor(rsm[:, 8, :], rsm[:, 3, :], rsm[:, 7, :], ALU.mult))
            step(nc.vector.tensor_tensor(WT, M1, wide(rsm[:, 7, :]), ALU.mult))
            step(nc.vector.tensor_tensor(W2, M2, wide(rsm[:, 8, :]), ALU.mult))
            step(nc.vector.tensor_tensor(WT, WT, W2, ALU.add))
            dve.wait_ge(wp_zero, 1)
            with dve.Fori(0, NG) as g:
                dve.wait_ge(wp_turned, g + 1)
                nc.vector.tensor_copy(w_pad[:, :, 0:E1], WT[:, bass.ds(g * 4, 4), :]).then_inc(wp_ready, 1)
                dve.wait_ge(wp_turned, g + 2)
                dve.wait_ge(b2_done, g * 4 + 1)
                nc.vector.tensor_copy(w_pad_t[:, :], bank[6][:, 0:P]).then_inc(wp_copied, 1)
                hg = h[:, bass.ds(g * 4, 4), :]
                dve.wait_ge(b2_done, g * 4 + 5)
                nc.vector.tensor_tensor(hg, bank[7][:, :].rearrange("p (a c) -> p a c", a=4), hg, ALU.add).then_inc(h_add, 1)
                dve.wait_ge(h_add, g + (NT + 1))
                for e in range(E1):
                    dve.wait_ge(e_done, g * 8 + (e + 3))
                    if e:
                        dve.wait_ge(y_taken, g * 32 + (NT + 4 * e + 1))
                    for t in range(4):
                        hn = h[:, bass.ds(g * 4 + t, 1), :].rearrange("p a c -> p (a c)")
                        nc.vector.scalar_tensor_tensor(hn, bank[2 + e % 2][:, t * C:(t + 1) * C],
                                                       WT[:, bass.ds(g * 4 + t, 1), e], hn,
                                                       ALU.mult, ALU.add).then_inc(y_taken, 1)
            dve.wait_ge(y_taken, NT + NG * 32 + 1)
            dve.sem_inc(e_sum, 1)

        @block.tensor
        def _(pe):
            pe.wait_ge(s_w, nW[0])
            pe.sem_inc(x_free, 2)
            with pe.Fori(0, B // 2) as it:
                for j in range(2):
                    pe.wait_ge(x_in[j], it * 32 + 32)
                    for u in range(2):
                        k = 2 * j + u
                        pe.wait_ge(conv_taken, it * 4 + (k + 1))
                        for t in range(5):
                            rows = P if t < 4 else CIN
                            mm = nc.tensor.matmul(bank[k][:, 0:C], xs[j][0:rows, u * P + 2 * t:u * P + 2 * t + P],
                                                  conv_w_sb[0:rows, t, :], start=(t == 0), stop=(t == 4))
                        mm.then_inc(conv_done, 1)
                        if u == 1:
                            pe.wait_ge(conv_done, it * 4 + (k + 1))
                            pe.sem_inc(x_free, 1)
            if STOP <= 1:
                return

            def turn(tile0, j, ks, t, dst=None):
                for u in range(2):
                    pe.wait_ge(t.norm_ready, tile0 + (u + 1))
                    nc.tensor.transpose(bank[j][:, u * P:(u + 1) * P], norm[ks + u][:, :], ident[:, :]).then_inc(t.turned, 1)

            pe.wait_ge(s_w2, nW[1])
            pe.sem_inc(t2.norm_used, 4)
            pe.sem_inc(t2.t_used, 2)
            with pe.Fori(0, B // 2) as it:
                for j in range(2):
                    pe.wait_ge(t2.copied, it * 2 + 1)
                    turn(it * 4 + 2 * j, j, 2 * j, t2)
                pe.wait_ge(t2.turned, it * 4 + 4)
                pe.sem_inc(t2.norm_used, 4)
                for j in range(2):
                    pe.wait_ge(t2.copied, it * 2 + (j + 2))
                    pe.wait_ge(qk_taken, it * 2 + 1)
                    pe.wait_ge(v_taken, it * 4 + 1)
                    for s in range(2):
                        mm = nc.tensor.matmul(bank[2 + j][:, s * L:(s + 1) * L], w_qk_sb[:, s * C:(s + 1) * C],
                                              norm_t[j][:, :], start=True, stop=True)
                    mm.then_inc(qkv_done, 1)
                    for u in range(2):
                        mm = nc.tensor.matmul(bank[4 + j][:, u * C:(u + 1) * C], norm_t[j][:, u * P:(u + 1) * P],
                                              w_v_sb[:, :], start=True, stop=True)
                    mm.then_inc(qkv_done, 1)
                    pe.wait_ge(qkv_done, it * 4 + 2 * j + 2)
                    pe.sem_inc(t2.t_used, 1)
            if STOP <= 3:
                return
            pe.wait_ge(qk_taken, B + 1)
            pe.wait_ge(v_taken, NT + 1)
            pe.wait_ge(op_one, 2)
            pe.wait_ge(op_mask, 64)
            pe.sem_inc(op_free, 2)
            pe.sem_inc(av_done, 2)

            def chunks(i, j, kt, c0, c1):
                for c in range(c0, c1):
                    n = i * 16 + (kt * NCHUNK + c)
                    pe.wait_ge(num_used, n + 1)
                    nc.tensor.matmul(bank[c % 4][:, :], k_op[j][0:ROWS, 0, kt * P:(kt + 1) * P],
                                     q_op[j][0:ROWS, 0, c * CHUNK:(c + 1) * CHUNK], start=True, stop=True).then_inc(mm_num, 1)
                    pe.wait_ge(den_used, n + 1)
                    nc.tensor.matmul(bank[4 + c % 2][:, :], k_op[j][0:ROWS, 1, kt * P:(kt + 1) * P],
                                     q_op[j][0:ROWS, 1, c * CHUNK:(c + 1) * CHUNK], start=True, stop=True).then_inc(mm_den, 1)

            def attend(i, j):
                pe.wait_ge(w4_ready, i * 2 + 2)
                pe.wait_ge(av_copied, i + 1)
                for u in range(2):
                    for kt in range(2):
                        mm = nc.tensor.matmul(bank[6 + j][:, u * (DH + 1):(u + 1) * (DH + 1)],
                                              weight4[j][:, kt, u * P:(u + 1) * P],
                                              v_ext[:, bass.ds(i, 1), kt, :].rearrange("p a d -> p (a d)"),
                                              start=(kt == 0), stop=(kt == 1))
                mm.then_inc(av_done, 1)

            def pe_head(i, wait_in, j, first):
                pe.wait_ge(op_in[j], wait_in)
                chunks(i, j, 0, 0, 8)
                chunks(i, j, 1, 0, 4)
                if not first:
                    attend(i - 1, 1 - j)
                chunks(i, j, 1, 4, 8)
                pe.wait_ge(mm_den, i * 16 + 16)
                pe.sem_inc(op_free, 1)

            pe_head(0, 32, 0, True)
            with pe.Fori(0, NHEAD // 2 - 1) as it:
                pe_head(it * 2 + 1, it * 32 + 32, 1, False)
                pe_head(it * 2 + 2, it * 32 + 64, 0, False)
            pe_head(NHEAD - 1, 32 * (NHEAD // 2), 1, False)
            attend(NHEAD - 1, 1)
            if STOP <= 4:
                return
            pe.sem_inc(t5.norm_used, 4)
            pe.sem_inc(t5.t_used, 2)
            pe.wait_ge(s_late, nW[2])
            with pe.Fori(0, B // 2) as it:
                for j in range(2):
                    pe.wait_ge(t5.copied, it * 2 + 1)
                    turn(it * 4 + 2 * j, j, 2 * j, t5)
                pe.wait_ge(t5.turned, it * 4 + 4)
                pe.sem_inc(t5.norm_used, 4)
                for j in range(2):
                    pe.wait_ge(t5.copied, it * 2 + (j + 2))
                    for u in range(2):
                        pe.wait_ge(proj_taken, it * 4 + 1)
                        nc.tensor.matmul(bank[2 + 2 * j + u][:, 0:C], norm_t[j][:, u * P:(u + 1) * P],
                                         w_proj_sb[:, :], start=True, stop=True).then_inc(proj_done, 1)
                    pe.wait_ge(proj_done, it * 4 + 2 * j + 2)
                    pe.sem_inc(t5.t_used, 1)
            if STOP <= 5:
                return
            pe.sem_inc(t6.norm_used, 4)
            with pe.Fori(0, B // 2) as it:
                for j in range(2):
                    pe.wait_ge(t6.copied, it * 2 + 1)
                    turn(it * 4 + 2 * j, j, 2 * j, t6)
                pe.wait_ge(t6.turned, it * 4 + 4)
                pe.sem_inc(t6.norm_used, 4)
            pe.wait_ge(g_sum, 1)
            nc.tensor.matmul(bank[6][0:B, 0:E0], tok_sum[:, :], gate0_w_sb[:, :], start=True, stop=True).then_inc(g_mm, 1)
            pe.wait_ge(g_chain, 7)
            pe.wait_ge(s_ones, 1)
            nc.tensor.matmul(bank[6][:, 32:32 + B], ones[0:B, :], gate_diag[:, :], start=True, stop=True).then_inc(g_mm, 1)
            pe.sem_inc(t6.t_used, 2)
            with pe.Fori(0, B // 2) as it:
                for j in range(2):
                    pe.wait_ge(g_copied, it * 2 + (j + 1))
                    pe.wait_ge(g_in[j], it * 32 + 32)
                    pe.wait_ge(y_taken, it * 4 + 1)
                    for u in range(2):
                        nc.tensor.matmul(bank[2 + 2 * j + u][:, 0:C], norm_t[j][:, u * P:(u + 1) * P],
                                         w_sel[j][:, :], start=True, stop=True).then_inc(y_done, 1)
                    pe.wait_ge(y_done, it * 4 + 2 * j + 2)
                    pe.sem_inc(t6.t_used, 1)
            if STOP <= 6:
                return
            pe.wait_ge(y_taken, NT + 1)
            pe.sem_inc(t7.norm_used, 2)
            pe.sem_inc(pt_done, 2)
            pe.sem_inc(pv_done, 2)
            pe.sem_inc(ot_done, 1)
            with pe.Fori(0, B) as b:
                pe.wait_ge(o_norm, b * 2 + 1)
                turn(b * 2, 0, 0, t7)
                pe.wait_ge(t7.turned, b * 2 + 2)
                pe.wait_ge(h_add, b * 2 + 2)
                pe.sem_inc(t7.norm_used, 2)
                pe.wait_ge(t7.copied, b + 1)
                pe.wait_ge(wo_sum, b * 2 + 1)
                for n, w in enumerate((wq1_sb, wq1_sb, wk1_sb, wk1_sb)):
                    if n == 3:
                        pe.wait_ge(p_act, b * 3 + 1)
                    for a in range(2):
                        g = 2 * (n % 2) + a
                        mm = nc.tensor.matmul(bank[1 + n % 3][:, a * L:(a + 1) * L], w[:, g * P:(g + 1) * P],
                                              norm_t[0][:, :], start=True, stop=True)
                    mm.then_inc(p_done, 1)
                for u in range(2):
                    pe.wait_ge(p_dve, b * 3 + 1) if u == 0 else pe.wait_ge(p_act, b * 3 + 2)
                    nc.tensor.matmul(bank[2 + u][:, :], norm_t[0][:, u * P:(u + 1) * P], wv1_sb[:, :],
                                     start=True, stop=True).then_inc(p_done, 1)
                pe.wait_ge(p_dve, b * 3 + 3)
                pe.wait_ge(p_act, b * 3 + 3)

                def logits(m):
                    u, g = m // 8, m % 8
                    r = D1 * (g % 2)
                    pe.wait_ge(s_exp, b * 16 + m) if m else None
                    nc.tensor.matmul(bank[4 + m % 2][:, 0:L], q1[r:r + D1, g // 2, u * P:(u + 1) * P],
                                     k1[r:r + D1, g // 2, :], start=True, stop=True).then_inc(s_done, 1)

                def turn_prob(m):
                    pe.wait_ge(s_exp, b * 16 + (m + 2))
                    pe.wait_ge(pt_copied, b * 16 + m) if m else None
                    for a in range(2):
                        mm = nc.tensor.transpose(bank[6 - 3 * (m % 2)][:, a * P:(a + 1) * P],
                                                 prob[m % 2][:, a * P:(a + 1) * P], ident[:, :])
                    mm.then_inc(pt_done, 1)

                def values(m):
                    u, g = m // 8, m % 8
                    o_ps = bank[7] if u == 0 else bank[0]
                    pe.wait_ge(pt_copied, b * 16 + (m + 2))
                    if m == 0:
                        pe.wait_ge(o_norm, b * 2 + 1)
                    for a in range(2):
                        mm = nc.tensor.matmul(o_ps[:, g * D1:(g + 1) * D1], prob_t[m % 2][:, a, :],
                                              v1[:, a, g * D1:(g + 1) * D1], start=(a == 0), stop=(a == 1))
                    mm.then_inc(pv_done, 1)

                def project(u):
                    pe.wait_ge(o_norm, b * 2 + (u + 2))
                    for a in range(4):
                        mm = nc.tensor.transpose(bank[1][:, a * P:(a + 1) * P], o1[:, a * P:(a + 1) * P], ident[:, :])
                    mm.then_inc(ot_done, 1)
                    pe.wait_ge(ot_copied, b * 2 + (u + 1))
                    pe.wait_ge(wo_sum, b * 2 + (u + 1))
                    for a in range(4):
                        mm = nc.tensor.matmul(bank[2][:, 0:C], o1_t[:, a, :], wo1_sb[:, a, :], start=(a == 0), stop=(a == 3))
                    mm.then_inc(wo_done, 1)

                logits(0)
                for m in range(16):
                    if m + 1 < 16:
                        logits(m + 1)
                    turn_prob(m)
                    if m:
                        values(m - 1)
                    if m == 11:
                        project(0)
                values(15)
                project(1)
            if STOP <= 7:
                return
            pe.sem_inc(t8.norm_used, 4)
            pe.sem_inc(t8.t_used, 2)
            with pe.Fori(0, B // 2) as it:
                for j in range(2):
                    pe.wait_ge(t8.copied, it * 4 + 1)
                    turn(it * 4 + 2 * j, j, 2 * j, t8)
                pe.wait_ge(t8.turned, it * 4 + 4)
                pe.sem_inc(t8.norm_used, 4)
                for j in range(2):
                    pe.wait_ge(t8.copied, it * 4 + (2 * (j + 1) + 1))
                    pe.wait_ge(l_taken, it * 4 + 1)
                    for u in range(2):
                        nc.tensor.matmul(bank[2 + 2 * j + u][:, 0:E1], norm_t[j][:, u * P:(u + 1) * P],
                                         gate1_w_sb[:, :], start=True, stop=True).then_inc(l_done, 1)
                    pe.wait_ge(l_done, it * 4 + 2 * j + 2)
                    pe.sem_inc(t8.t_used, 1)
            pe.wait_ge(l_taken, NT + 1)
            pe.sem_inc(e_done, 2)
            pe.sem_inc(wp_turned, 1)
            pe.sem_inc(b2_done, 1)
            with pe.Fori(0, NG) as g:
                pe.wait_ge(wp_ready, g + 1)
                nc.tensor.transpose(bank[6][:, 0:P], w_pad[:, :, :].rearrange("p a e -> p (a e)"), ident[:, :]).then_inc(wp_turned, 1)
                pe.wait_ge(wp_copied, g + 1)
                pe.wait_ge(h_add, g + NT)
                for t in range(4):
                    if t:
                        pe.wait_ge(b2_done, g * 4 + (t + 1))
                    nc.tensor.matmul(bank[7][:, t * C:(t + 1) * C], w_pad_t[32 * t:32 * t + E1, :],
                                     b2_sb[32 * t:32 * t + E1, :], start=True, stop=True).then_inc(b2_done, 1)

                def hidden(e):
                    for f in range(2):
                        n = 2 * e + f
                        pe.wait_ge(hid_ready, g * 16 + n) if n else None
                        nc.tensor.matmul(bank[n % 2][:, :], w1_sb[:, e, f * P:(f + 1) * P],
                                         all_t[:, bass.ds(g * 512, 512)], start=True, stop=True).then_inc(h_done, 1)

                def second(e):
                    pe.wait_ge(hid_ready, g * 16 + (2 * e + 3))
                    pe.wait_ge(y_taken, g * 32 + (NT + 4 * (e - 1) + 1))
                    for t in range(4):
                        for f in range(2):
                            mm = nc.tensor.matmul(bank[2 + e % 2][:, t * C:(t + 1) * C],
                                                  hid[(2 * e + f) % 4][:, t * P:(t + 1) * P], w2_sb[:, 2 * e + f, :],
                                                  start=(f == 0), stop=(f == 1))
                    mm.then_inc(e_done, 1)

                hidden(0)
                for e in range(E1):
                    if e + 1 < E1:
                        hidden(e + 1)
                    second(e)


_ORDER = ["x", "conv_w", "conv_b", "w_qk", "w_v", "w_proj", "b_proj", "param_r", "gate0_w", "gate0_b", "exp0_w",
          "exp0_b", "wq1", "wk1", "wv1", "wo1", "gate1_w", "gate1_b", "w1", "b1", "w2", "b2", "neg_mask", "ident_in"]


def kernel(x, L0_tok_weight, L0_tok_bias, L0_attn_w_qkv, L0_attn_w_proj, L0_attn_b_proj, L0_attn_paramR, L0_ffn_Wg,
           L0_ffn_bg, L0_ffn_We, L0_ffn_be, L1_attn_Wq, L1_attn_Wk, L1_attn_Wv, L1_attn_Wo, L1_ffn_gate_w,
           L1_ffn_gate_b, L1_ffn_w1, L1_ffn_b1, L1_ffn_w2, L1_ffn_b2):
    import ml_dtypes
    import concourse.bacc as bacc
    from concourse.bass_utils import run_bass_kernel_spmd

    qkv_t = np.asarray(L0_attn_w_qkv).T
    mask = np.zeros((NPIECE, DH, DH, L), ml_dtypes.bfloat16)
    for d in range(DH):
        mask[:, d, d, :] = -1
    data = dict(
        x=x, conv_w=np.transpose(L0_tok_weight, (2, 1, 0)), conv_b=L0_tok_bias, w_qk=qkv_t[:, 0:2 * C],
        w_v=qkv_t[:, 2 * C:3 * C], w_proj=np.transpose(L0_attn_w_proj), b_proj=L0_attn_b_proj,
        param_r=L0_attn_paramR, gate0_w=L0_ffn_Wg, gate0_b=L0_ffn_bg, exp0_w=L0_ffn_We, exp0_b=L0_ffn_be,
        wq1=np.transpose(L1_attn_Wq), wk1=np.transpose(L1_attn_Wk), wv1=np.transpose(L1_attn_Wv),
        wo1=np.transpose(L1_attn_Wo), gate1_w=L1_ffn_gate_w, gate1_b=L1_ffn_gate_b, w1=L1_ffn_w1, b1=L1_ffn_b1,
        w2=L1_ffn_w2, b2=L1_ffn_b2, neg_mask=mask.reshape(KROWS, DH * L), ident_in=np.eye(P, dtype=np.float32))
    nc = bacc.Bacc("TRN2", target_bir_lowering=False, num_devices=1)
    arrays, args = {}, []
    for name in _ORDER:
        a = np.ascontiguousarray(data[name])
        arrays[f"in_{name}"] = a
        args.append(nc.dram_tensor(f"in_{name}", a.shape, mybir.dt.from_np(a.dtype), kind="ExternalInput").ap())
    args.append(nc.dram_tensor("out_0", (B, L, C), F32, kind="ExternalOutput").ap())
    build(nc, *args)
    r = run_bass_kernel_spmd(nc, [arrays], core_ids=[0])
    return r.results[0]["out_0"]
```

```python
from contextlib import ExitStack

import numpy as np
import concourse.bass as bass
from concourse import mybir

ALU = mybir.AluOpType
ACT = mybir.ActivationFunctionType
AX = mybir.AxisListType
F32 = mybir.dt.float32
BF16 = mybir.dt.bfloat16
U32 = mybir.dt.uint32

STOP = 99

P = 128
B, CIN, L = 8, 64, 256
C, TAPS, PAD = 128, 9, 4
NT = B * L // P
H, DH = 8, 16
NHEAD = B * H
NPIECE = 3
KROWS = NPIECE * DH
QROW = 64
ROWS = QROW + NPIECE
LANES = 4
CHUNK = LANES * L
HALF = CHUNK // 2
EARLY, ATTEND = 7, 6
NCHUNK = DH // LANES
NUNIT = 2 * NHEAD
GUARD = 1e-7
LANE_SCALE = 2.0 ** 31
EXP_EVEN = 0x7F000000
EXP_FLIP = 0x7F800000
ATTN_EPS = 1e-6
LN_EPS = 1e-5
MAGIC = 1.5 * 2.0 ** 23
PI = float(np.float32(np.pi))
HALF_PI = float(np.nextafter(np.float32(np.pi / 2), np.float32(0)))
E0 = 16
H1, D1 = 8, 64
INNER = H1 * D1
E1, F1 = 8, 256
NG = 4


def build(nc, x, conv_w, conv_b, w_qk, w_v, w_proj, b_proj, param_r, gate0_w, gate0_b, exp0_w, exp0_b,
          wq1, wk1, wv1, wo1, gate1_w, gate1_b, w1, b1, w2, b2, neg_mask, ident_in, out):
    with ExitStack() as ctx:
        def sb(name, shape, dt=F32):
            return ctx.enter_context(nc.sbuf_tensor(name, shape, dt))

        def sem(name):
            return ctx.enter_context(nc.semaphore(name))

        pair = [ctx.enter_context(nc.psum_tensor(f"pair{i}", [P, 1024], F32)) for i in range(4)]
        bank = [pair[i // 2][:, (i % 2) * 512:(i % 2 + 1) * 512] for i in range(8)]

        q_dram = nc.dram_tensor("q_pieces", [NPIECE, 2, NHEAD, DH * L], BF16, kind="Internal").ap()
        k_dram = nc.dram_tensor("k_pieces", [NPIECE, NHEAD, DH, 2, L], BF16, kind="Internal").ap()

        ident = sb("ident", [P, P])
        ones = sb("ones", [P, P])
        conv_w_sb = sb("conv_w_sb", [P, 5, C])
        conv_b_sb = sb("conv_b_sb", [P, C])
        w_qk_sb = sb("w_qk_sb", [P, 2 * C])
        w_v_sb = sb("w_v_sb", [P, C])
        w_proj_sb = sb("w_proj_sb", [P, C])
        b_proj_sb = sb("b_proj_sb", [P, C])
        gate0_w_sb = sb("gate0_w_sb", [P, E0])
        gate0_b_sb = sb("gate0_b_sb", [B, E0])
        wq1_sb = sb("wq1_sb", [P, INNER])
        wk1_sb = sb("wk1_sb", [P, INNER])
        wv1_sb = sb("wv1_sb", [P, INNER])
        wo1_sb = sb("wo1_sb", [P, INNER // P, C])
        gate1_w_sb = sb("gate1_w_sb", [P, E1])
        gate1_b_sb = sb("gate1_b_sb", [P, E1])
        w1_sb = sb("w1_sb", [P, E1, F1])
        b1_sb = sb("b1_sb", [P, 2 * E1])
        w2_sb = sb("w2_sb", [P, 2 * E1, C])
        b2_sb = sb("b2_sb", [P, C])
        r_col = sb("r_col", [P, 1])
        r_pow = sb("r_pow", [P, 4])

        h = sb("h", [P, NT, C])
        stats = sb("stats", [P, NT, 6])
        ln = sb("ln", [P, 10, NT])
        mean, rstd = ln[:, 0, :], ln[:, 1, :]
        norm = [sb(f"norm{i}", [P, C]) for i in range(4)]
        norm_t = [sb(f"norm_t{i}", [P, L]) for i in range(2)]

        xs = [sb(f"xs{i}", [P, L + 2 * PAD]) for i in range(2)]
        v_ext = sb("v_ext", [P, NHEAD, 2, DH + 1])
        o_raw = sb("o_raw", [P, NHEAD, 2, DH + 1])
        o_rec = sb("o_rec", [P, NHEAD, 2])
        o_den = sb("o_den", [P, NHEAD, 2])

        qk = sb("qk", [P, 2, 2, B * L])
        rest = sb("rest", [P, 2, B * L])
        piece = [[sb(f"piece{p}_{s}", [P, 2, B * L], BF16) for s in range(2)] for p in range(2)]

        k_op = [sb(f"k_op{i}", [P, 2, L], BF16) for i in range(2)]
        q_op = [sb(f"q_op{i}", [P, 2, DH * L], BF16) for i in range(2)]
        num = [rest[:, 0, i * CHUNK:(i + 1) * CHUNK] for i in range(2)]
        den = [rest[:, 1, i * CHUNK:(i + 1) * CHUNK] for i in range(2)]
        first_sin = qk[:, 0, 0, 0:CHUNK]
        guard_col = sb("guard_col", [P, 1])
        num8 = qk[:, 0, 1, 0:2 * L]
        den8 = qk[:, 0, 1, 2 * L:4 * L]
        scale_f = sb("scale_f", [P, 2 * L])
        num_f = sb("num_f", [P, L])
        den_f = sb("den_f", [P, L])
        num_x = qk[:, 0, 0, CHUNK:CHUNK + L].rearrange("p (a t) -> p a t", a=2)
        den_pair = sb("den_pair", [P, P])
        rec_pair = sb("rec_pair", [P, P])
        ratio = [sb(f"ratio{i}", [P, L]) for i in range(2)]
        score2 = sb("score2", [P, L])
        weight4 = [sb(f"weight4_{i}", [P, 2, L]) for i in range(2)]

        all_t = qk[:, 0, 0, :]
        tok_sum = sb("tok_sum", [P, B])
        lg0 = sb("lg0", [B, E0])
        ex0 = sb("ex0", [B, E0])
        top0 = sb("top0", [B, 8])
        idx0 = sb("idx0", [B, 8], U32)
        idx_row = sb("idx_row", [1, B], U32)
        sm0 = sb("sm0", [B, 8])
        gate_diag = sb("gate_diag", [B, B])
        gate_col = sb("gate_col", [P, B])
        w_sel = [sb(f"w_sel{i}", [P, C]) for i in range(2)]
        b_sel = [sb(f"b_sel{i}", [P, C]) for i in range(2)]
        tmp = [sb(f"tmp{i}", [P, C]) for i in range(4)]

        q1 = rest[:, 0, 0:4 * L].rearrange("p (a t) -> p a t", a=4)
        k1 = rest[:, 0, 4 * L:8 * L].rearrange("p (a t) -> p a t", a=4)
        v1 = rest[:, 1, 0:2 * INNER].rearrange("p (a t) -> p a t", a=2)
        neg_max = sb("neg_max", [P, 16])
        row_sum = sb("row_sum", [P, 16])
        row_rec = sb("row_rec", [P, 16])
        prob = [sb(f"prob{i}", [P, L]) for i in range(2)]
        prob_t = [sb(f"prob_t{i}", [P, 2, P]) for i in range(2)]
        o1 = rest[:, 1, 2 * INNER:3 * INNER]
        o1_t = rest[:, 1, 3 * INNER:4 * INNER].rearrange("p (a t) -> p a t", a=4)

        route = qk[:, 1, 1, 0:8 * NT * E1].rearrange("p (i t e) -> p i t e", i=8, t=NT)
        iota = sb("iota", [P, NT, E1])
        rsm = sb("rsm", [P, 10, NT])
        w_pad = sb("w_pad", [P, 4, 32])
        w_pad_t = sb("w_pad_t", [P, P])
        hid = [qk[:, 1, 0, i * 4 * P:(i + 1) * 4 * P] for i in range(4)]

        s_ident = sem("s_ident"); s_ones = sem("s_ones")
        s_w = sem("s_w"); s_w2 = sem("s_w2"); s_r = sem("s_r"); s_rpow = sem("s_rpow")
        s_late = sem("s_late")
        x_clear = sem("x_clear"); x_free = sem("x_free"); x_in = [sem(f"x_in{i}") for i in range(2)]
        conv_done = sem("conv_done"); conv_taken = sem("conv_taken")
        stats_done = sem("stats_done"); ln_chain = sem("ln_chain"); ln_var = sem("ln_var"); ln_std = sem("ln_std")
        v_set = sem("v_set")

        LNC = [0]

        def ln_math(dve, nth):
            def step(ins):
                LNC[0] += 1
                ins.then_inc(ln_chain, 1)
                dve.wait_ge(ln_chain, LNC[0])
            dve.wait_ge(stats_done, NT * (nth + 1))
            me, m2e, mo, m2o = stats[:, :, 1], stats[:, :, 2], stats[:, :, 4], stats[:, :, 5]
            s, d, d2, v, v2, var, sd, y, t = (ln[:, i, :] for i in (2, 3, 4, 5, 6, 7, 8, 9, 2))
            nc.vector.tensor_tensor(s, me, mo, ALU.add)
            nc.vector.tensor_tensor(d, me, mo, ALU.subtract)
            step(nc.vector.tensor_tensor(v, m2e, m2o, ALU.add))
            nc.vector.tensor_scalar(mean, s, 0.5, None, ALU.mult)
            nc.vector.tensor_tensor(d2, d, d, ALU.mult)
            step(nc.vector.tensor_scalar(v2, v, 1.0 / C, LN_EPS, ALU.mult, ALU.add))
            nc.vector.scalar_tensor_tensor(var, d2, 0.25, v2, ALU.mult, ALU.add).then_inc(ln_var, 1)
            dve.wait_ge(ln_std, nth + 1)
            step(nc.vector.reciprocal(y, sd))
            step(nc.vector.tensor_tensor(t, y, y, ALU.mult))
            step(nc.vector.tensor_tensor(t, t, var, ALU.mult))
            step(nc.vector.tensor_scalar(t, t, -0.5, 1.5, ALU.mult, ALU.add))
            step(nc.vector.tensor_tensor(rstd, y, t, ALU.mult))

        def ln_sqrt(act, nth):
            act.wait_ge(ln_var, nth + 1)
            nc.scalar.activation(ln[:, 8, :], ln[:, 7, :], ACT.Sqrt).then_inc(ln_std, 1)

        class Turn:
            def __init__(self, name):
                self.norm_ready = sem(name + "_norm_ready")
                self.norm_used = sem(name + "_norm_used")
                self.turned = sem(name + "_turned")
                self.copied = sem(name + "_copied")
                self.t_used = sem(name + "_t_used")

        t2, t5, t6, t7, t8 = (Turn(f"t{n}") for n in (2, 5, 6, 7, 8))

        qkv_done = sem("qkv_done"); qk_taken = sem("qk_taken"); v_taken = sem("v_taken")
        red = sem("red"); hi_done = sem("hi_done"); sub_done = sem("sub_done"); piece_out = [sem(f"piece_out{n}") for n in range(2 * NPIECE)]
        op_in = [sem(f"op_in{i}") for i in range(2)]; op_zero = sem("op_zero"); op_one = sem("op_one"); op_mask = sem("op_mask")
        mm_num = sem("mm_num"); mm_den = sem("mm_den"); sin_done = sem("sin_done")
        num_used = sem("num_used"); den_used = sem("den_used")
        mm_early = sem("mm_early"); early_taken = sem("early_taken"); num_first = sem("num_first"); guard_set = sem("guard_set")
        den8_done = sem("den8_done"); num8_done = sem("num8_done"); scale_done = sem("scale_done")
        den_scaled = sem("den_scaled"); num_scaled = sem("num_scaled"); den_f_done = sem("den_f_done"); den_pair_done = sem("den_pair_done"); num_x_done = sem("num_x_done")
        num_f_done = sem("num_f_done"); rec_done = sem("rec_done")
        ratio_ready = sem("ratio_ready"); sq_done = sem("sq_done"); w4_ready = sem("w4_ready")
        av_done = sem("av_done"); av_copied = sem("av_copied")
        o_chain = sem("o_chain"); proj_done = sem("proj_done"); proj_taken = sem("proj_taken"); h_sum = sem("h_sum")
        g_sum = sem("g_sum"); g_mm = sem("g_mm"); g_chain = sem("g_chain"); g_act = sem("g_act")
        g_idx = sem("g_idx"); g_row = sem("g_row"); g_in = [sem(f"g_in{i}") for i in range(2)]
        g_copied = sem("g_copied"); y_done = sem("y_done"); y_taken = sem("y_taken"); y_sum = sem("y_sum")
        p_done = sem("p_done"); p_act = sem("p_act"); p_dve = sem("p_dve")
        s_done = sem("s_done"); s_max = sem("s_max"); s_exp = sem("s_exp")
        pt_done = sem("pt_done"); pt_copied = sem("pt_copied"); pv_done = sem("pv_done"); o_norm = sem("o_norm")
        rr = sem("rr"); ot_done = sem("ot_done"); ot_copied = sem("ot_copied"); wo_done = sem("wo_done"); wo_sum = sem("wo_sum")
        h_add = sem("h_add")
        l_done = sem("l_done"); l_taken = sem("l_taken"); r_iota = sem("r_iota"); r_chain = sem("r_chain"); r_exp = sem("r_exp")
        wp_ready = sem("wp_ready"); wp_turned = sem("wp_turned"); wp_copied = sem("wp_copied")
        b2_done = sem("b2_done"); h_done = sem("h_done"); hid_ready = sem("hid_ready")
        e_done = sem("e_done"); e_sum = sem("e_sum"); out_done = sem("out_done"); wp_zero = sem("wp_zero")

        def wait(eng, s, value):
            if not isinstance(value, int) or value > 0:
                eng.wait_ge(s, value)

        nW = [0, 0, 0]
        block = ctx.enter_context(nc.Block())

        @block.sync
        def _(sp):
            def load(dst, src, s, k):
                sp.dma_start(dst, src).then_inc(s, 16)
                nW[k] += 16
            cw = conv_w[0:8].rearrange("(j two) c o -> two c j o", two=2)
            load(conv_w_sb[0:CIN, 0:4, :], cw[0], s_w, 0)
            load(conv_w_sb[CIN:P, 0:4, :], cw[1], s_w, 0)
            load(conv_w_sb[0:CIN, 4, :], conv_w[8], s_w, 0)
            load(conv_b_sb[:, :], conv_b.rearrange("(a n) -> a n", a=1).to_broadcast([P, C]), s_w, 0)
            sp.wait_ge(x_clear, 2)
            with sp.Fori(0, B // 2) as it:
                for j in range(2):
                    sp.wait_ge(x_free, it * 2 + j + 1)
                    src = x[bass.ds(it * 2 + j, 1)].rearrange("a c l -> (a c) l")
                    sp.dma_start(xs[j][0:CIN, PAD:PAD + L], src).then_inc(x_in[j], 16)
                    sp.dma_start(xs[j][CIN:P, PAD - 1:PAD - 1 + L], src).then_inc(x_in[j], 16)
            sp.wait_ge(op_zero, 4)
            for j in range(2):
                for s in range(2):
                    sp.dma_start(q_op[j][0:KROWS, s, :], neg_mask).then_inc(op_mask, 16)
            for n in range(2 * NPIECE if STOP >= 3 else 0):
                p, s = n // 2, n % 2
                sp.wait_ge(hi_done, n + 1)
                t = piece[p % 2][s]
                sp.dma_start(q_dram[p, s].rearrange("(b g) (d t) -> (g d) b t", g=H, d=DH),
                             t[:, 0, :].rearrange("p (b t) -> p b t", b=B)).then_inc(piece_out[n], 16)
                sp.dma_start(k_dram[p, :, :, s, :].rearrange("(b g) d t -> (g d) b t", g=H),
                             t[:, 1, :].rearrange("p (b t) -> p b t", b=B)).then_inc(piece_out[n], 16)
            for n in range(2 * NPIECE if STOP >= 3 else 0):
                sp.wait_ge(piece_out[n], 32)
            def load_operands(i, j):
                if not isinstance(i, int):
                    sp.wait_ge(mm_den, i * 6 - 6)
                sp.dma_start(k_op[j][0:KROWS, :, :].rearrange("r s t -> r (s t)"),
                             k_dram[:, bass.ds(i, 1)].rearrange("p i d s t -> p (i d) (s t)")).then_inc(op_in[j], 16)
                sp.dma_start(q_op[j][QROW:QROW + NPIECE, :, :],
                             q_dram[:, :, bass.ds(i, 1), :].rearrange("p s i n -> p s (i n)")).then_inc(op_in[j], 16)

            for j in range(2):
                load_operands(j, j)
            with sp.Fori(1, NHEAD // 2) as it:
                for j in range(2):
                    load_operands(it * 2 + j, j)
            sp.wait_ge(g_idx, 1) if STOP >= 6 else None
            sp.dma_start(idx_row[0:1, :], idx0[:, 0:1]).then_inc(g_row, 16) if STOP >= 6 else None
            sp.wait_ge(g_row, 16) if STOP >= 6 else None
            with sp.Fori(0, B // 2 if STOP >= 6 else 1) as it:
                for j in range(2 if STOP >= 6 else 0):
                    sp.wait_ge(y_sum, it * 4 + (2 * j + 1))
                    e = sp.value_load(idx_row[0:1, bass.ds(it * 2 + j, 1)], min_val=0, max_val=E0 - 1)
                    sp.dma_start(w_sel[j][:, :], exp0_w[bass.ds(e, 1)].rearrange("a d o -> (a d) o")).then_inc(g_in[j], 16)
                    sp.dma_start(b_sel[j][:, :], exp0_b[bass.ds(e, 1), :].to_broadcast([P, C])).then_inc(g_in[j], 16)
            sp.wait_ge(e_sum, 1)
            sp.dma_start(out.rearrange("b (u p) c -> p (b u) c", p=P), h[:, :, :]).then_inc(out_done, 16)
            sp.wait_ge(out_done, 16)

        @block.gpsimd
        def _(pool):
            for j in range(2):
                nc.gpsimd.memset(xs[j][:, :], 0.0).then_inc(x_clear, 1)
            nc.gpsimd.memset(v_ext[:, :, :, :], 1.0).then_inc(v_set, 1)
            nc.gpsimd.memset(ones[:, :], 1.0).then_inc(s_ones, 1)
            for j in range(2):
                nc.gpsimd.memset(k_op[j][:, :, :], 0.0).then_inc(op_zero, 1)
                nc.gpsimd.memset(q_op[j][:, :, :], 0.0).then_inc(op_zero, 1)
            pool.wait_ge(op_zero, 4)
            for j in range(2):
                nc.gpsimd.memset(k_op[j][QROW:QROW + NPIECE, :, :], 1.0).then_inc(op_one, 1)
            pool.wait_ge(op_one, 2)
            nc.gpsimd.memset(w_pad[:, :, :], 0.0).then_inc(wp_zero, 1)
            nc.gpsimd.memset(guard_col[:, :], GUARD * LANE_SCALE).then_inc(guard_set, 1)
            nc.gpsimd.iota(iota[:, :, :], pattern=[[0, NT], [1, E1]], base=0, channel_multiplier=0,
                           allow_small_or_imprecise_dtypes=True).then_inc(r_iota, 1)

            if STOP <= 3:
                return

            def half(dst, src, n):
                return nc.gpsimd.tensor_tensor(dst, src[:, 0:n], src[:, n:2 * n], ALU.mult)

            def quotient(u, par):
                pool.wait_ge(den_used, u * 3 + 3)
                half(den8[:, :], den[par], 2 * L).then_inc(den8_done, 1)
                pool.wait_ge(num_used, u * 3 + 3)
                half(num8[:, :], num[par], 2 * L).then_inc(num8_done, 1)
                pool.wait_ge(scale_done, u + 1)
                pool.wait_ge(den8_done, u + 1)
                nc.gpsimd.tensor_tensor(den8[:, :], den8[:, :], scale_f[:, :], ALU.mult).then_inc(den_scaled, 1)
                pool.wait_ge(num8_done, u + 1)
                nc.gpsimd.tensor_tensor(num8[:, :], num8[:, :], scale_f[:, :], ALU.mult).then_inc(num_scaled, 1)
                pool.wait_ge(den_scaled, u + 1)
                half(den_f[:, :], den8, L).then_inc(den_f_done, 1)
                pool.wait_ge(den_f_done, u + 1)
                wait(pool, rec_done, u)
                half(den_pair[:, :], den_f, P).then_inc(den_pair_done, 1)
                pool.wait_ge(num_scaled, u + 1)
                half(num_f[:, :], num8, L).then_inc(num_f_done, 1)
                pool.wait_ge(num_f_done, u + 1)
                nc.gpsimd.tensor_tensor(num_x[:, :, :], num_f[:, :].rearrange("p (a t) -> p a t", a=2),
                                        den_f[:, :].rearrange("p (a t) -> p a t", a=2)[:, ::-1, :],
                                        ALU.mult).then_inc(num_x_done, 1)
                pool.wait_ge(num_x_done, u + 1)
                pool.wait_ge(rec_done, u + 1)
                wait(pool, sq_done, u - 1)
                nc.gpsimd.tensor_tensor(ratio[par][:, :].rearrange("p (a t) -> p a t", a=2), num_x[:, :, :],
                                        rec_pair[:, :].unsqueeze(1).to_broadcast([P, 2, P]),
                                        ALU.mult).then_inc(ratio_ready, 1)

            for k in range(4):
                quotient(k, k % 2)
            with pool.Fori(1, NUNIT // 4) as it:
                for k in range(4):
                    quotient(it * 4 + k, k % 2)

        @block.scalar
        def _(act):
            def load(dst, src, s, k):
                act.dma_start(dst, src).then_inc(s, 16)
                nW[k] += 16
            load(ident[:, :], ident_in, s_w2, 1)
            load(r_col[:, :], param_r.rearrange("(a n) -> a n", a=1).to_broadcast([P, 1]), s_w2, 1)
            load(w_qk_sb[:, :], w_qk, s_w2, 1)
            load(w_v_sb[:, :], w_v, s_w2, 1)
            load(w_proj_sb[:, :], w_proj, s_late, 2)
            load(b_proj_sb[:, :], b_proj.rearrange("(a n) -> a n", a=1).to_broadcast([P, C]), s_late, 2)
            load(gate0_w_sb[:, :], gate0_w, s_late, 2)
            load(gate0_b_sb[:, :], gate0_b.rearrange("(a n) -> a n", a=1).to_broadcast([B, E0]), s_late, 2)
            load(wq1_sb[:, :], wq1, s_late, 2)
            load(wk1_sb[:, :], wk1, s_late, 2)
            load(wv1_sb[:, :], wv1, s_late, 2)
            load(wo1_sb[:, :, :], wo1.rearrange("(k p) c -> p k c", p=P), s_late, 2)
            load(gate1_w_sb[:, :], gate1_w, s_late, 2)
            load(gate1_b_sb[:, :], gate1_b.rearrange("(a n) -> a n", a=1).to_broadcast([P, E1]), s_late, 2)
            load(w1_sb[:, :, :], w1.rearrange("e h f -> h e f"), s_late, 2)
            with nc.allow_non_contiguous_dma(reason="biases: 2048 single elements, once"):
                load(b1_sb[:, :], b1.rearrange("e (u p) -> p (e u)", p=P), s_late, 2)
            load(w2_sb[:, :, :], w2.rearrange("e (u p) h -> p (e u) h", p=P), s_late, 2)
            for t in range(4):
                load(b2_sb[32 * t:32 * t + E1, :], b2, s_late, 2)

            for s in (t2.copied, t5.copied, t6.copied, t8.copied, qk_taken, s_exp, hid_ready):
                act.sem_inc(s, 1)
            ln_sqrt(act, 0)
            if STOP <= 1:
                return
            act.wait_ge(s_w2, nW[1])
            with act.Fori(0, B // 2) as it:
                for j in range(2):
                    act.wait_ge(t2.turned, it * 4 + 2 * j + 2)
                    act.wait_ge(t2.t_used, it * 2 + (j + 1))
                    nc.scalar.copy(norm_t[j][:, :], bank[j][:, 0:L]).then_inc(t2.copied, 1)
                for j in range(2):
                    act.wait_ge(qkv_done, it * 4 + 2 * j + 1)
                    nc.scalar.activation(qk[:, 1, :, bass.ds((it * 2 + j) * L, L)],
                                         bank[2 + j][:, :].rearrange("p (s t) -> p s t", s=2),
                                         ACT.Copy, scale=r_col[:, 0:1]).then_inc(qk_taken, 1)
            for n in range(2 * NPIECE):
                p, s = n // 2, n % 2
                src = [[qk[:, 0], qk[:, 1]], [rest, qk[:, 0]], [rest, qk[:, 0]]]
                if p == 0:
                    act.wait_ge(red, 4) if s == 0 else act.wait_ge(qk_taken, B + 1)
                else:
                    act.wait_ge(sub_done, n - 1)
                if p == 2:
                    act.wait_ge(piece_out[s], 32)
                dst = piece[p % 2][s]
                in_ = (qk[:, s] if p == 0 else (rest[:, :, :] if s == 0 else qk[:, 0]))
                nc.scalar.copy(dst[:, :, :], in_).then_inc(hi_done, 1)
            if STOP <= 3:
                return
            act.wait_ge(s_rpow, 4)
            act.wait_ge(guard_set, 1)
            act.sem_inc(av_copied, 1)

            def squares(u, i, par, j):
                wait(act, w4_ready, u)
                act.wait_ge(ratio_ready, u + 1)
                nc.scalar.activation(score2[:, :], ratio[par][:, :], ACT.Square,
                                     scale=r_pow[:, 3:4]).then_inc(sq_done, 1)
                act.wait_ge(sq_done, u + 1)
                wait(act, av_done, i)
                nc.scalar.activation(weight4[j][:, par, :], score2[:, :], ACT.Square).then_inc(w4_ready, 1)

            def copy_av(i):
                act.wait_ge(av_done, i + 2)
                nc.scalar.copy(o_raw[:, bass.ds(i, 1), :, :].rearrange("p i u d -> p (i u d)"),
                               bank[ATTEND][:, 0:2 * (DH + 1)]).then_inc(av_copied, 1)

            def take_early(u, par, n):
                act.wait_ge(mm_early, u * 4 + (n + 1))
                if n < 2:
                    wait(act, num_first, u)
                    nc.scalar.activation(first_sin[:, n * HALF:(n + 1) * HALF], bank[EARLY],
                                         ACT.Sin).then_inc(early_taken, 1)
                else:
                    wait(act, den8_done, u - 1)
                    nc.scalar.activation(den[par][:, (n - 2) * HALF:(n - 1) * HALF], bank[EARLY], ACT.Identity,
                                         bias=guard_col[:, 0:1], scale=LANE_SCALE).then_inc(early_taken, 1)

            def first_factors(u, par):
                act.wait_ge(early_taken, u * 4 + 2)
                wait(act, num8_done, u - 1)
                nc.scalar.activation(num[par], first_sin, ACT.Identity, bias=guard_col[:, 0:1],
                                     scale=LANE_SCALE).then_inc(num_first, 1)

            def sines(u, par, c):
                act.wait_ge(mm_num, u * 3 + c)
                a = pair[(c - 1 + par) % 2]
                nc.scalar.activation(a[:, :], a[:, :], ACT.Sin).then_inc(sin_done, 1)

            def act_slot(q, k, first, last):
                u, i, par = q * 4 + k, q * 2 + k // 2, k % 2
                has_next = not (last and k == 3)
                sines(u, par, 1)
                take_early(u, par, 3)
                if has_next:
                    take_early(u + 1, 1 - par, 0)
                sines(u, par, 2)
                if not (first and k < 2):
                    squares(u - 2, i - 1, par, (k // 2 + 1) % 2)
                if has_next:
                    take_early(u + 1, 1 - par, 1)
                sines(u, par, 3)
                if has_next:
                    take_early(u + 1, 1 - par, 2)
                    first_factors(u + 1, 1 - par)
                if par == 1 and not first:
                    copy_av(i - 2)

            for n in range(3):
                take_early(0, 0, n)
            first_factors(0, 0)
            for k in range(4):
                act_slot(0, k, True, False)
            with act.Fori(1, NUNIT // 4 - 1) as it:
                for k in range(4):
                    act_slot(it, k, False, False)
            for k in range(4):
                act_slot(NUNIT // 4 - 1, k, False, True)
            squares(NUNIT - 2, NHEAD - 1, 0, 1)
            copy_av(NHEAD - 2)
            squares(NUNIT - 1, NHEAD - 1, 1, 1)
            copy_av(NHEAD - 1)
            if STOP <= 4:
                return
            with act.Fori(0, B // 2) as it:
                for j in range(2):
                    act.wait_ge(t5.turned, it * 4 + 2 * j + 2)
                    act.wait_ge(t5.t_used, it * 2 + (j + 1))
                    nc.scalar.copy(norm_t[j][:, :], bank[j][:, 0:L]).then_inc(t5.copied, 1)
            if STOP <= 5:
                return
            ln_sqrt(act, 1)
            with act.Fori(0, B // 2) as it:
                for j in range(2):
                    act.wait_ge(t6.turned, it * 4 + 2 * j + 2)
                    nc.scalar.copy(all_t[:, bass.ds((it * 2 + j) * L, L)], bank[j][:, 0:L]).then_inc(t6.copied, 1)
            act.wait_ge(g_chain, 3)
            nc.scalar.activation(ex0[:, :], lg0[:, :], ACT.Exp, bias=sm0[:, 1:2], accum_out=sm0[:, 2:3]).then_inc(g_act, 1)
            with act.Fori(0, B // 2) as it:
                for j in range(2):
                    act.wait_ge(t6.t_used, it * 2 + (j + 1))
                    nc.scalar.copy(norm_t[j][:, :], all_t[:, bass.ds((it * 2 + j) * L, L)]).then_inc(g_copied, 1)
            if STOP <= 6:
                return
            ln_sqrt(act, 2)
            with act.Fori(0, B) as b:
                act.wait_ge(t7.turned, b * 2 + 2)
                nc.scalar.copy(norm_t[0][:, :], bank[0][:, 0:L]).then_inc(t7.copied, 1)
                act.wait_ge(p_done, b * 6 + 1)
                nc.scalar.activation(q1[:, 0:2, :], bank[1][:, :].rearrange("p (a t) -> p a t", a=2), ACT.Copy,
                                     scale=float(D1) ** -0.5).then_inc(p_act, 1)
                act.wait_ge(p_done, b * 6 + 3)
                nc.scalar.copy(k1[:, 0:2, :], bank[3][:, :].rearrange("p (a t) -> p a t", a=2)).then_inc(p_act, 1)
                act.wait_ge(p_done, b * 6 + 5)
                nc.scalar.copy(v1[:, 0, :], bank[2][:, :]).then_inc(p_act, 1)
                for m in range(16):
                    act.wait_ge(s_max, b * 16 + m + 1)
                    act.wait_ge(pt_done, b * 16 + (m + 1))
                    nc.scalar.activation(prob[m % 2][:, :], bank[4 + m % 2][:, 0:L], ACT.Exp,
                                         bias=neg_max[:, m:m + 1], accum_out=row_sum[:, m:m + 1]).then_inc(s_exp, 1)
                    if m in (12, 15):
                        act.wait_ge(ot_done, b * 2 + (2 if m == 12 else 3))
                        nc.scalar.copy(o1_t[:, :, :], bank[1][:, :].rearrange("p (a t) -> p a t", a=4)).then_inc(ot_copied, 1)
            if STOP <= 7:
                return
            ln_sqrt(act, 3)
            with act.Fori(0, B // 2) as it:
                for j in range(2):
                    act.wait_ge(t8.turned, it * 4 + 2 * j + 2)
                    act.wait_ge(t8.t_used, it * 2 + (j + 1))
                    nc.scalar.copy(norm_t[j][:, :], bank[j][:, 0:L]).then_inc(t8.copied, 1)
                    nc.scalar.copy(all_t[:, bass.ds((it * 2 + j) * L, L)], bank[j][:, 0:L]).then_inc(t8.copied, 1)
            act.wait_ge(r_chain, 10)
            nc.scalar.activation(rsm[:, 3, :], rsm[:, 2, :], ACT.Exp).then_inc(r_exp, 1)
            with act.Fori(0, NG) as g:
                for n in range(2 * E1):
                    act.wait_ge(h_done, g * 16 + n + 1)
                    act.wait_ge(e_done, g * 8 + (n // 2 + 1))
                    nc.scalar.activation(hid[n % 4][:, :], bank[n % 2][:, :], ACT.Relu,
                                         bias=b1_sb[:, n:n + 1]).then_inc(hid_ready, 1)

        @block.vector
        def _(dve):
            dve.sem_inc(conv_taken, 4)
            for s in (v_taken, proj_taken, y_taken, o_norm, wo_sum, pt_copied, l_taken):
                dve.sem_inc(s, 1)
            dve.wait_ge(s_w, nW[0])
            with dve.Fori(0, B // 2) as it:
                for k in range(4):
                    n = it * 4 + k
                    dve.wait_ge(conv_done, n + 1)
                    nc.vector.tensor_tensor(h[:, bass.ds(n, 1), :].rearrange("p a c -> p (a c)"), bank[k][:, 0:C],
                                            conv_b_sb[:, :], ALU.add).then_inc(conv_taken, 1)
                    dve.wait_ge(conv_taken, n + 5)
                    nc.vector.bn_stats(stats[:, bass.ds(n, 1), :].rearrange("p a s -> p (a s)"),
                                       h[:, bass.ds(n, 1), :].rearrange("p a c -> p (a c)")).then_inc(stats_done, 1)
            ln_math(dve, 0)
            if STOP <= 1:
                dve.sem_inc(e_sum, 1)
                return

            def normalise(n, k, turn):
                dve.wait_ge(turn.norm_used, n + 1)
                nc.vector.tensor_scalar(norm[k][:, :], h[:, bass.ds(n, 1), :].rearrange("p a c -> p (a c)"),
                                        mean[:, bass.ds(n, 1)], rstd[:, bass.ds(n, 1)],
                                        ALU.subtract, ALU.mult).then_inc(turn.norm_ready, 1)

            dve.wait_ge(s_w2, nW[1])
            for n in range(4):
                a = r_col[:, 0:1] if n == 0 else r_pow[:, n - 1:n]
                if n:
                    dve.wait_ge(s_rpow, n)
                nc.vector.tensor_tensor(r_pow[:, n:n + 1], a, a, ALU.mult).then_inc(s_rpow, 1)
            dve.wait_ge(v_set, 1)
            with dve.Fori(0, B // 2) as it:
                for k in range(4):
                    normalise(it * 4 + k, k, t2)
                for j in range(2):
                    dve.wait_ge(qkv_done, it * 4 + 2 * j + 2)
                    for u in range(2):
                        nc.vector.tensor_copy(v_ext[:, bass.ds((it * 2 + j) * H, H), u, 0:DH],
                                              bank[4 + j][:, u * C:(u + 1) * C].rearrange("p (g d) -> p g d", g=H)
                                              ).then_inc(v_taken, 1)
            dve.wait_ge(qk_taken, B + 1)
            nc.vector.tensor_scalar(rest[:, :, :], qk[:, 1], 1.0 / PI, MAGIC, ALU.mult, ALU.add).then_inc(red, 1)
            dve.wait_ge(red, 1)
            nc.vector.tensor_scalar(rest[:, :, :], rest[:, :, :], MAGIC, -PI, ALU.subtract, ALU.mult).then_inc(red, 1)
            dve.wait_ge(red, 2)
            nc.vector.tensor_tensor(qk[:, 0], qk[:, 1], rest[:, :, :], ALU.add).then_inc(red, 1)
            dve.wait_ge(red, 3)
            nc.vector.tensor_scalar(qk[:, 0], qk[:, 0], HALF_PI, -HALF_PI, ALU.min, ALU.max).then_inc(red, 1)
            dve.wait_ge(red, 4)
            dve.wait_ge(hi_done, 1)
            nc.vector.tensor_tensor(rest[:, :, :], qk[:, 0], piece[0][0][:, :, :], ALU.subtract).then_inc(sub_done, 1)
            dve.wait_ge(hi_done, 2)
            dve.wait_ge(sub_done, 1)
            nc.vector.tensor_tensor(qk[:, 0], qk[:, 1], piece[0][1][:, :, :], ALU.subtract).then_inc(sub_done, 1)
            dve.wait_ge(hi_done, 3)
            nc.vector.tensor_tensor(rest[:, :, :], rest[:, :, :], piece[1][0][:, :, :], ALU.subtract).then_inc(sub_done, 1)
            dve.wait_ge(hi_done, 4)
            dve.wait_ge(sub_done, 2)
            nc.vector.tensor_tensor(qk[:, 0], qk[:, 0], piece[1][1][:, :, :], ALU.subtract).then_inc(sub_done, 1)
            if STOP <= 3:
                dve.sem_inc(e_sum, 1)
                return
            def scale_and_divide(u, part):
                if part == 0:
                    dve.wait_ge(den8_done, u + 1)
                    wait(dve, num_scaled, u)
                    nc.vector.tensor_scalar(scale_f[:, :].bitcast(U32), den8[:, :].bitcast(U32), EXP_EVEN, EXP_FLIP,
                                            ALU.bitwise_and, ALU.bitwise_xor).then_inc(scale_done, 1)
                else:
                    dve.wait_ge(den_pair_done, u + 1)
                    wait(dve, ratio_ready, u)
                    nc.vector.reciprocal(rec_pair[:, :], den_pair[:, :]).then_inc(rec_done, 1)

            def dve_slot(q, k, early):
                u, par = q * 4 + k, k % 2
                for c in range(1, NCHUNK):
                    dve.wait_ge(sin_done, u * 3 + c)
                    dve.wait_ge(num_first, u + 1) if c == 1 else dve.wait_ge(num_used, u * 3 + (c - 1))
                    nc.vector.scalar_tensor_tensor(num[par], pair[(c - 1 + par) % 2][:, :], GUARD, num[par],
                                                   ALU.add, ALU.mult).then_inc(num_used, 1)
                    dve.wait_ge(mm_den, u * 3 + c)
                    dve.wait_ge(early_taken, u * 4 + 4) if c == 1 else dve.wait_ge(den_used, u * 3 + (c - 1))
                    nc.vector.scalar_tensor_tensor(den[par], pair[2][:, :], GUARD, den[par],
                                                   ALU.add, ALU.mult).then_inc(den_used, 1)
                    if c != 2 and not (early and k == 0):
                        scale_and_divide(u - 1, 0 if c == 1 else 1)

            for k in range(4):
                dve_slot(0, k, True)
            with dve.Fori(1, NUNIT // 4) as it:
                for k in range(4):
                    dve_slot(it, k, False)
            scale_and_divide(NUNIT - 1, 0)
            scale_and_divide(NUNIT - 1, 1)
            if STOP <= 4:
                dve.sem_inc(e_sum, 1)
                return
            dve.wait_ge(av_copied, NHEAD + 1)
            nc.vector.tensor_scalar(o_den[:, :, :], o_raw[:, :, :, DH], ATTN_EPS, None, ALU.add).then_inc(o_chain, 1)
            dve.wait_ge(o_chain, 1)
            nc.vector.reciprocal(o_rec[:, :, :], o_den[:, :, :]).then_inc(o_chain, 1)
            dve.wait_ge(o_chain, 2)
            dve.wait_ge(s_late, nW[2])
            with dve.Fori(0, B // 2) as it:
                for k in range(4):
                    j, u = k // 2, k % 2
                    n = it * 4 + k
                    hs = bass.ds((it * 2 + j) * H, H)
                    dve.wait_ge(t5.norm_used, n + 1)
                    nc.vector.tensor_tensor(norm[k][:, :].rearrange("p (g d) -> p g d", g=H), o_raw[:, hs, u, 0:DH],
                                            o_rec[:, hs, u].unsqueeze(2).to_broadcast([P, H, DH]), ALU.mult
                                            ).then_inc(t5.norm_ready, 1)
                for k in range(4):
                    n = it * 4 + k
                    hn = h[:, bass.ds(n, 1), :].rearrange("p a c -> p (a c)")
                    dve.wait_ge(proj_done, n + 1)
                    nc.vector.tensor_tensor(tmp[k][:, :], bank[2 + k][:, 0:C], b_proj_sb[:, :], ALU.add).then_inc(proj_taken, 1)
                    dve.wait_ge(proj_taken, n + 2)
                    nc.vector.tensor_tensor(hn, tmp[k][:, :], hn, ALU.add).then_inc(h_sum, 1)
                    dve.wait_ge(h_sum, n + 1)
                    nc.vector.bn_stats(stats[:, bass.ds(n, 1), :].rearrange("p a s -> p (a s)"), hn).then_inc(stats_done, 1)
            if STOP <= 5:
                dve.wait_ge(stats_done, 2 * NT)
                dve.sem_inc(e_sum, 1)
                return
            ln_math(dve, 1)
            with dve.Fori(0, B // 2) as it:
                for k in range(4):
                    normalise(it * 4 + k, k, t6)
            dve.wait_ge(t6.copied, B + 1)
            nc.vector.tensor_reduce(tok_sum[:, :], all_t.rearrange("p (b t) -> p b t", b=B), AX.X, ALU.add).then_inc(g_sum, 1)
            dve.wait_ge(g_mm, 1)
            nc.vector.scalar_tensor_tensor(lg0[:, :], bank[6][0:B, 0:E0], 1.0 / L, gate0_b_sb[:, :],
                                           ALU.mult, ALU.add).then_inc(g_chain, 1)
            dve.wait_ge(g_chain, 1)
            nc.vector.tensor_reduce(sm0[:, 0:1], lg0[:, :], AX.X, ALU.max).then_inc(g_chain, 1)
            dve.wait_ge(g_chain, 2)
            nc.vector.tensor_scalar(sm0[:, 1:2], sm0[:, 0:1], -1.0, None, ALU.mult).then_inc(g_chain, 1)
            dve.wait_ge(g_act, 1)
            nc.vector.max(top0[:, :], ex0[:, :]).then_inc(g_chain, 1)
            nc.vector.reciprocal(sm0[:, 3:4], sm0[:, 2:3]).then_inc(g_chain, 1)
            dve.wait_ge(g_chain, 5)
            nc.vector.max_index(idx0[:, :], top0[:, :], ex0[:, :]).then_inc(g_idx, 1)
            nc.vector.tensor_tensor(sm0[:, 4:5], top0[:, 0:1], sm0[:, 3:4], ALU.mult).then_inc(g_chain, 1)
            dve.wait_ge(g_chain, 6)
            nc.vector.tensor_scalar(gate_diag[:, :], ident[0:B, 0:B], sm0[:, 4:5], None, ALU.mult).then_inc(g_chain, 1)
            dve.wait_ge(g_mm, 2)
            nc.vector.tensor_copy(gate_col[:, :], bank[6][:, 32:32 + B]).then_inc(g_chain, 1)
            dve.wait_ge(g_chain, 8)
            dve.sem_inc(y_sum, 3)
            with dve.Fori(0, B // 2) as it:
                for k in range(4):
                    j = k // 2
                    n = it * 4 + k
                    hn = h[:, bass.ds(n, 1), :].rearrange("p a c -> p (a c)")
                    dve.wait_ge(g_in[j], it * 32 + 32)
                    dve.wait_ge(y_done, n + 1)
                    nc.vector.tensor_tensor(tmp[k][:, :], bank[2 + k][:, 0:C], b_sel[j][:, :], ALU.add).then_inc(y_taken, 1)
                    dve.wait_ge(y_taken, n + 2)
                    nc.vector.scalar_tensor_tensor(hn, tmp[k][:, :], gate_col[:, bass.ds(it * 2 + j, 1)], hn,
                                                   ALU.mult, ALU.add).then_inc(y_sum, 1)
                    dve.wait_ge(y_sum, n + 4)
                    nc.vector.bn_stats(stats[:, bass.ds(n, 1), :].rearrange("p a s -> p (a s)"), hn).then_inc(stats_done, 1)
            if STOP <= 6:
                dve.wait_ge(stats_done, 3 * NT)
                dve.sem_inc(e_sum, 1)
                return
            ln_math(dve, 2)
            with dve.Fori(0, B) as b:
                for u in range(2):
                    hn = h[:, bass.ds(b * 2 + u, 1), :].rearrange("p a c -> p (a c)")
                    normalise(b * 2 + u, u, t7)
                    dve.wait_ge(t7.norm_ready, b * 2 + (u + 1))
                    nc.vector.tensor_tensor(hn, hn, norm[u][:, :], ALU.add).then_inc(h_add, 1)
                dve.wait_ge(p_done, b * 6 + 2)
                nc.vector.tensor_scalar(q1[:, 2:4, :], bank[2][:, :].rearrange("p (a t) -> p a t", a=2),
                                        float(D1) ** -0.5, None, ALU.mult).then_inc(p_dve, 1)
                dve.wait_ge(p_done, b * 6 + 4)
                nc.vector.tensor_copy(k1[:, 2:4, :], bank[1][:, :].rearrange("p (a t) -> p a t", a=2)).then_inc(p_dve, 1)
                dve.wait_ge(p_done, b * 6 + 6)
                nc.vector.tensor_copy(v1[:, 1, :], bank[3][:, :]).then_inc(p_dve, 1)

                def maxima(m):
                    dve.wait_ge(s_done, b * 16 + (m + 1))
                    nc.vector.tensor_reduce(neg_max[:, m:m + 1], bank[4 + m % 2][:, 0:L], AX.X, ALU.max,
                                            negate=True).then_inc(s_max, 1)

                def copy_pt(m):
                    dve.wait_ge(pt_done, b * 16 + (m + 3))
                    dve.wait_ge(pv_done, b * 16 + (m + 1))
                    nc.vector.tensor_copy(prob_t[m % 2][:, :, :],
                                          bank[6 - 3 * (m % 2)][:, 0:L].rearrange("p (a t) -> p a t", a=2)
                                          ).then_inc(pt_copied, 1)

                def norm_o(u):
                    o_ps = bank[7] if u == 0 else bank[0]
                    dve.wait_ge(s_exp, b * 16 + (8 * (u + 1) + 1))
                    nc.vector.reciprocal(row_rec[:, 8 * u:8 * u + 8], row_sum[:, 8 * u:8 * u + 8]).then_inc(rr, 1)
                    dve.wait_ge(rr, b * 2 + (u + 1))
                    dve.wait_ge(pv_done, b * 16 + (8 * (u + 1) + 2))
                    dve.wait_ge(ot_done, b * 2 + (u + 1))
                    nc.vector.tensor_tensor(o1.rearrange("p (g d) -> p g d", g=H1),
                                            o_ps[:, :].rearrange("p (g d) -> p g d", g=H1),
                                            row_rec[:, 8 * u:8 * u + 8].unsqueeze(2).to_broadcast([P, H1, D1]),
                                            ALU.mult).then_inc(o_norm, 1)

                def add_wo(u):
                    hn = h[:, bass.ds(b * 2 + u, 1), :].rearrange("p a c -> p (a c)")
                    dve.wait_ge(wo_done, b * 2 + (u + 1))
                    dve.wait_ge(h_add, b * 2 + (u + 1))
                    nc.vector.tensor_tensor(hn, bank[2][:, 0:C], hn, ALU.add).then_inc(wo_sum, 1)
                    dve.wait_ge(wo_sum, b * 2 + (u + 2))
                    nc.vector.bn_stats(stats[:, bass.ds(b * 2 + u, 1), :].rearrange("p a s -> p (a s)"), hn).then_inc(stats_done, 1)

                maxima(0)
                for m in range(16):
                    if m + 1 < 16:
                        maxima(m + 1)
                    copy_pt(m)
                    if m == 9:
                        norm_o(0)
                    if m == 13:
                        add_wo(0)
                norm_o(1)
                add_wo(1)
            if STOP <= 7:
                dve.wait_ge(stats_done, 4 * NT)
                dve.sem_inc(e_sum, 1)
                return
            ln_math(dve, 3)
            LG, A, M1, C1, M2, C2, WT, W2 = (route[:, i] for i in range(8))
            with dve.Fori(0, B // 2) as it:
                for k in range(4):
                    normalise(it * 4 + k, k, t8)
                for k in range(4):
                    dve.wait_ge(l_done, it * 4 + (k + 1))
                    nc.vector.tensor_tensor(LG[:, bass.ds(it * 4 + k, 1), :].rearrange("p a e -> p (a e)"),
                                            bank[2 + k][:, 0:E1], gate1_b_sb[:, :], ALU.add).then_inc(l_taken, 1)
            cnt = [0]

            def step(ins):
                cnt[0] += 1
                ins.then_inc(r_chain, 1)
                dve.wait_ge(r_chain, cnt[0])

            def wide(a):
                return a.unsqueeze(2).to_broadcast([P, NT, E1])
            dve.wait_ge(l_taken, NT + 1)
            dve.wait_ge(r_iota, 1)
            best, second, first_at, second_at = (rsm[:, i, :] for i in (0, 1, 4, 5))
            step(nc.vector.tensor_reduce(best, LG, AX.X, ALU.max))
            step(nc.vector.tensor_tensor(A, LG, wide(best), ALU.is_lt))
            step(nc.vector.scalar_tensor_tensor(C1, A, float(E1), iota[:, :, :], ALU.mult, ALU.add))
            step(nc.vector.tensor_reduce(first_at, C1, AX.X, ALU.min))
            step(nc.vector.tensor_tensor(M1, iota[:, :, :], wide(first_at), ALU.is_equal))
            step(nc.vector.scalar_tensor_tensor(C1, M1, -3e38, LG, ALU.mult, ALU.add))
            step(nc.vector.tensor_reduce(second, C1, AX.X, ALU.max))
            step(nc.vector.tensor_tensor(A, C1, wide(second), ALU.is_lt))
            step(nc.vector.scalar_tensor_tensor(C2, A, float(E1), iota[:, :, :], ALU.mult, ALU.add))
            step(nc.vector.tensor_tensor(rsm[:, 2, :], second, best, ALU.subtract))
            step(nc.vector.tensor_reduce(second_at, C2, AX.X, ALU.min))
            step(nc.vector.tensor_tensor(M2, iota[:, :, :], wide(second_at), ALU.is_equal))
            dve.wait_ge(r_exp, 1)
            step(nc.vector.tensor_scalar(rsm[:, 6, :], rsm[:, 3, :], 1.0, None, ALU.add))
            step(nc.vector.reciprocal(rsm[:, 7, :], rsm[:, 6, :]))
            step(nc.vector.tensor_tensor(rsm[:, 8, :], rsm[:, 3, :], rsm[:, 7, :], ALU.mult))
            step(nc.vector.tensor_tensor(WT, M1, wide(rsm[:, 7, :]), ALU.mult))
            step(nc.vector.tensor_tensor(W2, M2, wide(rsm[:, 8, :]), ALU.mult))
            step(nc.vector.tensor_tensor(WT, WT, W2, ALU.add))
            dve.wait_ge(wp_zero, 1)
            with dve.Fori(0, NG) as g:
                dve.wait_ge(wp_turned, g + 1)
                nc.vector.tensor_copy(w_pad[:, :, 0:E1], WT[:, bass.ds(g * 4, 4), :]).then_inc(wp_ready, 1)
                dve.wait_ge(wp_turned, g + 2)
                dve.wait_ge(b2_done, g * 4 + 1)
                nc.vector.tensor_copy(w_pad_t[:, :], bank[6][:, 0:P]).then_inc(wp_copied, 1)
                hg = h[:, bass.ds(g * 4, 4), :]
                dve.wait_ge(b2_done, g * 4 + 5)
                nc.vector.tensor_tensor(hg, bank[7][:, :].rearrange("p (a c) -> p a c", a=4), hg, ALU.add).then_inc(h_add, 1)
                dve.wait_ge(h_add, g + (NT + 1))
                for e in range(E1):
                    dve.wait_ge(e_done, g * 8 + (e + 3))
                    if e:
                        dve.wait_ge(y_taken, g * 32 + (NT + 4 * e + 1))
                    for t in range(4):
                        hn = h[:, bass.ds(g * 4 + t, 1), :].rearrange("p a c -> p (a c)")
                        nc.vector.scalar_tensor_tensor(hn, bank[2 + e % 2][:, t * C:(t + 1) * C],
                                                       WT[:, bass.ds(g * 4 + t, 1), e], hn,
                                                       ALU.mult, ALU.add).then_inc(y_taken, 1)
            dve.wait_ge(y_taken, NT + NG * 32 + 1)
            dve.sem_inc(e_sum, 1)

        @block.tensor
        def _(pe):
            pe.wait_ge(s_w, nW[0])
            pe.sem_inc(x_free, 2)
            with pe.Fori(0, B // 2) as it:
                for j in range(2):
                    pe.wait_ge(x_in[j], it * 32 + 32)
                    for u in range(2):
                        k = 2 * j + u
                        pe.wait_ge(conv_taken, it * 4 + (k + 1))
                        for t in range(5):
                            rows = P if t < 4 else CIN
                            mm = nc.tensor.matmul(bank[k][:, 0:C], xs[j][0:rows, u * P + 2 * t:u * P + 2 * t + P],
                                                  conv_w_sb[0:rows, t, :], start=(t == 0), stop=(t == 4))
                        mm.then_inc(conv_done, 1)
                        if u == 1:
                            pe.wait_ge(conv_done, it * 4 + (k + 1))
                            pe.sem_inc(x_free, 1)
            if STOP <= 1:
                return

            def turn(tile0, j, ks, t, dst=None):
                for u in range(2):
                    pe.wait_ge(t.norm_ready, tile0 + (u + 1))
                    nc.tensor.transpose(bank[j][:, u * P:(u + 1) * P], norm[ks + u][:, :], ident[:, :]).then_inc(t.turned, 1)

            pe.wait_ge(s_w2, nW[1])
            pe.sem_inc(t2.norm_used, 4)
            pe.sem_inc(t2.t_used, 2)
            with pe.Fori(0, B // 2) as it:
                for j in range(2):
                    pe.wait_ge(t2.copied, it * 2 + 1)
                    turn(it * 4 + 2 * j, j, 2 * j, t2)
                pe.wait_ge(t2.turned, it * 4 + 4)
                pe.sem_inc(t2.norm_used, 4)
                for j in range(2):
                    pe.wait_ge(t2.copied, it * 2 + (j + 2))
                    pe.wait_ge(qk_taken, it * 2 + 1)
                    pe.wait_ge(v_taken, it * 4 + 1)
                    for s in range(2):
                        mm = nc.tensor.matmul(bank[2 + j][:, s * L:(s + 1) * L], w_qk_sb[:, s * C:(s + 1) * C],
                                              norm_t[j][:, :], start=True, stop=True)
                    mm.then_inc(qkv_done, 1)
                    for u in range(2):
                        mm = nc.tensor.matmul(bank[4 + j][:, u * C:(u + 1) * C], norm_t[j][:, u * P:(u + 1) * P],
                                              w_v_sb[:, :], start=True, stop=True)
                    mm.then_inc(qkv_done, 1)
                    pe.wait_ge(qkv_done, it * 4 + 2 * j + 2)
                    pe.sem_inc(t2.t_used, 1)
            if STOP <= 3:
                return
            pe.wait_ge(qk_taken, B + 1)
            pe.wait_ge(v_taken, NT + 1)
            pe.wait_ge(op_one, 2)
            pe.wait_ge(op_mask, 64)
            pe.sem_inc(av_done, 1)

            def products(a, j, par, s, c):
                for t in range(2):
                    col = c * CHUNK + t * 512
                    mm = nc.tensor.matmul(pair[a][:, t * 512:(t + 1) * 512], k_op[j][0:ROWS, s, par * P:(par + 1) * P],
                                          q_op[j][0:ROWS, s, col:col + 512], start=True, stop=True)
                return mm

            def attend(i, j, t):
                if t == 0:
                    pe.wait_ge(w4_ready, i * 2 + 2)
                    pe.wait_ge(av_copied, i + 1)
                for kt in range(2):
                    mm = nc.tensor.matmul(bank[ATTEND][:, t * (DH + 1):(t + 1) * (DH + 1)],
                                          weight4[j][:, kt, t * P:(t + 1) * P],
                                          v_ext[:, bass.ds(i, 1), kt, :].rearrange("p a d -> p (a d)"),
                                          start=(kt == 0), stop=(kt == 1))
                if t == 1:
                    mm.then_inc(av_done, 1)

            def early(u, j, par, n):
                wait(pe, early_taken, u * 4 + n)
                nc.tensor.matmul(bank[EARLY], k_op[j][0:ROWS, n // 2, par * P:(par + 1) * P],
                                 q_op[j][0:ROWS, n // 2, (n % 2) * HALF:(n % 2 + 1) * HALF],
                                 start=True, stop=True).then_inc(mm_early, 1)

            def pe_slot(q, k, first, last):
                u, i, j, par = q * 4 + k, q * 2 + k // 2, k // 2, k % 2
                next_j, has_next = (k + 1) // 2 % 2, not (last and k == 3)
                wait(pe, num_used, u * 3 - 1)
                products((0 + par) % 2, j, par, 0, 1).then_inc(mm_num, 1)
                early(u, j, par, 3)
                wait(pe, den_used, u * 3)
                products(2, j, par, 1, 1).then_inc(mm_den, 1)
                if has_next:
                    if par == 1:
                        pe.wait_ge(op_in[next_j], (q + 1 - next_j) * 32 + 32)
                    early(u + 1, next_j, 1 - par, 0)
                wait(pe, num_used, u * 3)
                products((1 + par) % 2, j, par, 0, 2).then_inc(mm_num, 1)
                if has_next:
                    early(u + 1, next_j, 1 - par, 1)
                wait(pe, num_used, u * 3 + 1)
                products((2 + par) % 2, j, par, 0, 3).then_inc(mm_num, 1)
                wait(pe, den_used, u * 3 + 1)
                products(2, j, par, 1, 2).then_inc(mm_den, 1)
                if not first:
                    attend(i - 2, j, par)
                if has_next:
                    early(u + 1, next_j, 1 - par, 2)
                wait(pe, den_used, u * 3 + 2)
                products(2, j, par, 1, 3).then_inc(mm_den, 1)

            pe.wait_ge(op_in[0], 32)
            for n in range(3):
                early(0, 0, 0, n)
            for k in range(4):
                pe_slot(0, k, True, False)
            with pe.Fori(1, NUNIT // 4 - 1) as it:
                for k in range(4):
                    pe_slot(it, k, False, False)
            for k in range(4):
                pe_slot(NUNIT // 4 - 1, k, False, True)
            for j in range(2):
                for t in range(2):
                    attend(NHEAD - 2 + j, j, t)
            if STOP <= 4:
                return
            pe.sem_inc(t5.norm_used, 4)
            pe.sem_inc(t5.t_used, 2)
            pe.wait_ge(s_late, nW[2])
            with pe.Fori(0, B // 2) as it:
                for j in range(2):
                    pe.wait_ge(t5.copied, it * 2 + 1)
                    turn(it * 4 + 2 * j, j, 2 * j, t5)
                pe.wait_ge(t5.turned, it * 4 + 4)
                pe.sem_inc(t5.norm_used, 4)
                for j in range(2):
                    pe.wait_ge(t5.copied, it * 2 + (j + 2))
                    for u in range(2):
                        pe.wait_ge(proj_taken, it * 4 + 1)
                        nc.tensor.matmul(bank[2 + 2 * j + u][:, 0:C], norm_t[j][:, u * P:(u + 1) * P],
                                         w_proj_sb[:, :], start=True, stop=True).then_inc(proj_done, 1)
                    pe.wait_ge(proj_done, it * 4 + 2 * j + 2)
                    pe.sem_inc(t5.t_used, 1)
            if STOP <= 5:
                return
            pe.sem_inc(t6.norm_used, 4)
            with pe.Fori(0, B // 2) as it:
                for j in range(2):
                    pe.wait_ge(t6.copied, it * 2 + 1)
                    turn(it * 4 + 2 * j, j, 2 * j, t6)
                pe.wait_ge(t6.turned, it * 4 + 4)
                pe.sem_inc(t6.norm_used, 4)
            pe.wait_ge(g_sum, 1)
            nc.tensor.matmul(bank[6][0:B, 0:E0], tok_sum[:, :], gate0_w_sb[:, :], start=True, stop=True).then_inc(g_mm, 1)
            pe.wait_ge(g_chain, 7)
            pe.wait_ge(s_ones, 1)
            nc.tensor.matmul(bank[6][:, 32:32 + B], ones[0:B, :], gate_diag[:, :], start=True, stop=True).then_inc(g_mm, 1)
            pe.sem_inc(t6.t_used, 2)
            with pe.Fori(0, B // 2) as it:
                for j in range(2):
                    pe.wait_ge(g_copied, it * 2 + (j + 1))
                    pe.wait_ge(g_in[j], it * 32 + 32)
                    pe.wait_ge(y_taken, it * 4 + 1)
                    for u in range(2):
                        nc.tensor.matmul(bank[2 + 2 * j + u][:, 0:C], norm_t[j][:, u * P:(u + 1) * P],
                                         w_sel[j][:, :], start=True, stop=True).then_inc(y_done, 1)
                    pe.wait_ge(y_done, it * 4 + 2 * j + 2)
                    pe.sem_inc(t6.t_used, 1)
            if STOP <= 6:
                return
            pe.wait_ge(y_taken, NT + 1)
            pe.sem_inc(t7.norm_used, 2)
            pe.sem_inc(pt_done, 2)
            pe.sem_inc(pv_done, 2)
            pe.sem_inc(ot_done, 1)
            with pe.Fori(0, B) as b:
                pe.wait_ge(o_norm, b * 2 + 1)
                turn(b * 2, 0, 0, t7)
                pe.wait_ge(t7.turned, b * 2 + 2)
                pe.wait_ge(h_add, b * 2 + 2)
                pe.sem_inc(t7.norm_used, 2)
                pe.wait_ge(t7.copied, b + 1)
                pe.wait_ge(wo_sum, b * 2 + 1)
                for n, w in enumerate((wq1_sb, wq1_sb, wk1_sb, wk1_sb)):
                    if n == 3:
                        pe.wait_ge(p_act, b * 3 + 1)
                    for a in range(2):
                        g = 2 * (n % 2) + a
                        mm = nc.tensor.matmul(bank[1 + n % 3][:, a * L:(a + 1) * L], w[:, g * P:(g + 1) * P],
                                              norm_t[0][:, :], start=True, stop=True)
                    mm.then_inc(p_done, 1)
                for u in range(2):
                    pe.wait_ge(p_dve, b * 3 + 1) if u == 0 else pe.wait_ge(p_act, b * 3 + 2)
                    nc.tensor.matmul(bank[2 + u][:, :], norm_t[0][:, u * P:(u + 1) * P], wv1_sb[:, :],
                                     start=True, stop=True).then_inc(p_done, 1)
                pe.wait_ge(p_dve, b * 3 + 3)
                pe.wait_ge(p_act, b * 3 + 3)

                def logits(m):
                    u, g = m // 8, m % 8
                    r = D1 * (g % 2)
                    pe.wait_ge(s_exp, b * 16 + m) if m else None
                    nc.tensor.matmul(bank[4 + m % 2][:, 0:L], q1[r:r + D1, g // 2, u * P:(u + 1) * P],
                                     k1[r:r + D1, g // 2, :], start=True, stop=True).then_inc(s_done, 1)

                def turn_prob(m):
                    pe.wait_ge(s_exp, b * 16 + (m + 2))
                    pe.wait_ge(pt_copied, b * 16 + m) if m else None
                    for a in range(2):
                        mm = nc.tensor.transpose(bank[6 - 3 * (m % 2)][:, a * P:(a + 1) * P],
                                                 prob[m % 2][:, a * P:(a + 1) * P], ident[:, :])
                    mm.then_inc(pt_done, 1)

                def values(m):
                    u, g = m // 8, m % 8
                    o_ps = bank[7] if u == 0 else bank[0]
                    pe.wait_ge(pt_copied, b * 16 + (m + 2))
                    if m == 0:
                        pe.wait_ge(o_norm, b * 2 + 1)
                    for a in range(2):
                        mm = nc.tensor.matmul(o_ps[:, g * D1:(g + 1) * D1], prob_t[m % 2][:, a, :],
                                              v1[:, a, g * D1:(g + 1) * D1], start=(a == 0), stop=(a == 1))
                    mm.then_inc(pv_done, 1)

                def project(u):
                    pe.wait_ge(o_norm, b * 2 + (u + 2))
                    for a in range(4):
                        mm = nc.tensor.transpose(bank[1][:, a * P:(a + 1) * P], o1[:, a * P:(a + 1) * P], ident[:, :])
                    mm.then_inc(ot_done, 1)
                    pe.wait_ge(ot_copied, b * 2 + (u + 1))
                    pe.wait_ge(wo_sum, b * 2 + (u + 1))
                    for a in range(4):
                        mm = nc.tensor.matmul(bank[2][:, 0:C], o1_t[:, a, :], wo1_sb[:, a, :], start=(a == 0), stop=(a == 3))
                    mm.then_inc(wo_done, 1)

                logits(0)
                for m in range(16):
                    if m + 1 < 16:
                        logits(m + 1)
                    turn_prob(m)
                    if m:
                        values(m - 1)
                    if m == 11:
                        project(0)
                values(15)
                project(1)
            if STOP <= 7:
                return
            pe.sem_inc(t8.norm_used, 4)
            pe.sem_inc(t8.t_used, 2)
            with pe.Fori(0, B // 2) as it:
                for j in range(2):
                    pe.wait_ge(t8.copied, it * 4 + 1)
                    turn(it * 4 + 2 * j, j, 2 * j, t8)
                pe.wait_ge(t8.turned, it * 4 + 4)
                pe.sem_inc(t8.norm_used, 4)
                for j in range(2):
                    pe.wait_ge(t8.copied, it * 4 + (2 * (j + 1) + 1))
                    pe.wait_ge(l_taken, it * 4 + 1)
                    for u in range(2):
                        nc.tensor.matmul(bank[2 + 2 * j + u][:, 0:E1], norm_t[j][:, u * P:(u + 1) * P],
                                         gate1_w_sb[:, :], start=True, stop=True).then_inc(l_done, 1)
                    pe.wait_ge(l_done, it * 4 + 2 * j + 2)
                    pe.sem_inc(t8.t_used, 1)
            pe.wait_ge(l_taken, NT + 1)
            pe.sem_inc(e_done, 2)
            pe.sem_inc(wp_turned, 1)
            pe.sem_inc(b2_done, 1)
            with pe.Fori(0, NG) as g:
                pe.wait_ge(wp_ready, g + 1)
                nc.tensor.transpose(bank[6][:, 0:P], w_pad[:, :, :].rearrange("p a e -> p (a e)"), ident[:, :]).then_inc(wp_turned, 1)
                pe.wait_ge(wp_copied, g + 1)
                pe.wait_ge(h_add, g + NT)
                for t in range(4):
                    if t:
                        pe.wait_ge(b2_done, g * 4 + (t + 1))
                    nc.tensor.matmul(bank[7][:, t * C:(t + 1) * C], w_pad_t[32 * t:32 * t + E1, :],
                                     b2_sb[32 * t:32 * t + E1, :], start=True, stop=True).then_inc(b2_done, 1)

                def hidden(e):
                    for f in range(2):
                        n = 2 * e + f
                        pe.wait_ge(hid_ready, g * 16 + n) if n else None
                        nc.tensor.matmul(bank[n % 2][:, :], w1_sb[:, e, f * P:(f + 1) * P],
                                         all_t[:, bass.ds(g * 512, 512)], start=True, stop=True).then_inc(h_done, 1)

                def second(e):
                    pe.wait_ge(hid_ready, g * 16 + (2 * e + 3))
                    pe.wait_ge(y_taken, g * 32 + (NT + 4 * (e - 1) + 1))
                    for t in range(4):
                        for f in range(2):
                            mm = nc.tensor.matmul(bank[2 + e % 2][:, t * C:(t + 1) * C],
                                                  hid[(2 * e + f) % 4][:, t * P:(t + 1) * P], w2_sb[:, 2 * e + f, :],
                                                  start=(f == 0), stop=(f == 1))
                    mm.then_inc(e_done, 1)

                hidden(0)
                for e in range(E1):
                    if e + 1 < E1:
                        hidden(e + 1)
                    second(e)


_ORDER = ["x", "conv_w", "conv_b", "w_qk", "w_v", "w_proj", "b_proj", "param_r", "gate0_w", "gate0_b", "exp0_w",
          "exp0_b", "wq1", "wk1", "wv1", "wo1", "gate1_w", "gate1_b", "w1", "b1", "w2", "b2", "neg_mask", "ident_in"]


def kernel(x, L0_tok_weight, L0_tok_bias, L0_attn_w_qkv, L0_attn_w_proj, L0_attn_b_proj, L0_attn_paramR, L0_ffn_Wg,
           L0_ffn_bg, L0_ffn_We, L0_ffn_be, L1_attn_Wq, L1_attn_Wk, L1_attn_Wv, L1_attn_Wo, L1_ffn_gate_w,
           L1_ffn_gate_b, L1_ffn_w1, L1_ffn_b1, L1_ffn_w2, L1_ffn_b2):
    import ml_dtypes
    import concourse.bacc as bacc
    from concourse.bass_utils import run_bass_kernel_spmd

    qkv_t = np.asarray(L0_attn_w_qkv).T
    mask = np.zeros((NPIECE, DH, DH, L), ml_dtypes.bfloat16)
    for d in range(DH):
        mask[:, d, d, :] = -1
    data = dict(
        x=x, conv_w=np.transpose(L0_tok_weight, (2, 1, 0)), conv_b=L0_tok_bias, w_qk=qkv_t[:, 0:2 * C],
        w_v=qkv_t[:, 2 * C:3 * C], w_proj=np.transpose(L0_attn_w_proj), b_proj=L0_attn_b_proj,
        param_r=L0_attn_paramR, gate0_w=L0_ffn_Wg, gate0_b=L0_ffn_bg, exp0_w=L0_ffn_We, exp0_b=L0_ffn_be,
        wq1=np.transpose(L1_attn_Wq), wk1=np.transpose(L1_attn_Wk), wv1=np.transpose(L1_attn_Wv),
        wo1=np.transpose(L1_attn_Wo), gate1_w=L1_ffn_gate_w, gate1_b=L1_ffn_gate_b, w1=L1_ffn_w1, b1=L1_ffn_b1,
        w2=L1_ffn_w2, b2=L1_ffn_b2, neg_mask=mask.reshape(KROWS, DH * L), ident_in=np.eye(P, dtype=np.float32))
    nc = bacc.Bacc("TRN2", target_bir_lowering=False, num_devices=1)
    arrays, args = {}, []
    for name in _ORDER:
        a = np.ascontiguousarray(data[name])
        arrays[f"in_{name}"] = a
        args.append(nc.dram_tensor(f"in_{name}", a.shape, mybir.dt.from_np(a.dtype), kind="ExternalInput").ap())
    args.append(nc.dram_tensor("out_0", (B, L, C), F32, kind="ExternalOutput").ap())
    build(nc, *args)
    r = run_bass_kernel_spmd(nc, [arrays], core_ids=[0])
    return r.results[0]["out_0"]
```

```python
from contextlib import ExitStack

import numpy as np
import concourse.bass as bass
from concourse import mybir

ALU = mybir.AluOpType
ACT = mybir.ActivationFunctionType
AX = mybir.AxisListType
F32 = mybir.dt.float32
BF16 = mybir.dt.bfloat16
U32 = mybir.dt.uint32


P = 128
B, CIN, L = 8, 64, 256
C, TAPS, PAD = 128, 9, 4
NT = B * L // P
H, DH = 8, 16
NHEAD = B * H
NPIECE = 3
KROWS = NPIECE * DH
QROW = 64
ROWS = QROW + NPIECE
LANES = 4
CHUNK = LANES * L
HALF = CHUNK // 2
EARLY, ATTEND = 7, 6
NCHUNK = DH // LANES
NUNIT = 2 * NHEAD
GUARD = 1e-7
LANE_SCALE = 2.0 ** 31
EXP_EVEN = 0x7F000000
EXP_FLIP = 0x7F800000
ATTN_EPS = 1e-6
LN_EPS = 1e-5
MAGIC = 1.5 * 2.0 ** 23
PI = float(np.float32(np.pi))
HALF_PI = float(np.nextafter(np.float32(np.pi / 2), np.float32(0)))
E0 = 16
H1, D1 = 8, 64
INNER = H1 * D1
E1, F1 = 8, 256
NG = 4


def build(nc, x, conv_w, conv_b, w_qk, w_v, w_proj, b_proj, param_r, gate0_w, gate0_b, exp0_w, exp0_b,
          wq1, wk1, wv1, wo1, gate1_w, gate1_b, w1, b1, w2, b2, neg_mask, ident_in, out):
    with ExitStack() as ctx:
        def sb(name, shape, dt=F32):
            return ctx.enter_context(nc.sbuf_tensor(name, shape, dt))

        def sem(name):
            return ctx.enter_context(nc.semaphore(name))

        pair = [ctx.enter_context(nc.psum_tensor(f"pair{i}", [P, 1024], F32)) for i in range(4)]
        bank = [pair[i // 2][:, (i % 2) * 512:(i % 2 + 1) * 512] for i in range(8)]

        q_dram = nc.dram_tensor("q_pieces", [NPIECE, 2, NHEAD, DH * L], BF16, kind="Internal").ap()
        k_dram = nc.dram_tensor("k_pieces", [NPIECE, NHEAD, DH, 2, L], BF16, kind="Internal").ap()

        ident = sb("ident", [P, P])
        ones = sb("ones", [P, P])
        conv_w_sb = sb("conv_w_sb", [P, 5, C])
        conv_b_sb = sb("conv_b_sb", [P, C])
        w_qk_sb = sb("w_qk_sb", [P, 2 * C])
        w_v_sb = sb("w_v_sb", [P, C])
        w_proj_sb = sb("w_proj_sb", [P, C])
        b_proj_sb = sb("b_proj_sb", [P, C])
        gate0_w_sb = sb("gate0_w_sb", [P, E0])
        gate0_b_sb = sb("gate0_b_sb", [B, E0])
        wq1_sb = sb("wq1_sb", [P, INNER])
        wk1_sb = sb("wk1_sb", [P, INNER])
        wv1_sb = sb("wv1_sb", [P, INNER])
        wo1_sb = sb("wo1_sb", [P, INNER // P, C])
        gate1_w_sb = sb("gate1_w_sb", [P, E1])
        gate1_b_sb = sb("gate1_b_sb", [P, E1])
        w1_sb = sb("w1_sb", [P, E1, F1])
        b1_sb = sb("b1_sb", [P, 2 * E1])
        w2_sb = sb("w2_sb", [P, 2 * E1, C])
        b2_sb = sb("b2_sb", [P, C])
        r_col = sb("r_col", [P, 1])
        r_pow = sb("r_pow", [P, 4])

        h = sb("h", [P, NT, C])
        stats = sb("stats", [P, NT, 6])
        ln = sb("ln", [P, 10, NT])
        mean, rstd = ln[:, 0, :], ln[:, 1, :]
        norm = [sb(f"norm{i}", [P, C]) for i in range(4)]
        norm_t = [sb(f"norm_t{i}", [P, L]) for i in range(2)]

        xs = [sb(f"xs{i}", [P, L + 2 * PAD]) for i in range(2)]
        v_ext = sb("v_ext", [P, NHEAD, 2, DH + 1])
        o_raw = sb("o_raw", [P, NHEAD, 2, DH + 1])
        o_rec = sb("o_rec", [P, NHEAD, 2])
        o_den = sb("o_den", [P, NHEAD, 2])

        qk = sb("qk", [P, 2, 2, B * L])
        rest = sb("rest", [P, 2, B * L])
        piece = [[sb(f"piece{p}_{s}", [P, 2, B * L], BF16) for s in range(2)] for p in range(2)]

        k_op = [sb(f"k_op{i}", [P, 2, L], BF16) for i in range(2)]
        q_op = [sb(f"q_op{i}", [P, 2, DH * L], BF16) for i in range(2)]
        num = [rest[:, 0, i * CHUNK:(i + 1) * CHUNK] for i in range(2)]
        den = [rest[:, 1, i * CHUNK:(i + 1) * CHUNK] for i in range(2)]
        first_sin = qk[:, 0, 0, 0:CHUNK]
        guard_col = sb("guard_col", [P, 1])
        num8 = qk[:, 0, 1, 0:2 * L]
        den8 = qk[:, 0, 1, 2 * L:4 * L]
        scale_f = sb("scale_f", [P, 2 * L])
        num_f = sb("num_f", [P, L])
        den_f = sb("den_f", [P, L])
        num_x = qk[:, 0, 0, CHUNK:CHUNK + L].rearrange("p (a t) -> p a t", a=2)
        den_pair = sb("den_pair", [P, P])
        rec_pair = sb("rec_pair", [P, P])
        ratio = [sb(f"ratio{i}", [P, L]) for i in range(2)]
        score2 = sb("score2", [P, L])
        weight4 = [sb(f"weight4_{i}", [P, 2, L]) for i in range(2)]

        all_t = qk[:, 0, 0, :]
        tok_sum = sb("tok_sum", [P, B])
        lg0 = sb("lg0", [B, E0])
        ex0 = sb("ex0", [B, E0])
        top0 = sb("top0", [B, 8])
        idx0 = sb("idx0", [B, 8], U32)
        idx_row = sb("idx_row", [1, B], U32)
        sm0 = sb("sm0", [B, 8])
        gate_diag = sb("gate_diag", [B, B])
        gate_col = sb("gate_col", [P, B])
        w_sel = [rest[:, 0, i * C:(i + 1) * C] for i in range(4)]
        b_sel = [rest[:, 1, i * C:(i + 1) * C] for i in range(4)]
        tmp = [sb(f"tmp{i}", [P, C]) for i in range(4)]

        q1 = [t.rearrange("p (a t) -> p a t", a=4) for t in (rest[:, 0, 0:4 * L], piece[0][0][:, 0, :].bitcast(F32))]
        k1 = [t.rearrange("p (a t) -> p a t", a=4) for t in (rest[:, 0, 4 * L:8 * L], piece[0][0][:, 1, :].bitcast(F32))]
        v1 = [t.rearrange("p (a t) -> p a t", a=2) for t in (rest[:, 1, 0:2 * INNER], piece[0][1][:, 0, :].bitcast(F32))]
        neg_max = sb("neg_max", [P, 16])
        row_sum = sb("row_sum", [P, 16])
        row_rec = sb("row_rec", [P, 16])
        prob = [sb(f"prob{i}", [P, L]) for i in range(2)]
        prob_t = [sb(f"prob_t{i}", [P, 2, P]) for i in range(2)]
        o1 = rest[:, 1, 2 * INNER:3 * INNER]
        o1_t = rest[:, 1, 3 * INNER:4 * INNER].rearrange("p (a t) -> p a t", a=4)

        route = qk[:, 1, 1, 0:8 * NT * E1].rearrange("p (i t e) -> p i t e", i=8, t=NT)
        iota = sb("iota", [P, NT, E1])
        rsm = sb("rsm", [P, 10, NT])
        w_pad = sb("w_pad", [P, 4, 32])
        w_pad_t = sb("w_pad_t", [P, P])
        hid = [qk[:, 1, 0, i * 4 * P:(i + 1) * 4 * P] for i in range(4)]

        s_ident = sem("s_ident"); s_ones = sem("s_ones")
        s_w = sem("s_w"); s_w2 = sem("s_w2"); s_r = sem("s_r"); s_rpow = sem("s_rpow")
        s_late = sem("s_late")
        x_clear = sem("x_clear"); x_free = sem("x_free"); x_in = [sem(f"x_in{i}") for i in range(2)]
        conv_done = sem("conv_done"); conv_taken = sem("conv_taken")
        stats_done = sem("stats_done"); ln_chain = sem("ln_chain"); ln_var = sem("ln_var"); ln_std = sem("ln_std")
        v_set = sem("v_set")

        LNC = [0]

        def ln_math(dve, nth):
            def step(ins):
                LNC[0] += 1
                ins.then_inc(ln_chain, 1)
                dve.wait_ge(ln_chain, LNC[0])
            dve.wait_ge(stats_done, NT * (nth + 1))
            me, m2e, mo, m2o = stats[:, :, 1], stats[:, :, 2], stats[:, :, 4], stats[:, :, 5]
            s, d, d2, v, v2, var, sd, y, t = (ln[:, i, :] for i in (2, 3, 4, 5, 6, 7, 8, 9, 2))
            nc.vector.tensor_tensor(s, me, mo, ALU.add)
            nc.vector.tensor_tensor(d, me, mo, ALU.subtract)
            step(nc.vector.tensor_tensor(v, m2e, m2o, ALU.add))
            nc.vector.tensor_scalar(mean, s, 0.5, None, ALU.mult)
            nc.vector.tensor_tensor(d2, d, d, ALU.mult)
            step(nc.vector.tensor_scalar(v2, v, 1.0 / C, LN_EPS, ALU.mult, ALU.add))
            nc.vector.scalar_tensor_tensor(var, d2, 0.25, v2, ALU.mult, ALU.add).then_inc(ln_var, 1)
            dve.wait_ge(ln_std, nth + 1)
            step(nc.vector.reciprocal(y, sd))
            step(nc.vector.tensor_tensor(t, y, y, ALU.mult))
            step(nc.vector.tensor_tensor(t, t, var, ALU.mult))
            step(nc.vector.tensor_scalar(t, t, -0.5, 1.5, ALU.mult, ALU.add))
            step(nc.vector.tensor_tensor(rstd, y, t, ALU.mult))

        def ln_sqrt(act, nth):
            act.wait_ge(ln_var, nth + 1)
            nc.scalar.activation(ln[:, 8, :], ln[:, 7, :], ACT.Sqrt).then_inc(ln_std, 1)

        class Turn:
            def __init__(self, name):
                self.norm_ready = sem(name + "_norm_ready")
                self.norm_used = sem(name + "_norm_used")
                self.turned = sem(name + "_turned")
                self.copied = sem(name + "_copied")
                self.t_used = sem(name + "_t_used")

        t2, t5, t6, t7, t8 = (Turn(f"t{n}") for n in (2, 5, 6, 7, 8))

        qkv_done = sem("qkv_done"); qk_taken = sem("qk_taken"); v_taken = sem("v_taken")
        red = sem("red"); hi_done = sem("hi_done"); sub_done = sem("sub_done"); piece_out = [sem(f"piece_out{n}") for n in range(2 * NPIECE)]
        op_in = [sem(f"op_in{i}") for i in range(2)]; op_zero = sem("op_zero"); op_one = sem("op_one"); op_mask = sem("op_mask")
        mm_num = sem("mm_num"); mm_den = sem("mm_den"); sin_done = sem("sin_done")
        num_used = sem("num_used"); den_used = sem("den_used")
        mm_early = sem("mm_early"); early_taken = sem("early_taken"); num_first = sem("num_first"); guard_set = sem("guard_set")
        den8_done = sem("den8_done"); num8_done = sem("num8_done"); scale_done = sem("scale_done")
        den_scaled = sem("den_scaled"); num_scaled = sem("num_scaled"); den_f_done = sem("den_f_done"); den_pair_done = sem("den_pair_done"); num_x_done = sem("num_x_done")
        num_f_done = sem("num_f_done"); rec_done = sem("rec_done")
        ratio_ready = sem("ratio_ready"); sq_done = sem("sq_done"); w4_ready = sem("w4_ready")
        av_done = sem("av_done"); av_copied = sem("av_copied")
        o_chain = sem("o_chain"); proj_done = sem("proj_done"); proj_taken = sem("proj_taken"); h_sum = sem("h_sum")
        g_sum = sem("g_sum"); g_mm = sem("g_mm"); g_chain = sem("g_chain"); g_act = sem("g_act")
        g_idx = sem("g_idx"); g_row = sem("g_row"); g_in = [sem(f"g_in{i}") for i in range(4)]
        g_copied = sem("g_copied"); y_done = sem("y_done"); y_taken = sem("y_taken"); y_sum = sem("y_sum")
        p_done = sem("p_done"); p_act = sem("p_act"); p_dve = sem("p_dve")
        s_done = sem("s_done"); s_max = sem("s_max"); s_exp = sem("s_exp")
        pt_done = sem("pt_done"); pt_copied = sem("pt_copied"); pv_done = sem("pv_done"); o_norm = sem("o_norm")
        rr = sem("rr"); ot_done = sem("ot_done"); ot_copied = sem("ot_copied"); wo_done = sem("wo_done"); wo_sum = sem("wo_sum")
        h_add = sem("h_add")
        l_done = sem("l_done"); l_taken = sem("l_taken"); r_iota = sem("r_iota"); r_chain = sem("r_chain"); r_exp = sem("r_exp")
        wp_ready = sem("wp_ready"); wp_turned = sem("wp_turned"); wp_copied = sem("wp_copied")
        b2_done = sem("b2_done"); h_done = sem("h_done"); hid_ready = sem("hid_ready")
        e_done = sem("e_done"); e_sum = sem("e_sum"); out_done = sem("out_done"); wp_zero = sem("wp_zero")

        def wait(eng, s, value):
            if not isinstance(value, int) or value > 0:
                eng.wait_ge(s, value)

        nW = [0, 0, 0]
        block = ctx.enter_context(nc.Block())

        @block.sync
        def _(sp):
            def load(dst, src, s, k):
                sp.dma_start(dst, src).then_inc(s, 16)
                nW[k] += 16
            cw = conv_w[0:8].rearrange("(j two) c o -> two c j o", two=2)
            load(conv_w_sb[0:CIN, 0:4, :], cw[0], s_w, 0)
            load(conv_w_sb[CIN:P, 0:4, :], cw[1], s_w, 0)
            load(conv_w_sb[0:CIN, 4, :], conv_w[8], s_w, 0)
            load(conv_b_sb[:, :], conv_b.rearrange("(a n) -> a n", a=1).to_broadcast([P, C]), s_w, 0)
            sp.wait_ge(x_clear, 2)
            with sp.Fori(0, B // 2) as it:
                for j in range(2):
                    sp.wait_ge(x_free, it * 2 + j + 1)
                    src = x[bass.ds(it * 2 + j, 1)].rearrange("a c l -> (a c) l")
                    sp.dma_start(xs[j][0:CIN, PAD:PAD + L], src).then_inc(x_in[j], 16)
                    sp.dma_start(xs[j][CIN:P, PAD - 1:PAD - 1 + L], src).then_inc(x_in[j], 16)
            sp.wait_ge(op_zero, 4)
            for j in range(2):
                for s in range(2):
                    sp.dma_start(q_op[j][0:KROWS, s, :], neg_mask).then_inc(op_mask, 16)
            for n in range(2 * NPIECE):
                p, s = n // 2, n % 2
                sp.wait_ge(hi_done, n + 1)
                t = piece[p % 2][s]
                sp.dma_start(q_dram[p, s].rearrange("(b g) (d t) -> (g d) b t", g=H, d=DH),
                             t[:, 0, :].rearrange("p (b t) -> p b t", b=B)).then_inc(piece_out[n], 16)
                sp.dma_start(k_dram[p, :, :, s, :].rearrange("(b g) d t -> (g d) b t", g=H),
                             t[:, 1, :].rearrange("p (b t) -> p b t", b=B)).then_inc(piece_out[n], 16)
            for n in range(2 * NPIECE):
                sp.wait_ge(piece_out[n], 32)
            def load_operands(i, j):
                if not isinstance(i, int):
                    sp.wait_ge(mm_den, i * 6 - 6)
                sp.dma_start(k_op[j][0:KROWS, :, :].rearrange("r s t -> r (s t)"),
                             k_dram[:, bass.ds(i, 1)].rearrange("p i d s t -> p (i d) (s t)")).then_inc(op_in[j], 16)
                sp.dma_start(q_op[j][QROW:QROW + NPIECE, :, :],
                             q_dram[:, :, bass.ds(i, 1), :].rearrange("p s i n -> p s (i n)")).then_inc(op_in[j], 16)

            for j in range(2):
                load_operands(j, j)
            with sp.Fori(1, NHEAD // 2) as it:
                for j in range(2):
                    load_operands(it * 2 + j, j)
            sp.wait_ge(g_idx, 1)
            sp.dma_start(idx_row[0:1, :], idx0[:, 0:1]).then_inc(g_row, 16)
            sp.wait_ge(g_row, 16)
            for i in range(B):
                j = i % 4
                wait(sp, y_sum, 2 * (i - 3))
                e = sp.value_load(idx_row[0:1, i:i + 1], min_val=0, max_val=E0 - 1)
                sp.dma_start(w_sel[j][:, :], exp0_w[bass.ds(e, 1)].rearrange("a d o -> (a d) o")).then_inc(g_in[j], 16)
                sp.dma_start(b_sel[j][:, :], exp0_b[bass.ds(e, 1), :].to_broadcast([P, C])).then_inc(g_in[j], 16)
            sp.wait_ge(e_sum, 1)
            sp.dma_start(out.rearrange("b (u p) c -> p (b u) c", p=P), h[:, :, :]).then_inc(out_done, 16)
            sp.wait_ge(out_done, 16)

        @block.gpsimd
        def _(pool):
            for j in range(2):
                nc.gpsimd.memset(xs[j][:, :], 0.0).then_inc(x_clear, 1)
            nc.gpsimd.memset(v_ext[:, :, :, :], 1.0).then_inc(v_set, 1)
            nc.gpsimd.memset(ones[:, :], 1.0).then_inc(s_ones, 1)
            for j in range(2):
                nc.gpsimd.memset(k_op[j][:, :, :], 0.0).then_inc(op_zero, 1)
                nc.gpsimd.memset(q_op[j][:, :, :], 0.0).then_inc(op_zero, 1)
            pool.wait_ge(op_zero, 4)
            for j in range(2):
                nc.gpsimd.memset(k_op[j][QROW:QROW + NPIECE, :, :], 1.0).then_inc(op_one, 1)
            pool.wait_ge(op_one, 2)
            nc.gpsimd.memset(w_pad[:, :, :], 0.0).then_inc(wp_zero, 1)
            nc.gpsimd.memset(guard_col[:, :], GUARD * LANE_SCALE).then_inc(guard_set, 1)
            nc.gpsimd.iota(iota[:, :, :], pattern=[[0, NT], [1, E1]], base=0, channel_multiplier=0,
                           allow_small_or_imprecise_dtypes=True).then_inc(r_iota, 1)


            def half(dst, src, n):
                return nc.gpsimd.tensor_tensor(dst, src[:, 0:n], src[:, n:2 * n], ALU.mult)

            def quotient(u, par):
                pool.wait_ge(den_used, u * 3 + 3)
                half(den8[:, :], den[par], 2 * L).then_inc(den8_done, 1)
                pool.wait_ge(num_used, u * 3 + 3)
                half(num8[:, :], num[par], 2 * L).then_inc(num8_done, 1)
                pool.wait_ge(scale_done, u + 1)
                pool.wait_ge(den8_done, u + 1)
                nc.gpsimd.tensor_tensor(den8[:, :], den8[:, :], scale_f[:, :], ALU.mult).then_inc(den_scaled, 1)
                pool.wait_ge(num8_done, u + 1)
                nc.gpsimd.tensor_tensor(num8[:, :], num8[:, :], scale_f[:, :], ALU.mult).then_inc(num_scaled, 1)
                pool.wait_ge(den_scaled, u + 1)
                half(den_f[:, :], den8, L).then_inc(den_f_done, 1)
                pool.wait_ge(den_f_done, u + 1)
                wait(pool, rec_done, u)
                half(den_pair[:, :], den_f, P).then_inc(den_pair_done, 1)
                pool.wait_ge(num_scaled, u + 1)
                half(num_f[:, :], num8, L).then_inc(num_f_done, 1)
                pool.wait_ge(num_f_done, u + 1)
                nc.gpsimd.tensor_tensor(num_x[:, :, :], num_f[:, :].rearrange("p (a t) -> p a t", a=2),
                                        den_f[:, :].rearrange("p (a t) -> p a t", a=2)[:, ::-1, :],
                                        ALU.mult).then_inc(num_x_done, 1)
                pool.wait_ge(num_x_done, u + 1)
                pool.wait_ge(rec_done, u + 1)
                wait(pool, sq_done, u - 1)
                nc.gpsimd.tensor_tensor(ratio[par][:, :].rearrange("p (a t) -> p a t", a=2), num_x[:, :, :],
                                        rec_pair[:, :].unsqueeze(1).to_broadcast([P, 2, P]),
                                        ALU.mult).then_inc(ratio_ready, 1)

            for k in range(4):
                quotient(k, k % 2)
            with pool.Fori(1, NUNIT // 4) as it:
                for k in range(4):
                    quotient(it * 4 + k, k % 2)

        @block.scalar
        def _(act):
            def load(dst, src, s, k):
                act.dma_start(dst, src).then_inc(s, 16)
                nW[k] += 16
            load(ident[:, :], ident_in, s_w2, 1)
            load(r_col[:, :], param_r.rearrange("(a n) -> a n", a=1).to_broadcast([P, 1]), s_w2, 1)
            load(w_qk_sb[:, :], w_qk, s_w2, 1)
            load(w_v_sb[:, :], w_v, s_w2, 1)
            load(w_proj_sb[:, :], w_proj, s_late, 2)
            load(b_proj_sb[:, :], b_proj.rearrange("(a n) -> a n", a=1).to_broadcast([P, C]), s_late, 2)
            load(gate0_w_sb[:, :], gate0_w, s_late, 2)
            load(gate0_b_sb[:, :], gate0_b.rearrange("(a n) -> a n", a=1).to_broadcast([B, E0]), s_late, 2)
            load(wq1_sb[:, :], wq1, s_late, 2)
            load(wk1_sb[:, :], wk1, s_late, 2)
            load(wv1_sb[:, :], wv1, s_late, 2)
            load(wo1_sb[:, :, :], wo1.rearrange("(k p) c -> p k c", p=P), s_late, 2)
            load(gate1_w_sb[:, :], gate1_w, s_late, 2)
            load(gate1_b_sb[:, :], gate1_b.rearrange("(a n) -> a n", a=1).to_broadcast([P, E1]), s_late, 2)
            load(w1_sb[:, :, :], w1.rearrange("e h f -> h e f"), s_late, 2)
            with nc.allow_non_contiguous_dma(reason="biases: 2048 single elements, once"):
                load(b1_sb[:, :], b1.rearrange("e (u p) -> p (e u)", p=P), s_late, 2)
            load(w2_sb[:, :, :], w2.rearrange("e (u p) h -> p (e u) h", p=P), s_late, 2)
            for t in range(4):
                load(b2_sb[32 * t:32 * t + E1, :], b2, s_late, 2)

            for s in (t2.copied, t5.copied, t6.copied, t8.copied, qk_taken, hid_ready):
                act.sem_inc(s, 1)
            ln_sqrt(act, 0)
            act.wait_ge(s_w2, nW[1])
            with act.Fori(0, B // 2) as it:
                for j in range(2):
                    act.wait_ge(t2.turned, it * 4 + 2 * j + 2)
                    act.wait_ge(t2.t_used, it * 2 + (j + 1))
                    nc.scalar.copy(norm_t[j][:, :], bank[j][:, 0:L]).then_inc(t2.copied, 1)
                for j in range(2):
                    act.wait_ge(qkv_done, it * 4 + 2 * j + 1)
                    nc.scalar.activation(qk[:, 1, :, bass.ds((it * 2 + j) * L, L)],
                                         bank[2 + j][:, :].rearrange("p (s t) -> p s t", s=2),
                                         ACT.Copy, scale=r_col[:, 0:1]).then_inc(qk_taken, 1)
            for n in range(2 * NPIECE):
                p, s = n // 2, n % 2
                src = [[qk[:, 0], qk[:, 1]], [rest, qk[:, 0]], [rest, qk[:, 0]]]
                if p == 0:
                    act.wait_ge(red, 4) if s == 0 else act.wait_ge(qk_taken, B + 1)
                else:
                    act.wait_ge(sub_done, n - 1)
                if p == 2:
                    act.wait_ge(piece_out[s], 32)
                dst = piece[p % 2][s]
                in_ = (qk[:, s] if p == 0 else (rest[:, :, :] if s == 0 else qk[:, 0]))
                nc.scalar.copy(dst[:, :, :], in_).then_inc(hi_done, 1)
            act.wait_ge(s_rpow, 4)
            act.wait_ge(guard_set, 1)
            act.sem_inc(av_copied, 1)

            def squares(u, i, par, j):
                wait(act, w4_ready, u)
                act.wait_ge(ratio_ready, u + 1)
                nc.scalar.activation(score2[:, :], ratio[par][:, :], ACT.Square,
                                     scale=r_pow[:, 3:4]).then_inc(sq_done, 1)
                act.wait_ge(sq_done, u + 1)
                wait(act, av_done, i)
                nc.scalar.activation(weight4[j][:, par, :], score2[:, :], ACT.Square).then_inc(w4_ready, 1)

            def copy_av(i):
                act.wait_ge(av_done, i + 2)
                nc.scalar.copy(o_raw[:, bass.ds(i, 1), :, :].rearrange("p i u d -> p (i u d)"),
                               bank[ATTEND][:, 0:2 * (DH + 1)]).then_inc(av_copied, 1)

            def take_early(u, par, n):
                act.wait_ge(mm_early, u * 4 + (n + 1))
                if n < 2:
                    wait(act, num_first, u)
                    nc.scalar.activation(first_sin[:, n * HALF:(n + 1) * HALF], bank[EARLY],
                                         ACT.Sin).then_inc(early_taken, 1)
                else:
                    wait(act, den8_done, u - 1)
                    nc.scalar.activation(den[par][:, (n - 2) * HALF:(n - 1) * HALF], bank[EARLY], ACT.Identity,
                                         bias=guard_col[:, 0:1], scale=LANE_SCALE).then_inc(early_taken, 1)

            def first_factors(u, par):
                act.wait_ge(early_taken, u * 4 + 2)
                wait(act, num8_done, u - 1)
                nc.scalar.activation(num[par], first_sin, ACT.Identity, bias=guard_col[:, 0:1],
                                     scale=LANE_SCALE).then_inc(num_first, 1)

            def sines(u, par, c):
                act.wait_ge(mm_num, u * 3 + c)
                a = pair[(c - 1 + par) % 2]
                nc.scalar.activation(a[:, :], a[:, :], ACT.Sin).then_inc(sin_done, 1)

            def act_slot(q, k, first, last):
                u, i, par = q * 4 + k, q * 2 + k // 2, k % 2
                has_next = not (last and k == 3)
                sines(u, par, 1)
                take_early(u, par, 3)
                if has_next:
                    take_early(u + 1, 1 - par, 0)
                sines(u, par, 2)
                if not (first and k < 2):
                    squares(u - 2, i - 1, par, (k // 2 + 1) % 2)
                if has_next:
                    take_early(u + 1, 1 - par, 1)
                sines(u, par, 3)
                if has_next:
                    take_early(u + 1, 1 - par, 2)
                    first_factors(u + 1, 1 - par)
                if par == 1 and not first:
                    copy_av(i - 2)

            for n in range(3):
                take_early(0, 0, n)
            first_factors(0, 0)
            for k in range(4):
                act_slot(0, k, True, False)
            with act.Fori(1, NUNIT // 4 - 1) as it:
                for k in range(4):
                    act_slot(it, k, False, False)
            for k in range(4):
                act_slot(NUNIT // 4 - 1, k, False, True)
            squares(NUNIT - 2, NHEAD - 1, 0, 1)
            copy_av(NHEAD - 2)
            squares(NUNIT - 1, NHEAD - 1, 1, 1)
            copy_av(NHEAD - 1)
            with act.Fori(0, B // 2) as it:
                for j in range(2):
                    act.wait_ge(t5.turned, it * 4 + 2 * j + 2)
                    act.wait_ge(t5.t_used, it * 2 + (j + 1))
                    nc.scalar.copy(norm_t[j][:, :], bank[j][:, 0:L]).then_inc(t5.copied, 1)
            ln_sqrt(act, 1)
            with act.Fori(0, B // 2) as it:
                for j in range(2):
                    act.wait_ge(t6.turned, it * 4 + 2 * j + 2)
                    nc.scalar.copy(all_t[:, bass.ds((it * 2 + j) * L, L)], bank[j][:, 0:L]).then_inc(t6.copied, 1)
            act.wait_ge(g_chain, 3)
            nc.scalar.activation(ex0[:, :], lg0[:, :], ACT.Exp, bias=sm0[:, 1:2], accum_out=sm0[:, 2:3]).then_inc(g_act, 1)
            with act.Fori(0, B // 2) as it:
                for j in range(2):
                    act.wait_ge(t6.t_used, it * 2 + (j + 1))
                    nc.scalar.copy(norm_t[j][:, :], all_t[:, bass.ds((it * 2 + j) * L, L)]).then_inc(g_copied, 1)
            ln_sqrt(act, 2)

            def copy_norm1(b):
                act.wait_ge(t7.turned, b * 2 + 2)
                nc.scalar.copy(norm_t[0][:, :], bank[1][:, 0:L]).then_inc(t7.copied, 1)

            def keep_act(b, z, n):
                act.wait_ge(p_done, b * 6 + (n + 1))
                src = bank[1][:, :]
                if n == 0:
                    nc.scalar.activation(q1[z][:, 0:2, :], src.rearrange("p (a t) -> p a t", a=2), ACT.Copy,
                                         scale=float(D1) ** -0.5).then_inc(p_act, 1)
                elif n == 2:
                    nc.scalar.copy(k1[z][:, 0:2, :], src.rearrange("p (a t) -> p a t", a=2)).then_inc(p_act, 1)
                else:
                    nc.scalar.copy(v1[z][:, 0, :], src).then_inc(p_act, 1)

            def copy_o1(n):
                act.wait_ge(ot_done, n + 1)
                nc.scalar.copy(o1_t[:, :, :], bank[1][:, :].rearrange("p (a t) -> p a t", a=4)).then_inc(ot_copied, 1)

            def act_batch(b, z, first, last):
                for m in range(16):
                    act.wait_ge(s_max, b * 16 + (m + 1))
                    wait(act, pt_done, b * 16 + (m - 1))
                    nc.scalar.activation(prob[m % 2][:, :], bank[4 + m % 2][:, 0:L], ACT.Exp,
                                         bias=neg_max[:, m:m + 1], accum_out=row_sum[:, m:m + 1]).then_inc(s_exp, 1)
                    if m == 2 and not last:
                        copy_norm1(b + 1)
                    if m == 4 and not first:
                        copy_o1(b * 2 - 1)
                    if m in (6, 8, 10) and not last:
                        keep_act(b + 1, 1 - z, m - 6)
                    if m == 12:
                        copy_o1(b * 2)

            copy_norm1(0)
            for n in (0, 2, 4):
                keep_act(0, 0, n)
            act_batch(0, 0, True, False)
            with act.Fori(0, B // 2 - 1) as it:
                for z in range(2):
                    act_batch(it * 2 + (z + 1), 1 - z, False, False)
            act_batch(B - 1, 1, False, True)
            copy_o1(2 * B - 1)
            ln_sqrt(act, 3)
            with act.Fori(0, B // 2) as it:
                for j in range(2):
                    act.wait_ge(t8.turned, it * 4 + 2 * j + 2)
                    act.wait_ge(t8.t_used, it * 2 + (j + 1))
                    nc.scalar.copy(norm_t[j][:, :], bank[j][:, 0:L]).then_inc(t8.copied, 1)
                    nc.scalar.copy(all_t[:, bass.ds((it * 2 + j) * L, L)], bank[j][:, 0:L]).then_inc(t8.copied, 1)
            act.wait_ge(r_chain, 10)
            nc.scalar.activation(rsm[:, 3, :], rsm[:, 2, :], ACT.Exp).then_inc(r_exp, 1)
            with act.Fori(0, NG) as g:
                for n in range(2 * E1):
                    act.wait_ge(h_done, g * 16 + n + 1)
                    act.wait_ge(e_done, g * 8 + (n // 2 + 1))
                    nc.scalar.activation(hid[n % 4][:, :], bank[n % 2][:, :], ACT.Relu,
                                         bias=b1_sb[:, n:n + 1]).then_inc(hid_ready, 1)

        @block.vector
        def _(dve):
            dve.sem_inc(conv_taken, 4)
            for s in (v_taken, proj_taken, y_taken, l_taken):
                dve.sem_inc(s, 1)
            dve.wait_ge(s_w, nW[0])
            with dve.Fori(0, B // 2) as it:
                for k in range(4):
                    n = it * 4 + k
                    dve.wait_ge(conv_done, n + 1)
                    nc.vector.tensor_tensor(h[:, bass.ds(n, 1), :].rearrange("p a c -> p (a c)"), bank[k][:, 0:C],
                                            conv_b_sb[:, :], ALU.add).then_inc(conv_taken, 1)
                    dve.wait_ge(conv_taken, n + 5)
                    nc.vector.bn_stats(stats[:, bass.ds(n, 1), :].rearrange("p a s -> p (a s)"),
                                       h[:, bass.ds(n, 1), :].rearrange("p a c -> p (a c)")).then_inc(stats_done, 1)
            ln_math(dve, 0)

            def normalise(n, k, turn):
                dve.wait_ge(turn.norm_used, n + 1)
                nc.vector.tensor_scalar(norm[k][:, :], h[:, bass.ds(n, 1), :].rearrange("p a c -> p (a c)"),
                                        mean[:, bass.ds(n, 1)], rstd[:, bass.ds(n, 1)],
                                        ALU.subtract, ALU.mult).then_inc(turn.norm_ready, 1)

            dve.wait_ge(s_w2, nW[1])
            for n in range(4):
                a = r_col[:, 0:1] if n == 0 else r_pow[:, n - 1:n]
                if n:
                    dve.wait_ge(s_rpow, n)
                nc.vector.tensor_tensor(r_pow[:, n:n + 1], a, a, ALU.mult).then_inc(s_rpow, 1)
            dve.wait_ge(v_set, 1)

            def copy_values(it):
                for j in range(2):
                    dve.wait_ge(qkv_done, it * 4 + 2 * j + 2)
                    for u in range(2):
                        nc.vector.tensor_copy(v_ext[:, bass.ds((it * 2 + j) * H, H), u, 0:DH],
                                              bank[4 + j][:, u * C:(u + 1) * C].rearrange("p (g d) -> p g d", g=H)
                                              ).then_inc(v_taken, 1)

            for k in range(4):
                normalise(k, k, t2)
            with dve.Fori(0, B // 2 - 1) as it:
                for k in range(4):
                    normalise(it * 4 + (k + 4), k, t2)
                copy_values(it)
            copy_values(B // 2 - 1)
            dve.wait_ge(qk_taken, B + 1)
            nc.vector.tensor_scalar(rest[:, :, :], qk[:, 1], 1.0 / PI, MAGIC, ALU.mult, ALU.add).then_inc(red, 1)
            dve.wait_ge(red, 1)
            nc.vector.tensor_scalar(rest[:, :, :], rest[:, :, :], MAGIC, -PI, ALU.subtract, ALU.mult).then_inc(red, 1)
            dve.wait_ge(red, 2)
            nc.vector.tensor_tensor(qk[:, 0], qk[:, 1], rest[:, :, :], ALU.add).then_inc(red, 1)
            dve.wait_ge(red, 3)
            nc.vector.tensor_scalar(qk[:, 0], qk[:, 0], HALF_PI, -HALF_PI, ALU.min, ALU.max).then_inc(red, 1)
            dve.wait_ge(red, 4)
            dve.wait_ge(hi_done, 1)
            nc.vector.tensor_tensor(rest[:, :, :], qk[:, 0], piece[0][0][:, :, :], ALU.subtract).then_inc(sub_done, 1)
            dve.wait_ge(hi_done, 2)
            dve.wait_ge(sub_done, 1)
            nc.vector.tensor_tensor(qk[:, 0], qk[:, 1], piece[0][1][:, :, :], ALU.subtract).then_inc(sub_done, 1)
            dve.wait_ge(hi_done, 3)
            nc.vector.tensor_tensor(rest[:, :, :], rest[:, :, :], piece[1][0][:, :, :], ALU.subtract).then_inc(sub_done, 1)
            dve.wait_ge(hi_done, 4)
            dve.wait_ge(sub_done, 2)
            nc.vector.tensor_tensor(qk[:, 0], qk[:, 0], piece[1][1][:, :, :], ALU.subtract).then_inc(sub_done, 1)
            def scale_and_divide(u, part):
                if part == 0:
                    dve.wait_ge(den8_done, u + 1)
                    wait(dve, num_scaled, u)
                    nc.vector.tensor_scalar(scale_f[:, :].bitcast(U32), den8[:, :].bitcast(U32), EXP_EVEN, EXP_FLIP,
                                            ALU.bitwise_and, ALU.bitwise_xor).then_inc(scale_done, 1)
                else:
                    dve.wait_ge(den_pair_done, u + 1)
                    wait(dve, ratio_ready, u)
                    nc.vector.reciprocal(rec_pair[:, :], den_pair[:, :]).then_inc(rec_done, 1)

            def dve_slot(q, k, early):
                u, par = q * 4 + k, k % 2
                for c in range(1, NCHUNK):
                    dve.wait_ge(sin_done, u * 3 + c)
                    dve.wait_ge(num_first, u + 1) if c == 1 else dve.wait_ge(num_used, u * 3 + (c - 1))
                    nc.vector.scalar_tensor_tensor(num[par], pair[(c - 1 + par) % 2][:, :], GUARD, num[par],
                                                   ALU.add, ALU.mult).then_inc(num_used, 1)
                    dve.wait_ge(mm_den, u * 3 + c)
                    dve.wait_ge(early_taken, u * 4 + 4) if c == 1 else dve.wait_ge(den_used, u * 3 + (c - 1))
                    nc.vector.scalar_tensor_tensor(den[par], pair[2][:, :], GUARD, den[par],
                                                   ALU.add, ALU.mult).then_inc(den_used, 1)
                    if c != 2 and not (early and k == 0):
                        scale_and_divide(u - 1, 0 if c == 1 else 1)

            for k in range(4):
                dve_slot(0, k, True)
            with dve.Fori(1, NUNIT // 4) as it:
                for k in range(4):
                    dve_slot(it, k, False)
            scale_and_divide(NUNIT - 1, 0)
            scale_and_divide(NUNIT - 1, 1)
            dve.wait_ge(av_copied, NHEAD + 1)
            nc.vector.tensor_scalar(o_den[:, :, :], o_raw[:, :, :, DH], ATTN_EPS, None, ALU.add).then_inc(o_chain, 1)
            dve.wait_ge(o_chain, 1)
            nc.vector.reciprocal(o_rec[:, :, :], o_den[:, :, :]).then_inc(o_chain, 1)
            dve.wait_ge(o_chain, 2)
            dve.wait_ge(s_late, nW[2])

            def divide(it):
                for k in range(4):
                    j, u = k // 2, k % 2
                    hs = bass.ds((it * 2 + j) * H, H)
                    dve.wait_ge(t5.norm_used, it * 4 + (k + 1))
                    nc.vector.tensor_tensor(norm[k][:, :].rearrange("p (g d) -> p g d", g=H), o_raw[:, hs, u, 0:DH],
                                            o_rec[:, hs, u].unsqueeze(2).to_broadcast([P, H, DH]), ALU.mult
                                            ).then_inc(t5.norm_ready, 1)

            def tile(n):
                return h[:, bass.ds(n, 1), :].rearrange("p a c -> p (a c)")

            def tile_stats(n):
                nc.vector.bn_stats(stats[:, bass.ds(n, 1), :].rearrange("p a s -> p (a s)"), tile(n)).then_inc(stats_done, 1)

            def add_projection(it):
                for k in range(4):
                    dve.wait_ge(proj_done, it * 4 + (k + 1))
                    nc.vector.tensor_tensor(tmp[k][:, :], bank[2 + k][:, 0:C], b_proj_sb[:, :], ALU.add).then_inc(proj_taken, 1)
                for k in range(4):
                    dve.wait_ge(proj_taken, it * 4 + (k + 2))
                    nc.vector.tensor_tensor(tile(it * 4 + k), tmp[k][:, :], tile(it * 4 + k), ALU.add).then_inc(h_sum, 1)
                for k in range(4):
                    dve.wait_ge(h_sum, it * 4 + (k + 1))
                    tile_stats(it * 4 + k)

            divide(0)
            with dve.Fori(0, B // 2 - 1) as it:
                divide(it + 1)
                add_projection(it)
            add_projection(B // 2 - 1)
            ln_math(dve, 1)
            with dve.Fori(0, B // 2) as it:
                for k in range(4):
                    normalise(it * 4 + k, k, t6)
            dve.wait_ge(t6.copied, B + 1)
            nc.vector.tensor_reduce(tok_sum[:, :], all_t.rearrange("p (b t) -> p b t", b=B), AX.X, ALU.add).then_inc(g_sum, 1)
            dve.wait_ge(g_mm, 1)
            nc.vector.scalar_tensor_tensor(lg0[:, :], bank[6][0:B, 0:E0], 1.0 / L, gate0_b_sb[:, :],
                                           ALU.mult, ALU.add).then_inc(g_chain, 1)
            dve.wait_ge(g_chain, 1)
            nc.vector.tensor_reduce(sm0[:, 0:1], lg0[:, :], AX.X, ALU.max).then_inc(g_chain, 1)
            dve.wait_ge(g_chain, 2)
            nc.vector.tensor_scalar(sm0[:, 1:2], sm0[:, 0:1], -1.0, None, ALU.mult).then_inc(g_chain, 1)
            dve.wait_ge(g_act, 1)
            nc.vector.max(top0[:, :], ex0[:, :]).then_inc(g_chain, 1)
            nc.vector.reciprocal(sm0[:, 3:4], sm0[:, 2:3]).then_inc(g_chain, 1)
            dve.wait_ge(g_chain, 5)
            nc.vector.max_index(idx0[:, :], top0[:, :], ex0[:, :]).then_inc(g_idx, 1)
            nc.vector.tensor_tensor(sm0[:, 4:5], top0[:, 0:1], sm0[:, 3:4], ALU.mult).then_inc(g_chain, 1)
            dve.wait_ge(g_chain, 6)
            nc.vector.tensor_scalar(gate_diag[:, :], ident[0:B, 0:B], sm0[:, 4:5], None, ALU.mult).then_inc(g_chain, 1)
            dve.wait_ge(g_mm, 2)
            nc.vector.tensor_copy(gate_col[:, :], bank[6][:, 32:32 + B]).then_inc(g_chain, 1)
            dve.wait_ge(g_chain, 8)
            with dve.Fori(0, 2) as it:
                for half in range(2):
                    for k in range(4):
                        j, n = 2 * half + k // 2, it * 8 + (4 * half + k)
                        dve.wait_ge(g_in[j], it * 32 + 32)
                        dve.wait_ge(y_done, n + 1)
                        nc.vector.tensor_tensor(tmp[k][:, :], bank[2 + k][:, 0:C], b_sel[j][:, :], ALU.add).then_inc(y_taken, 1)
                    for k in range(4):
                        j, n = 2 * half + k // 2, it * 8 + (4 * half + k)
                        dve.wait_ge(y_taken, n + 2)
                        nc.vector.scalar_tensor_tensor(tile(n), tmp[k][:, :], gate_col[:, bass.ds(it * 4 + j, 1)], tile(n),
                                                       ALU.mult, ALU.add).then_inc(y_sum, 1)
                    for k in range(4):
                        n = it * 8 + (4 * half + k)
                        dve.wait_ge(y_sum, n + 1)
                        tile_stats(n)
            ln_math(dve, 2)

            def normalise1(b):
                for u in range(2):
                    wait(dve, t7.turned, b * 2 + (u - 1))
                    wait(dve, h_add, b * 2 + (u - 1))
                    nc.vector.tensor_scalar(norm[u][:, :], tile(b * 2 + u), mean[:, bass.ds(b * 2 + u, 1)],
                                            rstd[:, bass.ds(b * 2 + u, 1)],
                                            ALU.subtract, ALU.mult).then_inc(t7.norm_ready, 1)
                for u in range(2):
                    dve.wait_ge(t7.norm_ready, b * 2 + (u + 1))
                    nc.vector.tensor_tensor(tile(b * 2 + u), tile(b * 2 + u), norm[u][:, :], ALU.add).then_inc(h_add, 1)

            def keep_dve(b, z, n):
                dve.wait_ge(p_done, b * 6 + (n + 1))
                src = bank[2][:, :]
                if n == 1:
                    nc.vector.tensor_scalar(q1[z][:, 2:4, :], src.rearrange("p (a t) -> p a t", a=2),
                                            float(D1) ** -0.5, None, ALU.mult).then_inc(p_dve, 1)
                elif n == 3:
                    nc.vector.tensor_copy(k1[z][:, 2:4, :], src.rearrange("p (a t) -> p a t", a=2)).then_inc(p_dve, 1)
                else:
                    nc.vector.tensor_copy(v1[z][:, 1, :], src).then_inc(p_dve, 1)

            def maxima(b, m):
                dve.wait_ge(s_done, b * 16 + (m + 1))
                nc.vector.tensor_reduce(neg_max[:, m:m + 1], bank[4 + m % 2][:, 0:L], AX.X, ALU.max,
                                        negate=True).then_inc(s_max, 1)

            def copy_pt(b, m):
                dve.wait_ge(pt_done, b * 16 + (m + 1))
                wait(dve, pv_done, b * 16 + (m - 1))
                nc.vector.tensor_copy(prob_t[m % 2][:, :, :],
                                      bank[6 - 3 * (m % 2)][:, 0:L].rearrange("p (a t) -> p a t", a=2)
                                      ).then_inc(pt_copied, 1)

            def norm_o(n, u):
                o_ps = bank[7] if u == 0 else bank[0]
                dve.wait_ge(s_exp, n * 8 + 8)
                nc.vector.reciprocal(row_rec[:, 8 * u:8 * u + 8], row_sum[:, 8 * u:8 * u + 8]).then_inc(rr, 1)
                dve.wait_ge(rr, n + 1)
                dve.wait_ge(pv_done, n * 8 + 8)
                wait(dve, ot_done, n)
                nc.vector.tensor_tensor(o1.rearrange("p (g d) -> p g d", g=H1),
                                        o_ps[:, :].rearrange("p (g d) -> p g d", g=H1),
                                        row_rec[:, 8 * u:8 * u + 8].unsqueeze(2).to_broadcast([P, H1, D1]),
                                        ALU.mult).then_inc(o_norm, 1)

            def add_wo(n):
                dve.wait_ge(wo_done, n + 1)
                dve.wait_ge(h_add, n + 1)
                nc.vector.tensor_tensor(tile(n), bank[2][:, 0:C], tile(n), ALU.add).then_inc(wo_sum, 1)
                dve.wait_ge(wo_sum, n + 1)
                nc.vector.bn_stats(stats[:, bass.ds(n, 1), :].rearrange("p a s -> p (a s)"), tile(n)).then_inc(stats_done, 1)

            def dve_batch(b, z, first, last):
                for m in range(16):
                    if m == 6 and not first:
                        add_wo(b * 2 - 1)
                    if m == 14:
                        add_wo(b * 2)
                    if m + 1 < 16:
                        maxima(b, m + 1)
                    elif not last:
                        maxima(b + 1, 0)
                    copy_pt(b, m)
                    if m == 0 and not last:
                        normalise1(b + 1)
                    if m == 1 and not first:
                        norm_o(b * 2 - 1, 1)
                    if m in (7, 9, 11) and not last:
                        keep_dve(b + 1, 1 - z, m - 6)
                    if m == 9:
                        norm_o(b * 2, 0)

            normalise1(0)
            for n in (1, 3, 5):
                keep_dve(0, 0, n)
            maxima(0, 0)
            dve_batch(0, 0, True, False)
            with dve.Fori(0, B // 2 - 1) as it:
                for z in range(2):
                    dve_batch(it * 2 + (z + 1), 1 - z, False, False)
            dve_batch(B - 1, 1, False, True)
            norm_o(2 * B - 1, 1)
            add_wo(2 * B - 1)
            ln_math(dve, 3)
            LG, A, M1, C1, M2, C2, WT, W2 = (route[:, i] for i in range(8))

            def keep_logits(it):
                for k in range(4):
                    dve.wait_ge(l_done, it * 4 + (k + 1))
                    nc.vector.tensor_tensor(LG[:, bass.ds(it * 4 + k, 1), :].rearrange("p a e -> p (a e)"),
                                            bank[2 + k][:, 0:E1], gate1_b_sb[:, :], ALU.add).then_inc(l_taken, 1)

            for k in range(4):
                normalise(k, k, t8)
            with dve.Fori(0, B // 2 - 1) as it:
                for k in range(4):
                    normalise(it * 4 + (k + 4), k, t8)
                keep_logits(it)
            keep_logits(B // 2 - 1)
            cnt = [0]

            def step(ins):
                cnt[0] += 1
                ins.then_inc(r_chain, 1)
                dve.wait_ge(r_chain, cnt[0])

            def wide(a):
                return a.unsqueeze(2).to_broadcast([P, NT, E1])
            dve.wait_ge(l_taken, NT + 1)
            dve.wait_ge(r_iota, 1)
            best, second, first_at, second_at = (rsm[:, i, :] for i in (0, 1, 4, 5))
            step(nc.vector.tensor_reduce(best, LG, AX.X, ALU.max))
            step(nc.vector.tensor_tensor(A, LG, wide(best), ALU.is_lt))
            step(nc.vector.scalar_tensor_tensor(C1, A, float(E1), iota[:, :, :], ALU.mult, ALU.add))
            step(nc.vector.tensor_reduce(first_at, C1, AX.X, ALU.min))
            step(nc.vector.tensor_tensor(M1, iota[:, :, :], wide(first_at), ALU.is_equal))
            step(nc.vector.scalar_tensor_tensor(C1, M1, -3e38, LG, ALU.mult, ALU.add))
            step(nc.vector.tensor_reduce(second, C1, AX.X, ALU.max))
            step(nc.vector.tensor_tensor(A, C1, wide(second), ALU.is_lt))
            step(nc.vector.scalar_tensor_tensor(C2, A, float(E1), iota[:, :, :], ALU.mult, ALU.add))
            step(nc.vector.tensor_tensor(rsm[:, 2, :], second, best, ALU.subtract))
            step(nc.vector.tensor_reduce(second_at, C2, AX.X, ALU.min))
            step(nc.vector.tensor_tensor(M2, iota[:, :, :], wide(second_at), ALU.is_equal))
            dve.wait_ge(r_exp, 1)
            step(nc.vector.tensor_scalar(rsm[:, 6, :], rsm[:, 3, :], 1.0, None, ALU.add))
            step(nc.vector.reciprocal(rsm[:, 7, :], rsm[:, 6, :]))
            step(nc.vector.tensor_tensor(rsm[:, 8, :], rsm[:, 3, :], rsm[:, 7, :], ALU.mult))
            step(nc.vector.tensor_tensor(WT, M1, wide(rsm[:, 7, :]), ALU.mult))
            step(nc.vector.tensor_tensor(W2, M2, wide(rsm[:, 8, :]), ALU.mult))
            step(nc.vector.tensor_tensor(WT, WT, W2, ALU.add))
            dve.wait_ge(wp_zero, 1)

            def pad_weights(g):
                dve.wait_ge(wp_turned, g + 1)
                nc.vector.tensor_copy(w_pad[:, :, 0:E1], WT[:, bass.ds(g * 4, 4), :]).then_inc(wp_ready, 1)

            def keep_weights(g):
                dve.wait_ge(wp_turned, g + 2)
                dve.wait_ge(b2_done, g * 4 + 1)
                nc.vector.tensor_copy(w_pad_t[:, :], bank[6][:, 0:P]).then_inc(wp_copied, 1)

            def add_biases(g):
                hg = h[:, bass.ds(g * 4, 4), :]
                dve.wait_ge(b2_done, g * 4 + 5)
                nc.vector.tensor_tensor(hg, bank[7][:, :].rearrange("p (a c) -> p a c", a=4), hg, ALU.add).then_inc(h_add, 1)

            def add_experts(g, last):
                dve.wait_ge(h_add, g + (NT + 1))
                for e in range(E1):
                    dve.wait_ge(e_done, g * 8 + (e + 3))
                    if e:
                        dve.wait_ge(y_taken, g * 32 + (NT + 4 * e + 1))
                    for t in range(4):
                        nc.vector.scalar_tensor_tensor(tile(g * 4 + t), bank[2 + e % 2][:, t * C:(t + 1) * C],
                                                       WT[:, bass.ds(g * 4 + t, 1), e], tile(g * 4 + t),
                                                       ALU.mult, ALU.add).then_inc(y_taken, 1)
                    if not last:
                        if e == 1:
                            pad_weights(g + 1)
                        if e == 4:
                            keep_weights(g + 1)
                if not last:
                    add_biases(g + 1)

            pad_weights(0)
            keep_weights(0)
            add_biases(0)
            with dve.Fori(0, NG - 1) as g:
                add_experts(g, False)
            add_experts(NG - 1, True)
            dve.wait_ge(y_taken, NT + NG * 32 + 1)
            dve.sem_inc(e_sum, 1)

        @block.tensor
        def _(pe):
            pe.wait_ge(s_w, nW[0])
            pe.sem_inc(x_free, 2)
            with pe.Fori(0, B // 2) as it:
                for j in range(2):
                    pe.wait_ge(x_in[j], it * 32 + 32)
                    for u in range(2):
                        k = 2 * j + u
                        pe.wait_ge(conv_taken, it * 4 + (k + 1))
                        for t in range(5):
                            rows = P if t < 4 else CIN
                            mm = nc.tensor.matmul(bank[k][:, 0:C], xs[j][0:rows, u * P + 2 * t:u * P + 2 * t + P],
                                                  conv_w_sb[0:rows, t, :], start=(t == 0), stop=(t == 4))
                        mm.then_inc(conv_done, 1)
                        if u == 1:
                            pe.wait_ge(conv_done, it * 4 + (k + 1))
                            pe.sem_inc(x_free, 1)

            def turn(tile0, j, ks, t, dst=None):
                for u in range(2):
                    pe.wait_ge(t.norm_ready, tile0 + (u + 1))
                    nc.tensor.transpose(bank[j][:, u * P:(u + 1) * P], norm[ks + u][:, :], ident[:, :]).then_inc(t.turned, 1)

            pe.wait_ge(s_w2, nW[1])
            pe.sem_inc(t2.norm_used, 4)
            pe.sem_inc(t2.t_used, 2)
            with pe.Fori(0, B // 2) as it:
                for j in range(2):
                    pe.wait_ge(t2.copied, it * 2 + 1)
                    turn(it * 4 + 2 * j, j, 2 * j, t2)
                pe.wait_ge(t2.turned, it * 4 + 4)
                pe.sem_inc(t2.norm_used, 4)
                for j in range(2):
                    pe.wait_ge(t2.copied, it * 2 + (j + 2))
                    pe.wait_ge(qk_taken, it * 2 + 1)
                    pe.wait_ge(v_taken, it * 4 + 1)
                    for s in range(2):
                        mm = nc.tensor.matmul(bank[2 + j][:, s * L:(s + 1) * L], w_qk_sb[:, s * C:(s + 1) * C],
                                              norm_t[j][:, :], start=True, stop=True)
                    mm.then_inc(qkv_done, 1)
                    for u in range(2):
                        mm = nc.tensor.matmul(bank[4 + j][:, u * C:(u + 1) * C], norm_t[j][:, u * P:(u + 1) * P],
                                              w_v_sb[:, :], start=True, stop=True)
                    mm.then_inc(qkv_done, 1)
                    pe.wait_ge(qkv_done, it * 4 + 2 * j + 2)
                    pe.sem_inc(t2.t_used, 1)
            pe.wait_ge(qk_taken, B + 1)
            pe.wait_ge(v_taken, NT + 1)
            pe.wait_ge(op_one, 2)
            pe.wait_ge(op_mask, 64)
            pe.sem_inc(av_done, 1)

            def products(a, j, par, s, c):
                for t in range(2):
                    col = c * CHUNK + t * 512
                    mm = nc.tensor.matmul(pair[a][:, t * 512:(t + 1) * 512], k_op[j][0:ROWS, s, par * P:(par + 1) * P],
                                          q_op[j][0:ROWS, s, col:col + 512], start=True, stop=True)
                return mm

            def attend(i, j, t):
                if t == 0:
                    pe.wait_ge(w4_ready, i * 2 + 2)
                    pe.wait_ge(av_copied, i + 1)
                for kt in range(2):
                    mm = nc.tensor.matmul(bank[ATTEND][:, t * (DH + 1):(t + 1) * (DH + 1)],
                                          weight4[j][:, kt, t * P:(t + 1) * P],
                                          v_ext[:, bass.ds(i, 1), kt, :].rearrange("p a d -> p (a d)"),
                                          start=(kt == 0), stop=(kt == 1))
                if t == 1:
                    mm.then_inc(av_done, 1)

            def early(u, j, par, n):
                wait(pe, early_taken, u * 4 + n)
                nc.tensor.matmul(bank[EARLY], k_op[j][0:ROWS, n // 2, par * P:(par + 1) * P],
                                 q_op[j][0:ROWS, n // 2, (n % 2) * HALF:(n % 2 + 1) * HALF],
                                 start=True, stop=True).then_inc(mm_early, 1)

            def pe_slot(q, k, first, last):
                u, i, j, par = q * 4 + k, q * 2 + k // 2, k // 2, k % 2
                next_j, has_next = (k + 1) // 2 % 2, not (last and k == 3)
                wait(pe, num_used, u * 3 - 1)
                products((0 + par) % 2, j, par, 0, 1).then_inc(mm_num, 1)
                early(u, j, par, 3)
                wait(pe, den_used, u * 3)
                products(2, j, par, 1, 1).then_inc(mm_den, 1)
                if has_next:
                    if par == 1:
                        pe.wait_ge(op_in[next_j], (q + 1 - next_j) * 32 + 32)
                    early(u + 1, next_j, 1 - par, 0)
                wait(pe, num_used, u * 3)
                products((1 + par) % 2, j, par, 0, 2).then_inc(mm_num, 1)
                if has_next:
                    early(u + 1, next_j, 1 - par, 1)
                wait(pe, num_used, u * 3 + 1)
                products((2 + par) % 2, j, par, 0, 3).then_inc(mm_num, 1)
                wait(pe, den_used, u * 3 + 1)
                products(2, j, par, 1, 2).then_inc(mm_den, 1)
                if not first:
                    attend(i - 2, j, par)
                if has_next:
                    early(u + 1, next_j, 1 - par, 2)
                wait(pe, den_used, u * 3 + 2)
                products(2, j, par, 1, 3).then_inc(mm_den, 1)

            pe.wait_ge(op_in[0], 32)
            for n in range(3):
                early(0, 0, 0, n)
            for k in range(4):
                pe_slot(0, k, True, False)
            with pe.Fori(1, NUNIT // 4 - 1) as it:
                for k in range(4):
                    pe_slot(it, k, False, False)
            for k in range(4):
                pe_slot(NUNIT // 4 - 1, k, False, True)
            for j in range(2):
                for t in range(2):
                    attend(NHEAD - 2 + j, j, t)
            pe.sem_inc(t5.norm_used, 4)
            pe.sem_inc(t5.t_used, 2)
            pe.wait_ge(s_late, nW[2])
            with pe.Fori(0, B // 2) as it:
                for j in range(2):
                    pe.wait_ge(t5.copied, it * 2 + 1)
                    turn(it * 4 + 2 * j, j, 2 * j, t5)
                pe.wait_ge(t5.turned, it * 4 + 4)
                pe.sem_inc(t5.norm_used, 4)
                for j in range(2):
                    pe.wait_ge(t5.copied, it * 2 + (j + 2))
                    for u in range(2):
                        pe.wait_ge(proj_taken, it * 4 + 1)
                        nc.tensor.matmul(bank[2 + 2 * j + u][:, 0:C], norm_t[j][:, u * P:(u + 1) * P],
                                         w_proj_sb[:, :], start=True, stop=True).then_inc(proj_done, 1)
                    pe.wait_ge(proj_done, it * 4 + 2 * j + 2)
                    pe.sem_inc(t5.t_used, 1)
            pe.sem_inc(t6.norm_used, 4)
            with pe.Fori(0, B // 2) as it:
                for j in range(2):
                    pe.wait_ge(t6.copied, it * 2 + 1)
                    turn(it * 4 + 2 * j, j, 2 * j, t6)
                pe.wait_ge(t6.turned, it * 4 + 4)
                pe.sem_inc(t6.norm_used, 4)
            pe.wait_ge(g_sum, 1)
            nc.tensor.matmul(bank[6][0:B, 0:E0], tok_sum[:, :], gate0_w_sb[:, :], start=True, stop=True).then_inc(g_mm, 1)
            pe.wait_ge(g_chain, 7)
            pe.wait_ge(s_ones, 1)
            nc.tensor.matmul(bank[6][:, 32:32 + B], ones[0:B, :], gate_diag[:, :], start=True, stop=True).then_inc(g_mm, 1)
            pe.sem_inc(t6.t_used, 2)
            with pe.Fori(0, 2) as it:
                for j in range(4):
                    pe.wait_ge(g_copied, it * 4 + (j + 1))
                    pe.wait_ge(g_in[j], it * 32 + 32)
                    pe.wait_ge(y_taken, it * 8 + (4 * (j // 2) + 1))
                    for u in range(2):
                        nc.tensor.matmul(bank[2 + 2 * (j % 2) + u][:, 0:C], norm_t[j % 2][:, u * P:(u + 1) * P],
                                         w_sel[j][:, :], start=True, stop=True).then_inc(y_done, 1)
                    pe.wait_ge(y_done, it * 8 + (2 * j + 2))
                    pe.sem_inc(t6.t_used, 1)
            pe.wait_ge(y_taken, NT + 1)

            def turn_norm1(b):
                wait(pe, ot_copied, b * 2 - 3)
                turn(b * 2, 1, 0, t7)

            def project_in(b, z, n):
                if n < 2:
                    pe.wait_ge(t7.copied, b + 1)
                if n % 2 == 0:
                    wait(pe, *((p_act, b * 3 + n // 2) if n else (ot_copied, b * 2 - 2)))
                else:
                    wait(pe, *((p_dve, b * 3 + n // 2) if n > 1 else (wo_sum, b * 2 - 2)))
                if n < 4:
                    w = (wq1_sb, wk1_sb)[n // 2]
                    for a in range(2):
                        g = 2 * (n % 2) + a
                        mm = nc.tensor.matmul(bank[1 + n % 2][:, a * L:(a + 1) * L], w[:, g * P:(g + 1) * P],
                                              norm_t[0][:, :], start=True, stop=True)
                else:
                    u = n - 4
                    mm = nc.tensor.matmul(bank[1 + u][:, :], norm_t[0][:, u * P:(u + 1) * P], wv1_sb[:, :],
                                          start=True, stop=True)
                mm.then_inc(p_done, 1)

            def logits(b, z, m):
                u, g = m // 8, m % 8
                r = D1 * (g % 2)
                if m == 0:
                    pe.wait_ge(p_act, b * 3 + 3)
                    pe.wait_ge(p_dve, b * 3 + 3)
                wait(pe, s_exp, b * 16 + (m - 1))
                nc.tensor.matmul(bank[4 + m % 2][:, 0:L], q1[z][r:r + D1, g // 2, u * P:(u + 1) * P],
                                 k1[z][r:r + D1, g // 2, :], start=True, stop=True).then_inc(s_done, 1)

            def turn_prob(b, m):
                pe.wait_ge(s_exp, b * 16 + (m + 1))
                wait(pe, pt_copied, b * 16 + (m - 1))
                for a in range(2):
                    mm = nc.tensor.transpose(bank[6 - 3 * (m % 2)][:, a * P:(a + 1) * P],
                                             prob[m % 2][:, a * P:(a + 1) * P], ident[:, :])
                mm.then_inc(pt_done, 1)

            def values(b, z, m):
                u, g = m // 8, m % 8
                o_ps = bank[7] if u == 0 else bank[0]
                pe.wait_ge(pt_copied, b * 16 + (m + 1))
                if g == 0:
                    wait(pe, o_norm, b * 2 + (u - 1))
                for a in range(2):
                    mm = nc.tensor.matmul(o_ps[:, g * D1:(g + 1) * D1], prob_t[m % 2][:, a, :],
                                          v1[z][:, a, g * D1:(g + 1) * D1], start=(a == 0), stop=(a == 1))
                mm.then_inc(pv_done, 1)

            def turn_o1(n, b, after_inputs):
                pe.wait_ge(o_norm, n + 1)
                if after_inputs:
                    pe.wait_ge(p_act, b * 3 + 3)
                wait(pe, ot_copied, n)
                for a in range(4):
                    mm = nc.tensor.transpose(bank[1][:, a * P:(a + 1) * P], o1[:, a * P:(a + 1) * P], ident[:, :])
                mm.then_inc(ot_done, 1)

            def project_out(n, b, after_inputs):
                pe.wait_ge(ot_copied, n + 1)
                if after_inputs:
                    pe.wait_ge(p_dve, b * 3 + 3)
                wait(pe, wo_sum, n)
                for a in range(4):
                    mm = nc.tensor.matmul(bank[2][:, 0:C], o1_t[:, a, :], wo1_sb[:, a, :], start=(a == 0), stop=(a == 3))
                mm.then_inc(wo_done, 1)

            def pe_batch(b, z, first, last):
                for m in range(16):
                    if m + 1 < 16:
                        logits(b, z, m + 1)
                    elif not last:
                        logits(b + 1, 1 - z, 0)
                    turn_prob(b, m)
                    if m:
                        values(b, z, m - 1)
                    elif not first:
                        values(b - 1, 1 - z, 15)
                    if m == 1 and not last:
                        turn_norm1(b + 1)
                    if m == 3 and not first:
                        turn_o1(b * 2 - 1, b, False)
                    if m == 5 and not first:
                        project_out(b * 2 - 1, b, False)
                    if 5 <= m <= 10 and not last:
                        project_in(b + 1, 1 - z, m - 5)
                    if m == 11:
                        turn_o1(b * 2, b + 1, not last)
                    if m == 13:
                        project_out(b * 2, b + 1, not last)

            turn_norm1(0)
            for n in range(6):
                project_in(0, 0, n)
            logits(0, 0, 0)
            pe_batch(0, 0, True, False)
            with pe.Fori(0, B // 2 - 1) as it:
                for z in range(2):
                    pe_batch(it * 2 + (z + 1), 1 - z, False, False)
            pe_batch(B - 1, 1, False, True)
            values(B - 1, 1, 15)
            turn_o1(2 * B - 1, B, False)
            project_out(2 * B - 1, B, False)
            pe.sem_inc(t8.norm_used, 4)
            pe.sem_inc(t8.t_used, 2)
            with pe.Fori(0, B // 2) as it:
                for j in range(2):
                    pe.wait_ge(t8.copied, it * 4 + 1)
                    turn(it * 4 + 2 * j, j, 2 * j, t8)
                pe.wait_ge(t8.turned, it * 4 + 4)
                pe.sem_inc(t8.norm_used, 4)
                for j in range(2):
                    pe.wait_ge(t8.copied, it * 4 + (2 * (j + 1) + 1))
                    pe.wait_ge(l_taken, it * 4 + 1)
                    for u in range(2):
                        nc.tensor.matmul(bank[2 + 2 * j + u][:, 0:E1], norm_t[j][:, u * P:(u + 1) * P],
                                         gate1_w_sb[:, :], start=True, stop=True).then_inc(l_done, 1)
                    pe.wait_ge(l_done, it * 4 + 2 * j + 2)
                    pe.sem_inc(t8.t_used, 1)
            pe.wait_ge(l_taken, NT + 1)
            pe.sem_inc(e_done, 2)
            pe.sem_inc(wp_turned, 1)
            pe.sem_inc(b2_done, 1)

            def turn_weights(g):
                pe.wait_ge(wp_ready, g + 1)
                nc.tensor.transpose(bank[6][:, 0:P], w_pad[:, :, :].rearrange("p a e -> p (a e)"), ident[:, :]).then_inc(wp_turned, 1)

            def biases(g, t):
                if t == 0:
                    pe.wait_ge(wp_copied, g + 1)
                    pe.wait_ge(h_add, g + NT)
                else:
                    pe.wait_ge(b2_done, g * 4 + (t + 1))
                nc.tensor.matmul(bank[7][:, t * C:(t + 1) * C], w_pad_t[32 * t:32 * t + E1, :],
                                 b2_sb[32 * t:32 * t + E1, :], start=True, stop=True).then_inc(b2_done, 1)

            def hidden(g, e):
                for f in range(2):
                    n = 2 * e + f
                    wait(pe, hid_ready, g * 16 + n)
                    nc.tensor.matmul(bank[n % 2][:, :], w1_sb[:, e, f * P:(f + 1) * P],
                                     all_t[:, bass.ds(g * 512, 512)], start=True, stop=True).then_inc(h_done, 1)

            def second(g, e):
                pe.wait_ge(hid_ready, g * 16 + (2 * e + 3))
                pe.wait_ge(y_taken, g * 32 + (NT + 4 * (e - 1) + 1))
                for t in range(4):
                    for f in range(2):
                        mm = nc.tensor.matmul(bank[2 + e % 2][:, t * C:(t + 1) * C],
                                              hid[(2 * e + f) % 4][:, t * P:(t + 1) * P], w2_sb[:, 2 * e + f, :],
                                              start=(f == 0), stop=(f == 1))
                mm.then_inc(e_done, 1)

            def experts(g, last):
                for e in range(E1):
                    if e + 1 < E1:
                        hidden(g, e + 1)
                    elif not last:
                        hidden(g + 1, 0)
                    if e == 6 and not last:
                        biases(g + 1, 1)
                    second(g, e)
                    if not last:
                        if e == 3:
                            turn_weights(g + 1)
                        if e >= 5:
                            biases(g + 1, (0, 2, 3)[e - 5])

            hidden(0, 0)
            turn_weights(0)
            for t in range(4):
                biases(0, t)
            with pe.Fori(0, NG - 1) as g:
                experts(g, False)
            experts(NG - 1, True)


_ORDER = ["x", "conv_w", "conv_b", "w_qk", "w_v", "w_proj", "b_proj", "param_r", "gate0_w", "gate0_b", "exp0_w",
          "exp0_b", "wq1", "wk1", "wv1", "wo1", "gate1_w", "gate1_b", "w1", "b1", "w2", "b2", "neg_mask", "ident_in"]


def kernel(x, L0_tok_weight, L0_tok_bias, L0_attn_w_qkv, L0_attn_w_proj, L0_attn_b_proj, L0_attn_paramR, L0_ffn_Wg,
           L0_ffn_bg, L0_ffn_We, L0_ffn_be, L1_attn_Wq, L1_attn_Wk, L1_attn_Wv, L1_attn_Wo, L1_ffn_gate_w,
           L1_ffn_gate_b, L1_ffn_w1, L1_ffn_b1, L1_ffn_w2, L1_ffn_b2):
    import ml_dtypes
    import concourse.bacc as bacc
    from concourse.bass_utils import run_bass_kernel_spmd

    qkv_t = np.asarray(L0_attn_w_qkv).T
    mask = np.zeros((NPIECE, DH, DH, L), ml_dtypes.bfloat16)
    for d in range(DH):
        mask[:, d, d, :] = -1
    data = dict(
        x=x, conv_w=np.transpose(L0_tok_weight, (2, 1, 0)), conv_b=L0_tok_bias, w_qk=qkv_t[:, 0:2 * C],
        w_v=qkv_t[:, 2 * C:3 * C], w_proj=np.transpose(L0_attn_w_proj), b_proj=L0_attn_b_proj,
        param_r=L0_attn_paramR, gate0_w=L0_ffn_Wg, gate0_b=L0_ffn_bg, exp0_w=L0_ffn_We, exp0_b=L0_ffn_be,
        wq1=np.transpose(L1_attn_Wq), wk1=np.transpose(L1_attn_Wk), wv1=np.transpose(L1_attn_Wv),
        wo1=np.transpose(L1_attn_Wo), gate1_w=L1_ffn_gate_w, gate1_b=L1_ffn_gate_b, w1=L1_ffn_w1, b1=L1_ffn_b1,
        w2=L1_ffn_w2, b2=L1_ffn_b2, neg_mask=mask.reshape(KROWS, DH * L), ident_in=np.eye(P, dtype=np.float32))
    nc = bacc.Bacc("TRN2", target_bir_lowering=False, num_devices=1)
    arrays, args = {}, []
    for name in _ORDER:
        a = np.ascontiguousarray(data[name])
        arrays[f"in_{name}"] = a
        args.append(nc.dram_tensor(f"in_{name}", a.shape, mybir.dt.from_np(a.dtype), kind="ExternalInput").ap())
    args.append(nc.dram_tensor("out_0", (B, L, C), F32, kind="ExternalOutput").ap())
    build(nc, *args)
    r = run_bass_kernel_spmd(nc, [arrays], core_ids=[0])
    return r.results[0]["out_0"]
```
